# Optimizing a Trainium2 kernel written in Bass

```python
import numpy as np
import jax
import jax.numpy as jnp

def _softmax(x, axis=-1):
    return jax.nn.softmax(x, axis=axis)

def _gelu(x):
    return jax.nn.gelu(x, approximate=True)

def _silu(x):
    return jax.nn.silu(x)

def _sigmoid(x):
    return jax.nn.sigmoid(x)

def _layernorm(x, axis=-1, eps=1e-05):
    m = jnp.mean(x, axis=axis, keepdims=True)
    v = jnp.var(x, axis=axis, keepdims=True)
    return (x - m) / jnp.sqrt(v + eps)

def _scatter_add(tgt, idx, src, axis=0):
    return tgt.at[idx].add(src)

def _segment_sum(src, seg, n):
    return jax.ops.segment_sum(src, seg, n)
kernel_name = 'mk_decoder_preln_d2_seqx_r4_3a4373'

def setup_inputs(seed: int=0):
    np.random.seed(seed)
    _w = jnp.asarray

    def _rec_inputs():
        import jax
        import jax.numpy as jnp
        _rk = jax.random.key(seed)
        x = -0.0002928 + 1 * jax.random.normal(jax.random.fold_in(_rk, 1), (16, 112, 256), jnp.float32)
        _lenS = 112 - jax.random.randint(jax.random.fold_in(_rk, 7), (16,), 0, max(1, 112 // 4) + 1, jnp.int32)
        _lenS2 = 375 - jax.random.randint(jax.random.fold_in(_rk, 8), (16,), 0, max(1, 375 // 4) + 1, jnp.int32)
        _ctx_1024P = jax.random.normal(jax.random.fold_in(_rk, 11), (16, 16, 256), jnp.float32)
        _ctx_1024c = jax.random.dirichlet(jax.random.fold_in(_rk, 511), 0.3 * jnp.ones((16,), jnp.float32), (16, 375))
        _ctx_1024t = jnp.einsum('bsk,bkd->bsd', _ctx_1024c, _ctx_1024P)
        _ctx_1024t = _ctx_1024t * jax.lax.rsqrt(jnp.mean(jnp.square(_ctx_1024t)) + 1e-12) * 0.953939
        ctx_1024 = -1.39393e-06 + 0.999914 * (_ctx_1024t + 0.3 * jax.random.normal(jax.random.fold_in(_rk, 611), (16, 375, 256), jnp.float32))
        return (x, ctx_1024)
    x, ctx_1024 = _rec_inputs()

    def _L0_attn_setup():
        import jax, jax.numpy as jnp
        import numpy as np
        B, L, E, H = (8, 512, 256, 16)
        D = E // H
        EPS = 1e-06
        key = jax.random.key(seed)
        ks = jax.random.split(key, 9)
        s = 1.0 / np.sqrt(E)

        def lin_w(k):
            return jax.random.uniform(k, (E, E), jnp.float32, -s, s)

        def lin_b(k):
            return jax.random.uniform(k, (E,), jnp.float32, -s, s)
        return {'query': jax.random.normal(ks[0], (B, L, E), jnp.float32), 'Wq': lin_w(ks[1]), 'bq': lin_b(ks[2]), 'Wk': lin_w(ks[3]), 'bk': lin_b(ks[4]), 'Wv': lin_w(ks[5]), 'bv': lin_b(ks[6]), 'Wo': lin_w(ks[7]), 'bo': lin_b(ks[8])}
    _L0_attn_all = _L0_attn_setup()
    _L0_attn_in = {k: v for k, v in _L0_attn_all.items() if k in ('Wq', 'bq', 'Wk', 'bk', 'Wv', 'bv', 'Wo', 'bo')}
    del _L0_attn_all

    def _L0_xattn_setup():
        import jax, jax.numpy as jnp
        import numpy as np
        D_MODEL = 256
        N_HEADS = 16
        D_K = D_MODEL // N_HEADS
        key = jax.random.key(seed)
        ks = jax.random.split(key, 11)
        B, L, S = (2, 512, 512)
        scale = 1.0 / np.sqrt(D_MODEL)
        return {'x_q': jax.random.normal(ks[0], (B, L, D_MODEL), jnp.float32), 'x_k': jax.random.normal(ks[1], (B, S, D_MODEL), jnp.float32), 'x_v': jax.random.normal(ks[2], (B, S, D_MODEL), jnp.float32), 'W_Q': jax.random.normal(ks[3], (D_MODEL, D_MODEL), jnp.float32) * scale, 'b_Q': jax.random.normal(ks[4], (D_MODEL,), jnp.float32) * 0.01, 'W_K': jax.random.normal(ks[5], (D_MODEL, D_MODEL), jnp.float32) * scale, 'b_K': jax.random.normal(ks[6], (D_MODEL,), jnp.float32) * 0.01, 'W_V': jax.random.normal(ks[7], (D_MODEL, D_MODEL), jnp.float32) * scale, 'b_V': jax.random.normal(ks[8], (D_MODEL,), jnp.float32) * 0.01, 'W_O': jax.random.normal(ks[9], (D_MODEL, D_MODEL), jnp.float32) * scale, 'b_O': jax.random.normal(ks[10], (D_MODEL,), jnp.float32) * 0.01}
    _L0_xattn_all = _L0_xattn_setup()
    _L0_xattn_in = {k: v for k, v in _L0_xattn_all.items() if k in ('W_Q', 'b_Q', 'W_K', 'b_K', 'W_V', 'b_V', 'W_O', 'b_O')}
    del _L0_xattn_all

    def _L0_ffn_setup():
        import jax, jax.numpy as jnp
        import numpy as np
        B, S, D = (2, 512, 256)
        I = 128
        E = 16
        TOP_K = 2

        def _mlp(x, wg, wu, wd):
            return jnp.einsum('bsi,id->bsd', jax.nn.silu(x @ wg) * (x @ wu), wd)
        key = jax.random.key(seed)
        ks = jax.random.split(key, 10)
        sc_d = 1.0 / np.sqrt(D)
        sc_i = 1.0 / np.sqrt(I)
        return {'x': jax.random.normal(ks[0], (B, S, D), dtype=jnp.float32), 'gate_w': jax.random.normal(ks[1], (D, E), dtype=jnp.float32) * sc_d, 'gate_b': jnp.zeros((E,), dtype=jnp.float32), 'shared_wg': jax.random.normal(ks[2], (D, I), dtype=jnp.float32) * sc_d, 'shared_wu': jax.random.normal(ks[3], (D, I), dtype=jnp.float32) * sc_d, 'shared_wd': jax.random.normal(ks[4], (I, D), dtype=jnp.float32) * sc_i, 'experts_wg': jax.random.normal(ks[5], (E, D, I), dtype=jnp.float32) * sc_d, 'experts_wu': jax.random.normal(ks[6], (E, D, I), dtype=jnp.float32) * sc_d, 'experts_wd': jax.random.normal(ks[7], (E, I, D), dtype=jnp.float32) * sc_i}
    _L0_ffn_all = _L0_ffn_setup()
    _L0_ffn_in = {k: v for k, v in _L0_ffn_all.items() if k in ('gate_w', 'gate_b', 'shared_wg', 'shared_wu', 'shared_wd', 'experts_wg', 'experts_wu', 'experts_wd')}
    del _L0_ffn_all

    def _L1_attn_setup():
        import jax, jax.numpy as jnp
        import numpy as np
        D_MODEL, D_QKV, N_HEADS = (256, 64, 16)
        key = jax.random.key(seed)
        k_x, k_qkv, k_out = jax.random.split(key, 3)
        X = jax.random.normal(k_x, (2, 512, D_MODEL), dtype=jnp.float32)
        W_qkv = jax.random.normal(k_qkv, (D_MODEL, 3 * D_QKV * N_HEADS), dtype=jnp.float32) * D_MODEL ** (-0.5)
        W_out = jax.random.normal(k_out, (D_QKV * N_HEADS, D_MODEL), dtype=jnp.float32) * (D_QKV * N_HEADS) ** (-0.5)
        return {'X': X, 'W_qkv': W_qkv, 'W_out': W_out}
    _L1_attn_all = _L1_attn_setup()
    _L1_attn_in = {k: v for k, v in _L1_attn_all.items() if k in ('W_qkv', 'W_out')}
    del _L1_attn_all

    def _L1_xattn_setup():
        import jax, jax.numpy as jnp
        import numpy as np
        DIM = 256
        CTX_DIM = 256
        HEADS = 8
        DIM_HEAD = 64
        INNER = HEADS * DIM_HEAD
        EPS = 1e-05

        def _layer_norm(x, gamma, beta):
            mu = jnp.mean(x, axis=-1, keepdims=True)
            var = jnp.mean(jnp.square(x - mu), axis=-1, keepdims=True)
            return (x - mu) * jax.lax.rsqrt(var + EPS) * gamma + beta
        key = jax.random.key(seed)
        ks = jax.random.split(key, 8)
        b, n, m = (4, 512, 512)
        x = jax.random.normal(ks[0], (b, n, DIM), dtype=jnp.float32)
        context = jax.random.normal(ks[1], (b, m, CTX_DIM), dtype=jnp.float32)
        Wq = jax.random.normal(ks[2], (DIM, INNER), dtype=jnp.float32) / np.sqrt(DIM)
        Wkv = jax.random.normal(ks[3], (CTX_DIM, 2 * INNER), dtype=jnp.float32) / np.sqrt(CTX_DIM)
        Wout = jax.random.normal(ks[4], (INNER, DIM), dtype=jnp.float32) / np.sqrt(INNER)
        bout = jnp.zeros((DIM,), dtype=jnp.float32)
        g1 = jnp.ones((DIM,), dtype=jnp.float32)
        b1 = jnp.zeros((DIM,), dtype=jnp.float32)
        g2 = jnp.ones((CTX_DIM,), dtype=jnp.float32)
        b2 = jnp.zeros((CTX_DIM,), dtype=jnp.float32)
        return {'x': x, 'context': context, 'g1': g1, 'b1': b1, 'g2': g2, 'b2': b2, 'Wq': Wq, 'Wkv': Wkv, 'Wout': Wout, 'bout': bout}
    _L1_xattn_all = _L1_xattn_setup()
    _L1_xattn_in = {k: v for k, v in _L1_xattn_all.items() if k in ('g1', 'b1', 'g2', 'b2', 'Wq', 'Wkv', 'Wout', 'bout')}
    del _L1_xattn_all

    def _L1_ffn_setup():
        import jax, jax.numpy as jnp
        import numpy as np
        B, T, C = (8, 512, 256)
        H = 1024
        E = 8
        K = 2
        LOAD_FACTOR = 1.2
        N_LAYER = 12

        def _get_expert_inputs(x, logits, expert_capacity):
            Tt = logits.shape[0]
            Cc = x.shape[1]
            top_k_logits, expert_indices = jax.lax.top_k(logits, K)
            expert_probs = jax.nn.softmax(top_k_logits, axis=-1)
            ei = jnp.swapaxes(expert_indices, 0, 1).ravel()
            one_hot = jax.nn.one_hot(ei, E, dtype=jnp.int32)
            pos = jnp.cumsum(one_hot, axis=0) * one_hot - 1
            pos = pos.reshape(-1, Tt, E)
            pos = jnp.swapaxes(pos, 0, 1)
            pos = jnp.max(pos, axis=2)
            ei = jnp.swapaxes(ei.reshape(-1, Tt), 0, 1)
            buf = jnp.zeros((E, expert_capacity, Cc), x.dtype)
            xr = jnp.repeat(x, K, axis=0)
            expert_inputs = buf.at[ei.ravel(), pos.ravel()].add(xr)
            return (expert_probs, pos, ei, expert_inputs)
        key = jax.random.key(seed)
        ks = jax.random.split(key, 9)
        std = 0.02
        proj_std = 0.02 * (2 * N_LAYER) ** (-0.5)
        return {'x': jax.random.normal(ks[0], (B, T, C), jnp.float32), 'router_w': jax.random.normal(ks[1], (C, E), jnp.float32) * std, 'router_b': jnp.zeros((E,), jnp.float32), 'w_c_fc': jax.random.normal(ks[2], (E, C, H), jnp.float32) * std, 'b_c_fc': jnp.zeros((E, 1, H), jnp.float32), 'w_gate': jax.random.normal(ks[3], (E, C, H), jnp.float32) * std, 'b_gate': jnp.zeros((E, 1, H), jnp.float32), 'w_c_proj': jax.random.normal(ks[4], (E, H, C), jnp.float32) * proj_std, 'b_c_proj': jnp.zeros((E, 1, C), jnp.float32)}
    _L1_ffn_all = _L1_ffn_setup()
    _L1_ffn_in = {k: v for k, v in _L1_ffn_all.items() if k in ('router_w', 'router_b', 'w_c_fc', 'b_c_fc', 'w_gate', 'b_gate', 'w_c_proj', 'b_c_proj')}
    del _L1_ffn_all
    return {'x': x, 'ctx_1024': ctx_1024, 'L0_attn_Wq': _L0_attn_in['Wq'], 'L0_attn_bq': _L0_attn_in['bq'], 'L0_attn_Wk': _L0_attn_in['Wk'], 'L0_attn_bk': _L0_attn_in['bk'], 'L0_attn_Wv': _L0_attn_in['Wv'], 'L0_attn_bv': _L0_attn_in['bv'], 'L0_attn_Wo': _L0_attn_in['Wo'], 'L0_attn_bo': _L0_attn_in['bo'], 'L0_xattn_W_Q': _L0_xattn_in['W_Q'], 'L0_xattn_b_Q': _L0_xattn_in['b_Q'], 'L0_xattn_W_K': _L0_xattn_in['W_K'], 'L0_xattn_b_K': _L0_xattn_in['b_K'], 'L0_xattn_W_V': _L0_xattn_in['W_V'], 'L0_xattn_b_V': _L0_xattn_in['b_V'], 'L0_xattn_W_O': _L0_xattn_in['W_O'], 'L0_xattn_b_O': _L0_xattn_in['b_O'], 'L0_ffn_gate_w': _L0_ffn_in['gate_w'], 'L0_ffn_gate_b': _L0_ffn_in['gate_b'], 'L0_ffn_shared_wg': _L0_ffn_in['shared_wg'], 'L0_ffn_shared_wu': _L0_ffn_in['shared_wu'], 'L0_ffn_shared_wd': _L0_ffn_in['shared_wd'], 'L0_ffn_experts_wg': _L0_ffn_in['experts_wg'], 'L0_ffn_experts_wu': _L0_ffn_in['experts_wu'], 'L0_ffn_experts_wd': _L0_ffn_in['experts_wd'], 'L1_attn_W_qkv': _L1_attn_in['W_qkv'], 'L1_attn_W_out': _L1_attn_in['W_out'], 'L1_xattn_g1': _L1_xattn_in['g1'], 'L1_xattn_b1': _L1_xattn_in['b1'], 'L1_xattn_g2': _L1_xattn_in['g2'], 'L1_xattn_b2': _L1_xattn_in['b2'], 'L1_xattn_Wq': _L1_xattn_in['Wq'], 'L1_xattn_Wkv': _L1_xattn_in['Wkv'], 'L1_xattn_Wout': _L1_xattn_in['Wout'], 'L1_xattn_bout': _L1_xattn_in['bout'], 'L1_ffn_router_w': _L1_ffn_in['router_w'], 'L1_ffn_router_b': _L1_ffn_in['router_b'], 'L1_ffn_w_c_fc': _L1_ffn_in['w_c_fc'], 'L1_ffn_b_c_fc': _L1_ffn_in['b_c_fc'], 'L1_ffn_w_gate': _L1_ffn_in['w_gate'], 'L1_ffn_b_gate': _L1_ffn_in['b_gate'], 'L1_ffn_w_c_proj': _L1_ffn_in['w_c_proj'], 'L1_ffn_b_c_proj': _L1_ffn_in['b_c_proj']}

def reference(x, ctx_1024, L0_attn_Wq, L0_attn_bq, L0_attn_Wk, L0_attn_bk, L0_attn_Wv, L0_attn_bv, L0_attn_Wo, L0_attn_bo, L0_xattn_W_Q, L0_xattn_b_Q, L0_xattn_W_K, L0_xattn_b_K, L0_xattn_W_V, L0_xattn_b_V, L0_xattn_W_O, L0_xattn_b_O, L0_ffn_gate_w, L0_ffn_gate_b, L0_ffn_shared_wg, L0_ffn_shared_wu, L0_ffn_shared_wd, L0_ffn_experts_wg, L0_ffn_experts_wu, L0_ffn_experts_wd, L1_attn_W_qkv, L1_attn_W_out, L1_xattn_g1, L1_xattn_b1, L1_xattn_g2, L1_xattn_b2, L1_xattn_Wq, L1_xattn_Wkv, L1_xattn_Wout, L1_xattn_bout, L1_ffn_router_w, L1_ffn_router_b, L1_ffn_w_c_fc, L1_ffn_b_c_fc, L1_ffn_w_gate, L1_ffn_b_gate, L1_ffn_w_c_proj, L1_ffn_b_c_proj):
    import jax
    import jax.numpy as jnp

    def _L0_attn_ref(query, Wq, bq, Wk, bk, Wv, bv, Wo, bo):
        import jax, jax.numpy as jnp
        import numpy as np
        B, L, E, H = (8, 512, 256, 16)
        D = E // H
        EPS = 1e-06
        bsz, tgt_len, embed_dim = query.shape
        n_head = H
        head_dim = embed_dim // n_head
        m = tgt_len
        q = query @ Wq + bq
        k = query @ Wk + bk
        v = query @ Wv + bv

        def to_heads(x):
            return x.reshape(bsz, tgt_len, n_head, head_dim).transpose(0, 2, 1, 3)
        q = jax.nn.softmax(to_heads(q), axis=-1)
        k = jax.nn.softmax(to_heads(k), axis=-1)
        v = to_heads(v)
        comp_q = 1.0 - q
        comp_k = 1.0 - k
        idx = np.pi / 2 * jnp.arange(1, m + 1, dtype=jnp.float32) / m
        sin = jnp.sin(idx)[None, None, :, None]
        cos = jnp.cos(idx)[None, None, :, None]

        def feat(x):
            return jnp.concatenate([x * sin, x * cos], axis=-1)
        qf, comp_qf = (feat(q), feat(comp_q))
        kf, comp_kf = (feat(k), feat(comp_k))

        def branch(qf_, kf_):
            kv = jnp.einsum('bhld,bhlm->bhdm', kf_, v)
            z = 1.0 / jnp.maximum(jnp.einsum('bhld,bhd->bhl', qf_, kf_.sum(axis=2)), EPS)
            return jnp.einsum('bhld,bhdm,bhl->bhlm', qf_, kv, z)
        attn = branch(qf, kf) + branch(comp_qf, comp_kf)
        out = attn.transpose(2, 0, 1, 3).reshape(tgt_len, bsz, embed_dim)
        out = out @ Wo + bo
        return out.reshape(bsz, tgt_len, embed_dim)

    def _L0_xattn_ref(x_q, x_k, x_v, W_Q, b_Q, W_K, b_K, W_V, b_V, W_O, b_O):
        import jax, jax.numpy as jnp
        import numpy as np
        D_MODEL = 256
        N_HEADS = 16
        D_K = D_MODEL // N_HEADS
        B, L, _ = x_q.shape
        S = x_k.shape[1]
        H, dk = (N_HEADS, D_K)
        Q = (x_q @ W_Q + b_Q).reshape(B, L, H, dk).transpose(0, 2, 1, 3)
        K = (x_k @ W_K + b_K).reshape(B, S, H, dk).transpose(0, 2, 1, 3)
        V = (x_v @ W_V + b_V).reshape(B, S, H, dk).transpose(0, 2, 1, 3)
        scores = jnp.einsum('bhld,bhsd->bhls', Q, K) / jnp.sqrt(jnp.float32(dk))
        attn = jax.nn.softmax(scores, axis=-1)
        ctx = jnp.einsum('bhls,bhsd->bhld', attn, V)
        ctx = ctx.transpose(0, 2, 1, 3).reshape(B, L, H * dk)
        out = ctx @ W_O + b_O
        return out

    def _L0_ffn_ref(x, gate_w, gate_b, shared_wg, shared_wu, shared_wd, experts_wg, experts_wu, experts_wd):
        import jax, jax.numpy as jnp
        import numpy as np
        B, S, D = (2, 512, 256)
        I = 128
        E = 16
        TOP_K = 2

        def _mlp(x, wg, wu, wd):
            return jnp.einsum('bsi,id->bsd', jax.nn.silu(x @ wg) * (x @ wu), wd)
        router_logits = jax.nn.sigmoid(x @ gate_w + gate_b)
        expert_values, expert_indices = jax.lax.top_k(router_logits, k=TOP_K)
        expert_values = expert_values / jnp.sum(expert_values, axis=-1, keepdims=True)
        hg = jnp.einsum('bsd,edi->bsei', x, experts_wg)
        hu = jnp.einsum('bsd,edi->bsei', x, experts_wu)
        all_outputs = jnp.einsum('bsei,eid->bsed', jax.nn.silu(hg) * hu, experts_wd)
        selected = jnp.take_along_axis(all_outputs, expert_indices[..., None], axis=2)
        expert_weighted = jnp.sum(expert_values[..., None] * selected, axis=2)
        return x + _mlp(x, shared_wg, shared_wu, shared_wd) + expert_weighted

    def _L1_attn_ref(X, W_qkv, W_out):
        import jax, jax.numpy as jnp
        import numpy as np
        D_MODEL, D_QKV, N_HEADS = (256, 64, 16)
        b, s, _ = X.shape
        h, d = (N_HEADS, D_QKV)
        scale = d ** 0.5
        qkv = X @ W_qkv
        qkv = qkv.reshape(b, s, h, d, 3)
        q, k, v = (qkv[..., 0], qkv[..., 1], qkv[..., 2])
        scores = jnp.einsum('bqhd,bkhd->bhqk', q, k) / scale
        weights = jax.nn.softmax(scores, axis=-1)
        attn = jnp.einsum('bhqk,bkhd->bqhd', weights, v)
        return attn.reshape(b, s, h * d) @ W_out

    def _L1_xattn_ref(x, context, g1, b1, g2, b2, Wq, Wkv, Wout, bout):
        import jax, jax.numpy as jnp
        import numpy as np
        DIM = 256
        CTX_DIM = 256
        HEADS = 8
        DIM_HEAD = 64
        INNER = HEADS * DIM_HEAD
        EPS = 1e-05

        def _layer_norm(x, gamma, beta):
            mu = jnp.mean(x, axis=-1, keepdims=True)
            var = jnp.mean(jnp.square(x - mu), axis=-1, keepdims=True)
            return (x - mu) * jax.lax.rsqrt(var + EPS) * gamma + beta
        b, n, _ = x.shape
        m = context.shape[1]
        scale = DIM_HEAD ** (-0.5)
        xn = _layer_norm(x, g1, b1)
        cn = _layer_norm(context, g2, b2)
        q = xn @ Wq
        kv = cn @ Wkv
        k, v = jnp.split(kv, 2, axis=-1)
        q = q.reshape(b, n, HEADS, DIM_HEAD).transpose(0, 2, 1, 3)
        k = k.reshape(b, m, HEADS, DIM_HEAD).transpose(0, 2, 1, 3)
        v = v.reshape(b, m, HEADS, DIM_HEAD).transpose(0, 2, 1, 3)
        sim = jnp.einsum('bhid,bhjd->bhij', q, k) * scale
        attn = jax.nn.softmax(sim, axis=-1)
        out = jnp.einsum('bhij,bhjd->bhid', attn, v)
        out = out.transpose(0, 2, 1, 3).reshape(b, n, INNER)
        return out @ Wout + bout

    def _L1_ffn_ref(x, router_w, router_b, w_c_fc, b_c_fc, w_gate, b_gate, w_c_proj, b_c_proj):
        import jax, jax.numpy as jnp
        import numpy as np
        B, T, C = (8, 512, 256)
        H = 1024
        E = 8
        K = 2
        LOAD_FACTOR = 1.2
        N_LAYER = 12

        def _get_expert_inputs(x, logits, expert_capacity):
            Tt = logits.shape[0]
            Cc = x.shape[1]
            top_k_logits, expert_indices = jax.lax.top_k(logits, K)
            expert_probs = jax.nn.softmax(top_k_logits, axis=-1)
            ei = jnp.swapaxes(expert_indices, 0, 1).ravel()
            one_hot = jax.nn.one_hot(ei, E, dtype=jnp.int32)
            pos = jnp.cumsum(one_hot, axis=0) * one_hot - 1
            pos = pos.reshape(-1, Tt, E)
            pos = jnp.swapaxes(pos, 0, 1)
            pos = jnp.max(pos, axis=2)
            ei = jnp.swapaxes(ei.reshape(-1, Tt), 0, 1)
            buf = jnp.zeros((E, expert_capacity, Cc), x.dtype)
            xr = jnp.repeat(x, K, axis=0)
            expert_inputs = buf.at[ei.ravel(), pos.ravel()].add(xr)
            return (expert_probs, pos, ei, expert_inputs)
        Bb, Tt, Cc = x.shape
        logits = jnp.einsum('btc,ce->bte', x, router_w) + router_b
        cap = int(LOAD_FACTOR * K * Tt // E)
        probs, pos, idx, einp = jax.vmap(lambda xb, lb: _get_expert_inputs(xb, lb, cap))(x, logits)
        if Bb % E == 0:
            t = einp.reshape(E, Bb // E, E, cap, Cc)
            t = jnp.swapaxes(t, 0, 2)
        else:
            t = jnp.swapaxes(einp, 0, 1)
        einp2 = t.reshape(E, Bb * cap, Cc)
        h = jnp.einsum('eti,eih->eth', einp2, w_c_fc) + b_c_fc
        g = jnp.einsum('eti,eih->eth', einp2, w_gate) + b_gate
        o = jnp.einsum('eth,eho->eto', jax.nn.silu(h * g), w_c_proj) + b_c_proj
        if Bb % E == 0:
            o = o.reshape(E, Bb // E, E, cap, Cc)
            o = jnp.swapaxes(o, 0, 2)
            o = o.reshape(Bb, E, cap, Cc)
        else:
            o = o.reshape(E, Bb, cap, Cc)
            o = jnp.swapaxes(o, 0, 1)

        def collect(eo, i, p, pr):
            sel = eo[i, p]
            return jnp.sum(pr[..., None] * sel, axis=1)
        return jax.vmap(collect)(o, idx, pos, probs)
    x = x + _L0_attn_ref(_layernorm(x, axis=-1), L0_attn_Wq, L0_attn_bq, L0_attn_Wk, L0_attn_bk, L0_attn_Wv, L0_attn_bv, L0_attn_Wo, L0_attn_bo)
    x = x + _L0_xattn_ref(_layernorm(x, axis=-1), ctx_1024, ctx_1024, L0_xattn_W_Q, L0_xattn_b_Q, L0_xattn_W_K, L0_xattn_b_K, L0_xattn_W_V, L0_xattn_b_V, L0_xattn_W_O, L0_xattn_b_O)
    x = x + _L0_ffn_ref(_layernorm(x, axis=-1), L0_ffn_gate_w, L0_ffn_gate_b, L0_ffn_shared_wg, L0_ffn_shared_wu, L0_ffn_shared_wd, L0_ffn_experts_wg, L0_ffn_experts_wu, L0_ffn_experts_wd)
    x = x + _L1_attn_ref(_layernorm(x, axis=-1), L1_attn_W_qkv, L1_attn_W_out)
    x = x + _L1_xattn_ref(_layernorm(x, axis=-1), ctx_1024, L1_xattn_g1, L1_xattn_b1, L1_xattn_g2, L1_xattn_b2, L1_xattn_Wq, L1_xattn_Wkv, L1_xattn_Wout, L1_xattn_bout)
    x = x + _L1_ffn_ref(_layernorm(x, axis=-1), L1_ffn_router_w, L1_ffn_router_b, L1_ffn_w_c_fc, L1_ffn_b_c_fc, L1_ffn_w_gate, L1_ffn_b_gate, L1_ffn_w_c_proj, L1_ffn_b_c_proj)
    return x

_drawn_inputs = setup_inputs


def setup_inputs(seed=0):
    import zlib

    import numpy as np

    out = dict(_drawn_inputs(seed))
    spreads = {'L0_ffn_gate_b': (0.0, 0.1),
     'L1_xattn_g1': (1.0, 0.6),
     'L1_xattn_b1': (0.0, 0.8),
     'L1_xattn_g2': (1.0, 0.2),
     'L1_xattn_b2': (0.0, 0.1),
     'L1_xattn_bout': (0.0, 0.1),
     'L1_ffn_router_b': (0.0, 0.479),
     'L1_ffn_b_c_fc': (0.0, 0.8),
     'L1_ffn_b_gate': (0.0, 0.8),
     'L1_ffn_b_c_proj': (0.0, 0.508)}
    factors = {'L0_attn_Wq': 4.568,
     'L0_attn_bq': 8.0,
     'L0_attn_Wk': 5.194,
     'L0_attn_bk': 8.0,
     'L0_xattn_b_Q': 7.399,
     'L0_xattn_b_K': 64.0,
     'L0_xattn_b_V': 2.772,
     'L0_xattn_b_O': 2.824,
     'L1_ffn_w_c_fc': 8.0,
     'L1_ffn_w_gate': 8.0,
     'L1_ffn_w_c_proj': 8.0}
    for name, (base, spread) in spreads.items():
        noise = np.random.default_rng([zlib.crc32(name.encode()), seed]).standard_normal(out[name].shape)
        drawn = base * np.exp(spread * noise) if base else spread * noise
        out[name] = jnp.asarray(drawn.astype(out[name].dtype))
    for name, factor in factors.items():
        out[name] = (out[name] * factor).astype(out[name].dtype)
    return out
```

```python
import concourse.bass as bass
import concourse.mybir as mybir
import numpy as np
from contextlib import ExitStack

B, T, D = 16, 112, 256
S, KC, NK = 375, 125, 3
F32, BF16 = mybir.dt.float32, mybir.dt.bfloat16
ALU = mybir.AluOpType
ACT = mybir.ActivationFunctionType
AX = mybir.AxisListType
LN_EPS = 1e-5
HA, DA = 16, 16
E0, I0 = 16, 128
E1, H1 = 8, 1024
CAP = int(1.2 * 2 * T // E1)
FAR = 3.0e38
FIRST = 0

CONSTS = {}


def constant_columns():
    parts = []

    def put(name, a):
        a = np.asarray(a, np.float32)
        full = np.zeros((128, a.shape[1]), np.float32)
        full[: a.shape[0]] = a
        CONSTS[name] = (sum(x.shape[1] for x in parts), a.shape[1])
        parts.append(full)

    angle = (np.pi / 2 * np.arange(1, T + 1, dtype=np.float32) / T).astype(np.float32)
    put("ident", np.eye(128))
    put("block16", np.kron(np.eye(8), np.ones((16, 16))))
    put("head16", np.kron(np.eye(8), np.ones((16, 1))))
    put("sincos", np.stack([np.sin(angle), np.cos(angle)], 1))
    put("count16", np.tile(np.arange(16, 0, -1), (T, 1)))
    put("slots", np.tile(np.arange(CAP), (T, 1)))
    put("upto", np.triu(np.ones((T, T))))
    put("ones", np.ones((T, T)))
    put("minus_half", -0.5 * np.ones((128, 4)))
    pick = np.zeros((48, E0 * 128))
    for e in range(E0):
        for part in range(3):
            pick[part * 16 + e, e * 128:(e + 1) * 128] = 1
    put("pick", pick)
    return np.concatenate(parts, 1)


CONST_ARRAY = constant_columns()
N_CONST = CONSTS["pick"][0]


def bc(ap, n):
    return ap.unsqueeze(len(ap.shape)).broadcast_to(list(ap.shape) + [n])


def mid(ap, n):
    return ap.unsqueeze(1).broadcast_to([ap.shape[0], n, ap.shape[1]])


def chained(eng, sem, base):
    count = [0]

    def link(ins, apart=None):
        count[0] += 1
        ins.then_inc(sem, 1)
        eng.wait_ge(sem, base + count[0])
        if apart is not None:
            eng.sem_inc(apart, 1)
        return count[0]

    return link


class Shared:
    pass


def sem_maker(nc, ctx, prefix):
    held = []

    def give_back():
        nc.clear_and_free_semaphores(held)
        nc.all_engine_barrier()

    ctx.callback(give_back)

    def sem(name):
        held.append(nc.alloc_semaphore(name=prefix + name))
        return held[-1]

    return sem



LN_LINKS = 5


def norm_rows(nc, sh, dve, link, ln, x, out, n=T, nth=None):
    dve.sem_inc(ln.passed, 1)
    link(nc.vector.bn_stats(ln.stats[:n, :], x), ln.passed)
    link(nc.vector.bn_aggr(ln.mv[:n, :], ln.stats[:n, :]))
    nc.vector.tensor_scalar(ln.veps[:n, :], ln.mv[:n, 1:2], LN_EPS, None, ALU.add).then_inc(ln.var_ready, 1)
    dve.wait_ge(ln.rstd_ready, nth)
    return nc.vector.tensor_scalar(out, x, ln.mv[:n, 0:1], ln.rstd[:n, :], ALU.subtract, ALU.mult)


def norm_power(nc, sh, pool, ln, nth, n=T):
    pool.wait_ge(ln.var_ready, nth)
    nc.gpsimd.tensor_tensor(ln.rstd[:n, :], ln.veps[:n, :], sh.c("minus_half")[:n, 0:1],
                            ALU.pow).then_inc(ln.rstd_ready, 1)


def norm_memory(nc, ctx, prefix, sem):
    ln = Shared()
    ln.stats = ctx.enter_context(nc.sbuf_tensor(prefix + "stats", [128, 6], F32))
    ln.mv = ctx.enter_context(nc.sbuf_tensor(prefix + "mean_var", [128, 2], F32))
    ln.veps = ctx.enter_context(nc.sbuf_tensor(prefix + "var_eps", [128, 1], F32))
    ln.rstd = ctx.enter_context(nc.sbuf_tensor(prefix + "rstd", [128, 1], F32))
    ln.var_ready = sem("var_ready")
    ln.passed = sem("passed")
    ln.rstd_ready = sem("rstd_ready")
    return ln



def linear_attention(nc, sh):
    with ExitStack() as ctx:
        sb = lambda name, shape, dt=F32: ctx.enter_context(nc.sbuf_tensor("la_" + name, shape, dt))
        sem = sem_maker(nc, ctx, "la_")
        ps = sh.ps
        ln = norm_memory(nc, ctx, "la_", sem)
        w = sb("wqkv", [128, 2, 3 * D])
        bias = sb("bias", [T, 3 * D])
        xn = sb("xn", [T, D])
        xnTs = sb("xnTs", [128, 2, T])
        qk = sb("qk", [T, 2 * D])
        mx = sb("mx", [T, 32])
        rs = sb("rs", [T, 32])
        v = sb("v", [T, D])
        vsc = sb("vsc", [T, 2, 2, 129])
        ck = sb("ck", [T, D])
        kvm = sb("kvm", [128, 4, 2, 136])
        qT = sb("qT", [128, 2, T])
        cqT = sb("cqT", [128, 2, T])
        t1 = sb("t1", [T, 4, 136])
        t2 = sb("t2", [T, 4, 136])
        zr = sb("zr", [T, 4, 8])
        at = sb("at", [T, D])
        P_T, P_QK, P_V, P_KV, P_A = 0, 1, 2, 3, 7
        xn_ready, xnT_mm, xnT_ready = sem("xn_ready"), sem("xnT_mm"), sem("xnT_ready")
        qkv_mm, v_ready, vsc_ready = sem("qkv_mm"), sem("v_ready"), sem("vsc_ready")
        shifted, exp_done, qk_ready, ck_ready = sem("shifted"), sem("exp_done"), sem("qk_ready"), sem("ck_ready")
        kv_mm, kvm_ready, qT_mm, qT_ready, cqT_ready = (
            sem("kv_mm"), sem("kvm_ready"), sem("qT_mm"), sem("qT_ready"), sem("cqT_ready"))
        out_mm, at_ready, aT_mm, aT_ready = sem("out_mm"), sem("at_ready"), sem("aT_mm"), sem("aT_ready")
        chain1, chain2, k_seen = sem("chain1"), sem("chain2"), sem("k_seen")
        loaded = sem("loaded")
        sin_col, cos_col = sh.c("sincos")[:T, 0:1], sh.c("sincos")[:T, 1:2]
        LINKS1, LINKS2 = 7, 6
        block = ctx.enter_context(nc.Block())

        @block.sync
        def _(sp):
            sp.dma_start(sh.const[:, :], sh.consts_in[:, 0:N_CONST]).then_inc(sh.const_loaded, 16)
            sp.dma_start(sh.X[:, :, :], sh.ins["x"].rearrange("b t d -> t b d")).then_inc(sh.x_loaded, 16)
            for j, name in enumerate(("Wq", "Wk", "Wv")):
                sp.dma_start(w[:, :, j * D:(j + 1) * D],
                             sh.ins["L0_attn_" + name].rearrange("(c p) n -> p c n", p=128)).then_inc(loaded, 16)
            for j, name in enumerate(("bq", "bk", "bv")):
                sp.dma_start(bias[:, j * D:(j + 1) * D],
                             sh.ins["L0_attn_" + name].partition_broadcast(T)).then_inc(loaded, 16)
            for dst, src, name in sh.early_loads:
                sp.dma_start(dst, src).then_inc(sh.w_loaded[name], 16)

        @block.gpsimd
        def _(pool):
            pool.wait_ge(sh.const_loaded, 16)

            def step(i):
                norm_power(nc, sh, pool, ln, i + 1)
                pool.wait_ge(qk_ready, i + 1)
                pool.sem_inc(k_seen, 1)
                nc.gpsimd.tensor_scalar(ck[:, :], qk[:, D:2 * D], -1.0, 1.0, ALU.mult, ALU.add).then_inc(ck_ready, 1)

            with pool.Fori(0, B) as i:
                step(i)

        @block.scalar
        def _(act):
            act.wait_ge(sh.const_loaded, 16)
            for c in range(2):
                nc.scalar.copy(vsc[:, c, :, 128], sh.c("sincos")[:T, :])

            def before(i):
                act.wait_ge(xnT_mm, i + 1)
                nc.scalar.copy(xnTs[:, :, :], ps[:, P_T, 0:2 * T].rearrange("p (c t) -> p c t", c=2)).then_inc(xnT_ready, 1)
                act.wait_ge(v_ready, i + 1)
                vv = v[:, :].rearrange("p (c n) -> p c n", c=2)
                nc.scalar.mul(vsc[:, :, 0, 0:128], vv, sin_col)
                nc.scalar.mul(vsc[:, :, 1, 0:128], vv, cos_col).then_inc(vsc_ready, 1)
                act.wait_ge(shifted, i + 1)
                nc.scalar.activation(qk[:, :], qk[:, :], ACT.Exp).then_inc(exp_done, 1)

            def queries(i):
                act.wait_ge(qT_mm, i + 1)
                nc.scalar.copy(qT[:, :, :], ps[:, P_A, 0:2 * T].rearrange("p (c t) -> p c t", c=2)).then_inc(qT_ready, 1)

            def after(i):
                act.wait_ge(aT_mm, i + 1)
                nc.scalar.copy(sh.attnT[:, :, i, :], ps[:, P_A, 0:2 * T].rearrange("p (c t) -> p c t", c=2)).then_inc(aT_ready, 1)

            before(0)
            with act.Fori(0, B - 1) as i:
                queries(i)
                before(i + 1)
                after(i)
            queries(B - 1)
            after(B - 1)

        @block.vector
        def _(dve):
            dve.wait_ge(sh.x_loaded, 16)

            def before(i):
                link = chained(dve, chain1, i * LINKS1)
                norm_rows(nc, sh, dve, link, ln, sh.X[:, i, :], xn[:, :], nth=i + 1).then_inc(xn_ready, 1)
                dve.wait_ge(qkv_mm, i + 1)
                nc.vector.tensor_tensor(v[:, :], ps[:T, P_V, 0:D], bias[:, 2 * D:3 * D], ALU.add).then_inc(v_ready, 1)
                link(nc.vector.tensor_tensor(qk[:, :], ps[:T, P_QK, :], bias[:, 0:2 * D], ALU.add))
                q3 = qk[:, :].rearrange("p (g d) -> p g d", d=DA)
                link(nc.vector.tensor_reduce(mx[:, :], q3, AX.X, ALU.max))
                nc.vector.tensor_tensor(q3, q3, bc(mx[:, :], DA), ALU.subtract).then_inc(shifted, 1)
                dve.wait_ge(exp_done, i + 1)
                link(nc.vector.tensor_reduce(rs[:, :], q3, AX.X, ALU.add))
                link(nc.vector.reciprocal(rs[:, :], rs[:, :]))
                n = link(nc.vector.tensor_tensor(q3, q3, bc(rs[:, :], DA), ALU.mult))
                nc.vector.sem_inc(qk_ready, 1)
                assert n == LINKS1

            def after(i):
                link = chained(dve, chain2, i * LINKS2)
                dve.wait_ge(kv_mm, i + 1)
                for rc in range(4):
                    nc.vector.tensor_tensor(kvm[:, rc, :, 0:128],
                                            ps[:, P_KV + rc, 0:258].rearrange("p (s n) -> p s n", s=2)[:, :, 0:128],
                                            mid(sh.c("block16"), 2), ALU.mult)
                sums = ps[:, P_KV:P_KV + 4, 0:258].rearrange("p r (s n) -> p r s n", s=2)[:, :, :, 128]
                for s in range(2):
                    last = nc.vector.tensor_tensor(kvm[:, :, s, 128:136], bc(sums[:, :, s], 8),
                                                   mid(sh.c("head16"), 4), ALU.mult)
                last.then_inc(kvm_ready, 1)
                dve.wait_ge(qT_ready, i + 1)
                nc.vector.tensor_scalar(cqT[:, :, :], qT[:, :, :], -1.0, 1.0, ALU.mult, ALU.add).then_inc(cqT_ready, 1)
                dve.wait_ge(out_mm, i + 1)
                o = ps[:T, P_KV:P_KV + 4, 0:272].rearrange("p r (s n) -> p r s n", s=2)
                link(nc.vector.tensor_scalar(t1[:, :, :], o[:, :, 1, :], cos_col, None, ALU.mult))
                link(nc.vector.scalar_tensor_tensor(t2[:, :, :], o[:, :, 0, :], sin_col, t1[:, :, :], ALU.mult, ALU.add))
                link(nc.vector.tensor_scalar(zr[:, :, :], t2[:, :, 128:136], 1e-6, None, ALU.max))
                link(nc.vector.reciprocal(zr[:, :, :], zr[:, :, :]))
                link(nc.vector.tensor_tensor(t1[:, :, 0:128].rearrange("p r (h d) -> p r h d", d=DA),
                                             t2[:, :, 0:128].rearrange("p r (h d) -> p r h d", d=DA),
                                             bc(zr[:, :, :], DA), ALU.mult))
                n = link(nc.vector.tensor_tensor(at[:, :].rearrange("p (c n) -> p c n", c=2),
                                                 t1[:, 0:2, 0:128], t1[:, 2:4, 0:128], ALU.add))
                nc.vector.sem_inc(at_ready, 1)
                assert n == LINKS2

            dve.wait_ge(sh.const_loaded, 16)
            dve.wait_ge(loaded, 96)
            before(0)
            with dve.Fori(0, B - 1) as i:
                before(i + 1)
                after(i)
            after(B - 1)

        @block.tensor
        def _(pe):
            pe.wait_ge(sh.const_loaded, 16)
            pe.wait_ge(loaded, 96)
            ident = sh.c("ident")

            def before(i):
                pe.wait_ge(xn_ready, i + 1)
                for c in range(2):
                    last = nc.tensor.transpose(ps[:, P_T, c * T:(c + 1) * T], xn[:, c * 128:(c + 1) * 128], ident[:T, :T])
                last.then_inc(xnT_mm, 1)
                pe.wait_ge(xnT_ready, i + 1)
                for lo, hi, bank in ((0, 2 * D, P_QK), (2 * D, 3 * D, P_V)):
                    for c in range(2):
                        last = nc.tensor.matmul(ps[:T, bank, 0:hi - lo], xnTs[:, c, :], w[:, c, lo:hi],
                                                start=(c == 0), stop=(c == 1))
                last.then_inc(qkv_mm, 1)

            def keys(i):
                pe.wait_ge(qk_ready, i + 1)
                pe.wait_ge(ck_ready, i + 1)
                pe.wait_ge(vsc_ready, i + 1)
                for r, k in enumerate((qk[:, D:2 * D], ck[:, :])):
                    for c in range(2):
                        last = nc.tensor.matmul(ps[:, P_KV + 2 * r + c, 0:258], k[:, c * 128:(c + 1) * 128],
                                                vsc[:, c, :, :].rearrange("p s n -> p (s n)"), start=True, stop=True)
                last.then_inc(kv_mm, 1)
                if i is not FIRST:
                    pe.wait_ge(aT_ready, i)
                for c in range(2):
                    last = nc.tensor.transpose(ps[:, P_A, c * T:(c + 1) * T],
                                               qk[:, c * 128:(c + 1) * 128], ident[:T, :T])
                last.then_inc(qT_mm, 1)

            def result(i):
                pe.wait_ge(kvm_ready, i + 1)
                pe.wait_ge(qT_ready, i + 1)
                pe.wait_ge(cqT_ready, i + 1)
                for r, q in enumerate((qT, cqT)):
                    for c in range(2):
                        rc = 2 * r + c
                        last = nc.tensor.matmul(ps[:T, P_KV + rc, 0:272], q[:, c, :],
                                                kvm[:, rc, :, :].rearrange("p s n -> p (s n)"), start=True, stop=True)
                last.then_inc(out_mm, 1)
                pe.wait_ge(at_ready, i + 1)
                for c in range(2):
                    last = nc.tensor.transpose(ps[:, P_A, c * T:(c + 1) * T], at[:, c * 128:(c + 1) * 128], ident[:T, :T])
                last.then_inc(aT_mm, 1)

            before(0)
            keys(FIRST)
            before(1)
            result(0)
            with pe.Fori(1, B - 1) as i:
                keys(i)
                before(i + 1)
                result(i)
            keys(B - 1)
            result(B - 1)



def add_and_norm(nc, sh, tag, gather, weight=None, bias=None, keep_rows=False):
    with ExitStack() as ctx:
        sb = lambda name, shape, dt=F32: ctx.enter_context(nc.sbuf_tensor(tag + name, shape, dt))
        sem = sem_maker(nc, ctx, tag)
        ps = sh.ps
        ln = norm_memory(nc, ctx, tag, sem)
        own = sb("own", [128, 2, T])
        xn = sb("xn", [T, D])
        own_ready, y_mm, xn_ready, xnT_mm, xnT_ready = (
            sem("own_ready"), sem("y_mm"), sem("xn_ready"), sem("xnT_mm"), sem("xnT_ready"))
        chain = sem("chain")
        LINKS = 3 + (bias is not None)
        block = ctx.enter_context(nc.Block())
        n_own = len(gather(0).shape)

        @block.gpsimd
        def _(pool):
            with pool.Fori(0, B) as i:
                norm_power(nc, sh, pool, ln, i + 1)

        @block.scalar
        def _(act):
            def copy_in(i):
                dst = own[:, :, :] if n_own == 3 else own[:, :, :].rearrange("p c (l b) -> p c l b", b=B)
                nc.scalar.copy(dst, gather(i)).then_inc(own_ready, 1)

            copy_in(0)
            with act.Fori(0, B - 1) as i:
                act.wait_ge(y_mm, i + 1)
                copy_in(i + 1)
                act.wait_ge(xnT_mm, i + 1)
                nc.scalar.copy(sh.xnT[:, :, i, :], ps[:, 4, 0:2 * T].rearrange("p (c t) -> p c t", c=2)).then_inc(xnT_ready, 1)
            act.wait_ge(xnT_mm, B)
            nc.scalar.copy(sh.xnT[:, :, B - 1, :], ps[:, 4, 0:2 * T].rearrange("p (c t) -> p c t", c=2)).then_inc(xnT_ready, 1)

        @block.vector
        def _(dve):
            with dve.Fori(0, B) as i:
                link = chained(dve, chain, i * LINKS)
                dve.wait_ge(y_mm, i + 1)
                link(nc.vector.tensor_tensor(sh.X[:, i, :], sh.X[:, i, :], ps[:T, 0, 0:D], ALU.add))
                if bias is not None:
                    link(nc.vector.tensor_tensor(sh.X[:, i, :], sh.X[:, i, :], bias, ALU.add))
                norm_rows(nc, sh, dve, link, ln, sh.X[:, i, :], xn[:, :], nth=i + 1).then_inc(xn_ready, 1)

        @block.tensor
        def _(pe):
            ident = sh.c("ident")

            def product(i):
                pe.wait_ge(own_ready, i + 1)
                for c in range(2):
                    if weight is None:
                        last = nc.tensor.transpose(ps[:T, 0, c * 128:(c + 1) * 128], own[:, c, :], ident)
                    else:
                        last = nc.tensor.matmul(ps[:T, 0, 0:D], own[:, c, :], weight[:, c, :], start=(c == 0), stop=(c == 1))
                last.then_inc(y_mm, 1)

            def transposes(i):
                pe.wait_ge(xn_ready, i + 1)
                for c in range(2):
                    last = nc.tensor.transpose(ps[:, 4, c * T:(c + 1) * T], xn[:, c * 128:(c + 1) * 128], ident[:T, :T])
                last.then_inc(xnT_mm, 1)

            product(0)
            transposes(0)
            with pe.Fori(1, B) as i:
                product(i)
                pe.wait_ge(xnT_ready, i)
                transposes(i)


def bias_columns(nc, sh):
    with ExitStack() as ctx:
        sem = sem_maker(nc, ctx, "bc_")
        rows = [ctx.enter_context(nc.sbuf_tensor(f"bc_rows{n}", [128, 128], F32)) for n in range(2)]
        rows_loaded, cols_mm = sem("rows_loaded"), sem("cols_mm")
        made = sem("made")
        block = ctx.enter_context(nc.Block())
        ident = sh.c("ident")
        small = [("L1_ffn_b_c_proj", 16), ("L1_xattn_g1", 2), ("L1_xattn_b1", 2), ("L1_xattn_g2", 2),
                 ("L1_xattn_b2", 2), ("L0_xattn_b_Q", 2), ("L0_xattn_b_K", 2), ("L0_xattn_b_V", 2)]

        @block.sync
        def _(sp):
            for n, name in enumerate(("L1_ffn_b_c_fc", "L1_ffn_b_gate")):
                sp.dma_start(rows[0][64 * n:64 * n + 64, :],
                             sh.ins[name].rearrange("e o (j p) -> (e o j) p", p=128)).then_inc(rows_loaded, 16)
            at = 0
            for name, n in small:
                src = sh.ins[name]
                src = src.rearrange("e o (j p) -> (e o j) p", p=128) if n == 16 else src.rearrange("(j p) -> j p", p=128)
                sp.dma_start(rows[1][at:at + n, :], src).then_inc(rows_loaded, 16)
                at += n

        @block.tensor
        def _(pe):
            pe.wait_ge(rows_loaded, 16 * (2 + len(small)))
            nc.tensor.transpose(sh.ps[:, 0, 0:128], rows[0][:, :], ident)
            nc.tensor.transpose(sh.ps[:, 0, 128:158], rows[1][:30, :], ident[:30, :30]).then_inc(cols_mm, 1)

        @block.vector
        def _(dve):
            dve.wait_ge(cols_mm, 1)
            nc.vector.tensor_copy(sh.columns[:, 0:158], sh.ps[:, 0, 0:158]).then_inc(made, 1)
            dve.wait_ge(made, 1)
            nc.vector.tensor_scalar(sh.columns[:, 158:160], sh.columns[:, 152:154], 0.25, None, ALU.mult)



class Plan:

    def __init__(self, n_prep, n_fin, fin_at, n_slots):
        self.n_prep, self.n_fin = n_prep, n_fin
        full = [("prep", k) for k in range(n_prep)]
        for k, at in enumerate(fin_at):
            full.insert(at, ("fin", k))
        assert full[-1][0] == "prep"
        self.full, self.n_slots = full, n_slots
        self.only_prep = [s for s in full if s[0] == "prep"]
        self.only_fin = [s for s in full if s[0] == "fin"]

    def base(self, b):
        return self.n_prep - self.n_fin + b * (self.n_prep + self.n_fin)

    def prep_end(self, b):
        return self.n_prep if isinstance(b, int) and b == 0 else self.n_prep * 2 + (b - 1) * (self.n_prep + self.n_fin)

    def slots(self, steps):
        n = self.n_slots
        cut = [round(s * len(steps) / n) for s in range(n + 1)]
        return [[(p, *steps[p]) for p in range(cut[s], cut[s + 1])] for s in range(n)]


def attention(nc, sh, cfg):
    with ExitStack() as ctx:
        tag = cfg.tag
        sb = lambda name, shape, dt=F32: ctx.enter_context(nc.sbuf_tensor(tag + name, shape, dt))
        sem = sem_maker(nc, ctx, tag)
        ps = sh.ps
        H, dh, HS, KT, NC = cfg.heads, cfg.dh, cfg.per_stage, cfg.keys, cfg.key_chunks
        KCH = KT // NC
        NS = H // HS
        HD = H * dh
        NF = cfg.out_chunks
        ln = norm_memory(nc, ctx, tag, sem)
        v = sb("v", [KCH, 2, NC, NF, (128 // dh) * (128 + dh)])
        cfg.v_at = lambda par, k: v[:, par, k, :, :].rearrange("p c (j x) -> p c j x", x=128 + dh)[:, :, :, 0:dh]
        cfg.allocate(ctx, sb, sem)
        cleared = sem("cleared")
        probs = sb("probs", [T, 2, HS, KT])
        pT = sb("pT", [KCH, 2, HS * NC * T])
        negmax = sb("negmax", [T, 2, H])
        sums = sb("sums", [T, 2, H])
        inv = sb("inv", [T, H])
        inv_wide = sb("inv_wide", [T, H, dh])
        invT = sb("invT", [128, NF, T])
        oT = sb("oT", [128, NF, T])
        y = sb("y", [T, D])
        xn = sb("xn", [T, D])
        scores_mm, max_done, exp_done = sem("scores_mm"), sem("max_done"), sem("exp_done")
        pT_mm, pT_ready, o_mm, o_ready, inv_ready = (
            sem("pT_mm"), sem("pT_ready"), sem("o_mm"), sem("o_ready"), sem("inv_ready"))
        side_mm, side_done, xn_ready = sem("side_mm"), sem("side_done"), sem("xn_ready")
        chain_i, chain_o, chain_x = sem("chain_i"), sem("chain_o"), sem("chain_x")
        cfg.sem_side_done = side_done
        n_prep = len(cfg.prep_mm)
        n_fin = cfg.n_oT_steps + 2
        plan = Plan(n_prep, n_fin, cfg.fin_at, NS + 2)
        BANK_S, BANK_PT, BANK_O, BANK_SIDE, N_SIDE = cfg.banks
        s_banks = cfg.score_banks
        n_ptb = cfg.pt_buffers
        YSTEP = cfg.n_oT_steps
        block = ctx.enter_context(nc.Block())

        def scores_bank(par, x):
            if s_banks == 1:
                return ps[:T, BANK_S + par, x * KT:(x + 1) * KT]
            return ps[:T, BANK_S + par * s_banks + x, 0:KT]

        def scores_all(par):
            if s_banks == 1:
                return ps[:T, BANK_S + par, 0:HS * KT].rearrange("p (h k) -> p h k", h=HS)
            return ps[:T, BANK_S + par * s_banks:BANK_S + (par + 1) * s_banks, 0:KT]

        per_bank = HS if s_banks == 1 else 1
        pt_banks = HS // per_bank

        def pT_psum(par, x, k):
            bank = BANK_PT + (par % n_ptb) * pt_banks + x // per_bank
            col = (x % per_bank * NC + k) * T
            return ps[:KCH, bank, col:col + T]

        def pT_psum_all(par):
            bank = BANK_PT + (par % n_ptb) * pt_banks
            return ps[:KCH, bank:bank + pt_banks, 0:per_bank * NC * T]

        hpc = 128 // dh
        c_per_bank = NF if NF * T <= 512 else 4

        @block.sync
        def _(sp):
            cfg.sync(sp, plan)

        @block.gpsimd
        def _(pool):
            for u in range(2):
                nc.gpsimd.memset(v[:, u, :, :, :], 0.0).then_inc(cleared, 1)
            if dh == 64:
                nc.gpsimd.memset(cfg.qT[:, :, :, :, :], 0.0).then_inc(cleared, 1)
            cfg.pool(pool, plan, ln)

        @block.scalar
        def _(act):
            def side(p, kind, k, base, b, par):
                act.wait_ge(side_mm, base + p + 1)
                bank = BANK_SIDE + p % N_SIDE
                if kind == "prep":
                    last = cfg.prep_act(k, ps[:, bank, :], b + 1, par)
                elif k < cfg.n_oT_steps:
                    n = NF // cfg.n_oT_steps
                    last = nc.scalar.copy(invT[:, k * n:(k + 1) * n, :], ps[:, bank, 0:n * T].rearrange("p (c t) -> p c t", c=n))
                elif k == YSTEP:
                    last = nc.scalar.copy(y[:, :], ps[:T, bank, 0:D])
                else:
                    last = cfg.xnT_act(b - 1, ps[:, bank, 0:2 * T].rearrange("p (c t) -> p c t", c=2))
                last.then_inc(side_done, 1)

            def exps(b, par, i):
                act.wait_ge(max_done, b * NS + i + 1)
                for x, h in enumerate(cfg.stage_heads(i)):
                    last = nc.scalar.activation(probs[:, i % 2, x, :], scores_bank(i % 2, x), ACT.Exp,
                                                bias=negmax[:, par, h:h + 1], scale=cfg.scale,
                                                accum_out=sums[:, par, h:h + 1])
                last.then_inc(exp_done, 1)

            def iteration(b, par, steps, base):
                for s, todo in enumerate(plan.slots(steps)):
                    for p, kind, k in todo:
                        side(p, kind, k, base, b, 1 - par)
                    if s < NS:
                        exps(b, par, s)

            cfg.wait_weights(act)
            act.wait_ge(cleared, 2 + (dh == 64))
            for p, (kind, k) in enumerate(plan.only_prep):
                side(p, kind, k, 0, -1, 0)
            iteration(0, 0, plan.only_prep, plan.n_prep)
            with act.Fori(1, B - 2, 2) as b:
                iteration(b, 1, plan.full, plan.base(b))
                iteration(b + 1, 0, plan.full, plan.base(b + 1))
            iteration(B - 1, 1, plan.only_fin, plan.base(B - 1))
            for p, (kind, k) in enumerate(plan.only_fin):
                side(p, kind, k, plan.base(B - 1) + plan.n_fin, B, None)

        @block.vector
        def _(dve):
            LINKS_X = 3 + (cfg.out_bias is not None) + 3 * cfg.twice

            def residual(b, base, p):
                link = chained(dve, chain_x, b * LINKS_X)
                dve.wait_ge(side_done, base + p + 1)
                n = link(nc.vector.tensor_tensor(sh.X[:, b, :], sh.X[:, b, :], y[:, :], ALU.add))
                if cfg.out_bias is not None:
                    n = link(nc.vector.tensor_tensor(sh.X[:, b, :], sh.X[:, b, :], cfg.out_bias, ALU.add))
                if cfg.twice:
                    link(norm_rows(nc, sh, dve, link, ln, sh.X[:, b, :], xn[:, :], nth=b * 2 + 1))
                    norm_rows(nc, sh, dve, link, ln, xn[:, :], xn[:, :], nth=b * 2 + 2).then_inc(xn_ready, 1)
                else:
                    norm_rows(nc, sh, dve, link, ln, sh.X[:, b, :], xn[:, :], nth=b + 1).then_inc(xn_ready, 1)
                    if cfg.keep_rows:
                        nc.vector.tensor_scalar(sh.XN[:, b, :], sh.X[:, b, :], ln.mv[:T, 0:1], ln.rstd[:T, :],
                                                ALU.subtract, ALU.mult)

            def inverse_sums(b, par):
                dve.wait_ge(exp_done, b * NS + NS)
                nc.vector.reciprocal(inv[:, :], sums[:, par, :]).then_inc(chain_i, 1)
                dve.wait_ge(chain_i, b + 1)
                nc.vector.tensor_copy(inv_wide[:, :, :], bc(inv[:, :], dh)).then_inc(inv_ready, 1)

            def scale_heads(b, base, p):
                dve.wait_ge(side_done, base + p + 1)
                dve.wait_ge(o_mm, b + 1)
                for n in range(NF // c_per_bank):
                    cs = slice(n * c_per_bank, (n + 1) * c_per_bank)
                    last = nc.vector.tensor_tensor(oT[:, cs, :], invT[:, cs, :],
                                                   ps[:, BANK_O + n, 0:c_per_bank * T].rearrange("p (c t) -> p c t", t=T), ALU.mult)
                if cfg.v_bias is not None:
                    last.then_inc(chain_o, 1)
                    dve.wait_ge(chain_o, b + 1)
                    for c in range(NF):
                        last = nc.vector.tensor_scalar(oT[:, c, :], oT[:, c, :], cfg.v_bias[:, c:c + 1], None, ALU.add)
                last.then_inc(o_ready, 1)

            def iteration(b, par, steps, base):
                slots = plan.slots(steps)
                due = None
                for s in range(NS + 2):
                    for p, kind, k in slots[s]:
                        if (kind, k) == ("fin", YSTEP - 1):
                            scale_heads(b - 1, base, p)
                    if s < NS:
                        dve.wait_ge(scores_mm, b * NS + s + 1)
                        nc.vector.tensor_reduce(negmax[:, par, cfg.stage_columns(s)], scores_all(s % 2),
                                                AX.X, ALU.max, negate=True).then_inc(max_done, 1)
                    if 1 <= s <= NS:
                        dve.wait_ge(pT_mm, b * NS + s)
                        nc.vector.tensor_copy(pT[:, (s - 1) % 2, :].rearrange("p (n k) -> p n k", n=pt_banks),
                                              pT_psum_all((s - 1) % 2)).then_inc(pT_ready, 1)
                    if due is not None:
                        residual(b - 1, base, due)
                        due = None
                    for p, kind, k in slots[s]:
                        if (kind, k) == ("fin", YSTEP):
                            due = p
                    if cfg.dve_slot:
                        cfg.dve_slot(dve, s, b, 1 - par, ln, steps is not plan.only_fin)
                if due is not None:
                    residual(b - 1, base, due)
                inverse_sums(b, par)

            cfg.wait_weights(dve)
            if cfg.dve_before:
                cfg.dve_before(dve, ln)
            iteration(0, 0, plan.only_prep, plan.n_prep)
            with dve.Fori(1, B - 2, 2) as b:
                iteration(b, 1, plan.full, plan.base(b))
                iteration(b + 1, 0, plan.full, plan.base(b + 1))
            iteration(B - 1, 1, plan.only_fin, plan.base(B - 1))
            scale_heads(B - 1, plan.base(B - 1) + plan.n_fin, YSTEP - 1)
            residual(B - 1, plan.base(B - 1) + plan.n_fin, YSTEP)

        @block.tensor
        def _(pe):
            ident = sh.c("ident")

            def side(p, kind, k, base, b, par):
                if p < N_SIDE:
                    if not (isinstance(base, int) and base == 0):
                        pe.wait_ge(side_done, base)
                else:
                    pe.wait_ge(side_done, base + p - N_SIDE + 1)
                bank = BANK_SIDE + p % N_SIDE
                if kind == "prep":
                    last = cfg.prep_mm[k](pe, k, ps[:, bank, :], b + 1, base + p, par)
                elif k < cfg.n_oT_steps:
                    pe.wait_ge(inv_ready, b)
                    n = NF // cfg.n_oT_steps
                    for c in range(n):
                        f = k * n + c
                        last = nc.tensor.transpose(ps[:, bank, c * T:(c + 1) * T], inv_wide[:, f * hpc:(f + 1) * hpc, :].rearrange("p h d -> p (h d)"), ident[:T, :T])
                elif k == YSTEP:
                    pe.wait_ge(o_ready, b)
                    for c in range(NF):
                        last = nc.tensor.matmul(ps[:T, bank, 0:D], oT[:, c, :], cfg.w_out[:, c, :],
                                                start=(c == 0), stop=(c == NF - 1))
                else:
                    pe.wait_ge(xn_ready, b)
                    for c in range(2):
                        last = nc.tensor.transpose(ps[:, bank, c * T:(c + 1) * T], xn[:, c * 128:(c + 1) * 128], ident[:T, :T])
                last.then_inc(side_mm, 1)

            steps_at = {}

            def order(steps):
                steps_at.clear()
                steps_at.update({s: p for p, s in enumerate(steps)})

            cfg.steps_at = steps_at

            def stage_scores(b, par, i):
                for x, h in enumerate(cfg.stage_heads(i)):
                    q, kk = cfg.head_operands(par, h)
                    last = nc.tensor.matmul(scores_bank(i % 2, x), q, kk, start=True, stop=True)
                last.then_inc(scores_mm, 1)

            def stage_transposes(b, i):
                pe.wait_ge(exp_done, b * NS + i + 1)
                if not (isinstance(b, int) and b == 0 and i < n_ptb):
                    pe.wait_ge(pT_ready, b * NS + i + 1 - n_ptb)
                for x in range(HS):
                    for k in range(NC):
                        last = nc.tensor.transpose(pT_psum(i, x, k), probs[:, i % 2, x, k * KCH:(k + 1) * KCH], ident[:T, :T])
                last.then_inc(pT_mm, 1)

            def stage_values(b, par, i):
                pe.wait_ge(pT_ready, b * NS + i + 1)
                if i == 0 and not (isinstance(b, int) and b == 0):
                    pe.wait_ge(o_ready, b)
                for x, h in enumerate(cfg.stage_heads(i)):
                    c, j = h // hpc, h % hpc
                    bank, col = BANK_O + c // c_per_bank, c % c_per_bank * T
                    for k in range(NC):
                        at = (x * NC + k) * T
                        last = nc.tensor.matmul(ps[:, bank, col:col + T], v[:, par, k, c, j * 128:(j + 1) * 128], pT[:, i % 2, at:at + T],
                                                start=(j == 0 and k == 0), stop=(j == hpc - 1 and k == NC - 1))
                if i == NS - 1:
                    last.then_inc(o_mm, 1)

            def iteration(b, par, steps, base):
                order(steps)
                pe.wait_ge(side_done, plan.prep_end(b))
                if dh == 16:
                    pe.wait_ge(cfg.q_ready, b + 1)
                for s, todo in enumerate(plan.slots(steps)):
                    if s < NS:
                        stage_scores(b, par, s)
                    for p, kind, k in todo:
                        side(p, kind, k, base, b, 1 - par)
                    if 1 <= s <= NS:
                        stage_transposes(b, s - 1)
                    if s >= 2:
                        stage_values(b, par, s - 2)

            cfg.wait_weights(pe)
            order(plan.only_prep)
            for p, (kind, k) in enumerate(plan.only_prep):
                side(p, kind, k, 0, -1, 0)
            iteration(0, 0, plan.only_prep, plan.n_prep)
            with pe.Fori(1, B - 2, 2) as b:
                iteration(b, 1, plan.full, plan.base(b))
                iteration(b + 1, 0, plan.full, plan.base(b + 1))
            iteration(B - 1, 1, plan.only_fin, plan.base(B - 1))
            for p, (kind, k) in enumerate(plan.only_fin):
                side(p, kind, k, plan.base(B - 1) + plan.n_fin, B, None)


def load_context(nc, sh, cfg, sp, plan):
    src = sh.ins["ctx_1024"].rearrange("b (j p) d -> b p j d", p=KC)

    def load(b, u):
        sp.dma_start(cfg.ctx_in[:, u, :, :], src[b]).then_inc(cfg.ctx_loaded[u], 16)

    load(0, 0)
    load(1, 1)
    sp.wait_ge(cfg.sem_side_done, cfg.ctx_last_use + 1)
    load(2, 0)
    sp.wait_ge(cfg.sem_side_done, plan.n_prep + cfg.ctx_last_use + 1)
    load(3, 1)
    at = plan.full.index(("prep", cfg.ctx_last_use))
    with sp.Fori(4, B - 1, 2) as b:
        for u in range(2):
            sp.wait_ge(cfg.sem_side_done, plan.base(b + u - 3) + at + 1)
            load(b + u, u)



def context_attention_0(nc, sh, w):
    cfg = Shared()
    cfg.tag, cfg.heads, cfg.dh, cfg.per_stage, cfg.keys, cfg.key_chunks = "c0_", 16, 16, 2, S, NK
    cfg.out_chunks, cfg.n_oT_steps = 2, 1
    cfg.banks, cfg.score_banks, cfg.pt_buffers = (0, 4, 6, 7, 1), 2, 1
    cfg.scale = 1.0
    cfg.fin_at = [0, 4, 8]
    cfg.twice = cfg.keep_rows = False
    cfg.out_bias, cfg.v_bias, cfg.w_out = w.bo[:, :], w.bv, w.wo
    cfg.dve_slot = None
    cfg.dve_before = None
    cfg.norm_nth = None
    ident = sh.c("ident")

    cfg.stage_heads = lambda i: [2 * i, 2 * i + 1]
    cfg.stage_columns = lambda i: slice(2 * i, 2 * i + 2)

    def allocate(ctx, sb, sem):
        cfg.ctx_in = sb("ctx_in", [KC, 2, NK, D])
        cfg.ctxT = sb("ctxT", [128, 2, S])
        cfg.kT = sb("kT", [128, 2, 2, S])
        cfg.q_all = sb("q_all", [128, 2, T])
        cfg.qT = sb("qT", [128, 2, 2, 8, T])
        cfg.q_ready = sem("q_ready")
        cfg.ctx_loaded = [sem(f"ctx_loaded{u}") for u in range(2)]

    cfg.allocate = allocate

    def head_operands(par, h):
        return cfg.qT[:, par, h // 8, h % 8, :], cfg.kT[:, par, h // 8, :]

    cfg.head_operands = head_operands

    def wait_weights(eng):
        eng.wait_ge(sh.w_loaded["c0"], w.n_loads * 16)

    cfg.wait_weights = wait_weights

    def transposes(pe, k, bank, b, at, par):
        if k == 1:
            pe.wait_ge(cfg.ctx_loaded[par], b * 8 + 16 - 8 * par)
        for j in range(NK):
            last = nc.tensor.transpose(bank[:, j * KC:(j + 1) * KC], cfg.ctx_in[:, par, j, (k - 1) * 128:k * 128], ident[:KC, :KC])
        return last

    def keys(pe, k, bank, b, at, par):
        m = k - 3
        if m == 0:
            pe.wait_ge(cfg.sem_side_done, at)
        for c in range(2):
            last = nc.tensor.matmul(bank[:, 0:S], w.wk[:, c, m * 128:(m + 1) * 128], cfg.ctxT[:, c, :], start=(c == 0), stop=(c == 1))
        return last

    def values(pe, k, bank, b, at, par):
        for j in ((0, 1) if k == 5 else (2,)):
            for c in range(2):
                last = nc.tensor.matmul(bank[:KC, j % 2 * D:(j % 2 + 1) * D], cfg.ctxT[:, c, j * KC:(j + 1) * KC],
                                        w.wv[:, c, :], start=(c == 0), stop=(c == 1))
        return last

    def queries(pe, k, bank, b, at, par):
        for m in range(2):
            for c in range(2):
                last = nc.tensor.matmul(bank[:, m * T:(m + 1) * T], w.wq[:, c, m * 128:(m + 1) * 128], sh.xnT[:, c, b, :],
                                        start=(c == 0), stop=(c == 1))
        return last

    cfg.prep_mm = [queries, transposes, transposes, keys, keys, values, values]
    cfg.ctx_last_use = 2

    def prep_act(k, bank, b, par):
        if k == 0:
            for m in range(2):
                last = nc.scalar.activation(cfg.q_all[:, m, :], bank[:, m * T:(m + 1) * T], ACT.Identity,
                                            bias=w.bq_scaled[:, m:m + 1], scale=0.25)
            return last
        if k < 3:
            return nc.scalar.copy(cfg.ctxT[:, k - 1, :], bank[:, 0:S])
        if k < 5:
            return nc.scalar.activation(cfg.kT[:, par, k - 3, :], bank[:, 0:S], ACT.Identity, bias=w.bk[:, k - 3:k - 2])
        if k == 5:
            for j in range(2):
                last = nc.scalar.copy(cfg.v_at(par, j), bank[:KC, j * D:(j + 1) * D].rearrange("p (c j d) -> p c j d", c=2, d=16))
            return last
        return nc.scalar.copy(cfg.v_at(par, 2), bank[:KC, 0:D].rearrange("p (c j d) -> p c j d", c=2, d=16))

    cfg.prep_act = prep_act
    cfg.xnT_act = lambda b, src: nc.scalar.copy(sh.xnT[:, :, b, :], src)

    cfg.sync = lambda sp, plan: load_context(nc, sh, cfg, sp, plan)

    def pool(eng, plan, ln):
        at = plan.full.index(("prep", 0))

        def masked_queries(par, side_steps):
            eng.wait_ge(cfg.sem_side_done, side_steps)
            for m in range(2):
                last = nc.gpsimd.tensor_tensor(cfg.qT[:, par, m, :, :], mid(cfg.q_all[:, m, :], 8), bc(sh.c("head16"), T), ALU.mult)
            last.then_inc(cfg.q_ready, 1)

        masked_queries(0, 1)
        masked_queries(1, plan.n_prep + 1)
        with eng.Fori(1, B - 2, 2) as b:
            for u in range(2):
                masked_queries(u, plan.base(b + u) + at + 1)
                norm_power(nc, sh, eng, ln, b + u)
        norm_power(nc, sh, eng, ln, B - 1)
        norm_power(nc, sh, eng, ln, B)

    cfg.pool = pool
    attention(nc, sh, cfg)




def top_two(nc, link, v, n, width, count, m):
    for best, hot in ((m.m1, m.oh1), (m.m2, m.oh2)):
        link(nc.vector.tensor_reduce(best[:, :], v[:, :, :], AX.X, ALU.max))
        link(nc.vector.tensor_tensor(m.t[:, :, :], v[:, :, :], bc(best[:, :], width), ALU.is_equal))
        link(nc.vector.tensor_tensor(m.t[:, :, :], m.t[:, :, :], mid(count, n), ALU.mult))
        link(nc.vector.tensor_reduce(m.r[:, :], m.t[:, :, :], AX.X, ALU.max))
        link(nc.vector.tensor_tensor(hot[:, :, :], m.t[:, :, :], bc(m.r[:, :], width), ALU.is_equal))
        if best is m.m1:
            link(nc.vector.scalar_tensor_tensor(v[:, :, :], hot[:, :, :], -FAR, v[:, :, :], ALU.mult, ALU.add))


def experts_0(nc, sh, w):
    NE = E0 + 1
    G = 4
    GT = G * T
    with ExitStack() as ctx:
        sb = lambda name, shape, dt=F32: ctx.enter_context(nc.sbuf_tensor("e0_" + name, shape, dt))
        sem = sem_maker(nc, ctx, "e0_")
        ps = sh.ps
        wT = sb("wT", [48, B, T], BF16)
        pick = sb("pick", [48, E0 * 128], BF16)
        with ExitStack() as gates:
            gb = lambda name, shape, dt=F32: gates.enter_context(nc.sbuf_tensor("e0_" + name, shape, dt))
            m = Shared()
            m.t, m.r, m.oh1, m.oh2 = gb("t", [T, B, E0]), gb("r", [T, B]), gb("oh1", [T, B, E0]), gb("oh2", [T, B, E0])
            m.m1, m.m2 = gb("m1", [T, B]), gb("m2", [T, B])
            v = gb("v", [T, B, E0])
            high, middle = gb("high", [T, B, E0], BF16), gb("middle", [T, B, E0], BF16)
            parts = gb("parts", [T, B, 3, E0])
            pick32 = gb("pick32", [48, E0 * 128])
            logits_mm, logit_ready, exp_done, parts_ready, wT_mm = (
                sem("logits_mm"), sem("logit_ready"), sem("exp_done"), sem("parts_ready"), sem("wT_mm"))
            chain, pick_loaded = sem("gate_chain"), sem("pick_loaded")
            with nc.Block() as block:
                @block.sync
                def _(sp):
                    sp.dma_start(pick32[:, :], sh.consts_in[0:48, N_CONST:N_CONST + E0 * 128]).then_inc(pick_loaded, 16)

                @block.gpsimd
                def _(pool):
                    pool.wait_ge(pick_loaded, 16)
                    nc.gpsimd.tensor_copy(pick[:, :], pick32[:, :])

                @block.tensor
                def _(pe):
                    pe.wait_ge(sh.w_loaded["gate0"], 32)
                    for b in range(B):
                        for c in range(2):
                            last = nc.tensor.matmul(ps[:T, 0, b * E0:(b + 1) * E0], sh.xnT[:, c, b, :], w.gate[:, c, :],
                                                    start=(c == 0), stop=(c == 1))
                    last.then_inc(logits_mm, 1)
                    pe.wait_ge(parts_ready, 1)
                    for g in range(B // G):
                        for u in range(G):
                            last = nc.tensor.transpose(ps[:48, 1 + g, u * T:(u + 1) * T],
                                                       parts[:, g * G + u, :, :].rearrange("p k e -> p (k e)"), sh.c("ident")[:T, :T])
                        last.then_inc(wT_mm, 1)

                @block.scalar
                def _(act):
                    act.wait_ge(logit_ready, 1)
                    nc.scalar.activation(v[:, :, :], v[:, :, :], ACT.Exp, scale=-1.0).then_inc(exp_done, 1)
                    for g in range(B // G):
                        act.wait_ge(wT_mm, g + 1)
                        nc.scalar.copy(wT[:, g * G:(g + 1) * G, :], ps[:48, 1 + g, 0:GT].rearrange("p (b t) -> p b t", b=G))

                @block.vector
                def _(dve):
                    link = chained(dve, chain, 0)
                    dve.wait_ge(sh.w_loaded["gate0"], 32)
                    dve.wait_ge(logits_mm, 1)
                    nc.vector.tensor_tensor(v[:, :, :], ps[:T, 0, 0:B * E0].rearrange("p (b e) -> p b e", e=E0),
                                            mid(w.gate_b[:, :], B), ALU.add).then_inc(logit_ready, 1)
                    dve.wait_ge(exp_done, 1)
                    link(nc.vector.tensor_scalar(v[:, :, :], v[:, :, :], 1.0, None, ALU.add))
                    link(nc.vector.reciprocal(v[:, :, :], v[:, :, :]))
                    top_two(nc, link, v, B, E0, sh.c("count16")[:T, :], m)
                    link(nc.vector.tensor_tensor(m.r[:, :], m.m1[:, :], m.m2[:, :], ALU.add))
                    link(nc.vector.reciprocal(m.r[:, :], m.r[:, :]))
                    link(nc.vector.tensor_tensor(m.m1[:, :], m.m1[:, :], m.r[:, :], ALU.mult))
                    link(nc.vector.tensor_tensor(m.m2[:, :], m.m2[:, :], m.r[:, :], ALU.mult))
                    link(nc.vector.tensor_tensor(m.oh1[:, :, :], m.oh1[:, :, :], bc(m.m1[:, :], E0), ALU.mult))
                    link(nc.vector.tensor_tensor(m.oh2[:, :, :], m.oh2[:, :, :], bc(m.m2[:, :], E0), ALU.mult))
                    link(nc.vector.tensor_tensor(v[:, :, :], m.oh1[:, :, :], m.oh2[:, :, :], ALU.add))
                    link(nc.vector.tensor_copy(high[:, :, :], v[:, :, :]))
                    link(nc.vector.tensor_tensor(v[:, :, :], v[:, :, :], high[:, :, :], ALU.subtract))
                    link(nc.vector.tensor_copy(middle[:, :, :], v[:, :, :]))
                    nc.vector.tensor_copy(parts[:, :, 0, :], high[:, :, :])
                    nc.vector.tensor_copy(parts[:, :, 1, :], middle[:, :, :])
                    nc.vector.tensor_tensor(parts[:, :, 2, :], v[:, :, :], middle[:, :, :], ALU.subtract).then_inc(parts_ready, 1)

        act_out = sb("act_out", [128, 2, GT])
        gated = sb("gated", [128, 2, GT])
        hidden = sb("hidden", [128, 2, GT])
        gate_mm, up_mm, silu_done, hidden_ready, sum_mm, sum_taken = (
            sem("gate_mm"), sem("up_mm"), sem("silu_done"), sem("hidden_ready"), sem("sum_mm"), sem("sum_taken"))
        chain = sem("chain")
        with nc.Block() as block:
            @block.scalar
            def _(act):
                with act.Fori(0, B // G) as g:
                    for e in range(NE):
                        act.wait_ge(gate_mm, g * NE + e + 1)
                        nc.scalar.activation(act_out[:, e % 2, :], ps[:, 3 * (e % 2), 0:GT], ACT.Silu).then_inc(silu_done, 1)

            @block.vector
            def _(dve):
                dve.sem_inc(sum_taken, 1)
                with dve.Fori(0, B // G) as g:
                    for e in range(NE):
                        par = e % 2
                        dve.wait_ge(silu_done, g * NE + e + 1)
                        dve.wait_ge(up_mm, g * NE + e + 1)
                        if e < E0:
                            nc.vector.tensor_tensor(gated[:, par, :], act_out[:, par, :], ps[:, 3 * par + 1, 0:GT], ALU.mult).then_inc(chain, 1)
                            dve.wait_ge(chain, g * E0 + e + 1)
                            nc.vector.tensor_tensor(hidden[:, par, :], gated[:, par, :], ps[:, 3 * par + 2, 0:GT], ALU.mult).then_inc(hidden_ready, 1)
                        else:
                            nc.vector.tensor_tensor(hidden[:, par, :], act_out[:, par, :], ps[:, 3 * par + 1, 0:GT], ALU.mult).then_inc(hidden_ready, 1)
                    dve.wait_ge(sum_mm, g + 1)
                    x = sh.xnT[:, :, bass.ds(g * G, G), :].rearrange("p c b t -> p c (b t)")
                    nc.vector.tensor_tensor(x, x, ps[:, 6:8, 0:GT], ALU.add).then_inc(sum_taken, 1)

            @block.tensor
            def _(pe):
                pe.wait_ge(sh.w_loaded["experts0"], 16 * 6)

                def down(g, e):
                    pe.wait_ge(hidden_ready, g * NE + e + 1)
                    if e == 0:
                        pe.wait_ge(sum_taken, g + 1)
                    for mo in range(2):
                        last = nc.tensor.matmul(ps[:, 6 + mo, 0:GT], w.down[:, e, mo * 128:(mo + 1) * 128], hidden[:, e % 2, :],
                                                start=(e == 0), stop=(e == NE - 1))
                    return last

                with pe.Fori(0, B // G) as g:
                    x = sh.xnT[:, :, bass.ds(g * G, G), :].rearrange("p c b t -> p c (b t)")
                    for e in range(NE):
                        bank = 3 * (e % 2)
                        for c in range(2):
                            last = nc.tensor.matmul(ps[:, bank, 0:GT], w.gates[:, e, c, :], x[:, c, :], start=(c == 0), stop=(c == 1))
                        last.then_inc(gate_mm, 1)
                        for c in range(2):
                            last = nc.tensor.matmul(ps[:, bank + 1, 0:GT], w.up[:, e, c, :], x[:, c, :], start=(c == 0), stop=(c == 1))
                        if e < E0:
                            last = nc.tensor.matmul(ps[:, bank + 2, 0:GT], pick[:, e * 128:(e + 1) * 128],
                                                    wT[:, bass.ds(g * G, G), :].rearrange("p b t -> p (b t)"), start=True, stop=True)
                        last.then_inc(up_mm, 1)
                        if e > 0:
                            down(g, e - 1)
                    down(g, NE - 1).then_inc(sum_mm, 1)



def self_attention_1(nc, sh, w):
    cfg = Shared()
    cfg.tag, cfg.heads, cfg.dh, cfg.per_stage, cfg.keys, cfg.key_chunks = "s1_", 16, 64, 4, T, 1
    cfg.out_chunks, cfg.n_oT_steps = 8, 2
    cfg.banks, cfg.score_banks, cfg.pt_buffers = (0, 2, 4, 6, 2), 1, 2
    cfg.scale = 1.0 / 8
    cfg.fin_at = [0, 1, 4, 8]
    cfg.twice, cfg.keep_rows = True, False
    cfg.out_bias = cfg.v_bias = None
    cfg.w_out = w.out
    cfg.dve_slot = cfg.dve_before = None
    cfg.stage_heads = lambda i: [4 * i + x for x in range(4)]
    cfg.stage_columns = lambda i: slice(4 * i, 4 * i + 4)
    wv = w.qkv[:, :, :].rearrange("p c (n j) -> p c j n", j=3)

    def allocate(ctx, sb, sem):
        cfg.kT = sb("kT", [128, 2, 8, T])
        cfg.qT = sb("qT", [128, 2, 2, 8, T])
        cfg.own = sb("own", [128, 2, T])

    cfg.allocate = allocate

    def head_operands(par, h):
        return cfg.qT[:, par, h % 2, h // 2, :], cfg.kT[:, par, h // 2, :]

    cfg.head_operands = head_operands
    cfg.wait_weights = lambda eng: eng.wait_ge(sh.w_loaded["s1"], 32)

    def queries_keys(pe, k, bank, b, at, par):
        for u in range(4):
            n = k % 2 * 4 + u
            for c in range(2):
                last = nc.tensor.matmul(bank[:, u * T:(u + 1) * T], wv[:, c, k // 2, n * 128:(n + 1) * 128], sh.xnT[:, c, b, :],
                                        start=(c == 0), stop=(c == 1))
        return last

    def values(pe, k, bank, b, at, par):
        if k == 4:
            pe.wait_ge(cfg.sem_side_done, at - 1)
        for c in range(2):
            last = nc.tensor.matmul(bank[:T, :], cfg.own[:, c, :], wv[:, c, 2, (k - 4) * 512:(k - 3) * 512],
                                    start=(c == 0), stop=(c == 1))
        return last

    cfg.prep_mm = [queries_keys] * 4 + [values] * 2

    def prep_act(k, bank, b, par):
        if k < 4:
            pairs, src = slice(k % 2 * 4, k % 2 * 4 + 4), bank[:, 0:4 * T].rearrange("p (u t) -> p u t", u=4)
            if k >= 2:
                return nc.scalar.copy(cfg.kT[:, par, pairs, :], src)
            for half in range(2):
                rows = slice(64 * half, 64 * half + 64)
                last = nc.scalar.copy(cfg.qT[rows, par, half, pairs, :], src[rows])
            if k == 0:
                last = nc.scalar.copy(cfg.own[:, :, :], sh.xnT[:, :, b, :])
            return last
        return nc.scalar.copy(cfg.v_at(par, 0)[:, (k - 4) * 4:(k - 3) * 4], bank[:T, :].rearrange("p (c j d) -> p c j d", c=4, d=64))

    cfg.prep_act = prep_act

    def xnT_act(b, src):
        for c in range(2):
            last = nc.scalar.activation(sh.xnT[:, c, b, :], src[:, c, :], ACT.Identity,
                                        bias=sh.columns[:, 146 + c:147 + c], scale=sh.columns[:, 144 + c:145 + c])
        return last

    cfg.xnT_act = xnT_act
    cfg.sync = lambda sp, plan: None

    def pool(eng, plan, ln):
        with eng.Fori(0, B) as b:
            norm_power(nc, sh, eng, ln, b * 2 + 1)
            norm_power(nc, sh, eng, ln, b * 2 + 2)

    cfg.pool = pool
    attention(nc, sh, cfg)



def context_attention_1(nc, sh, w):
    cfg = Shared()
    cfg.tag, cfg.heads, cfg.dh, cfg.per_stage, cfg.keys, cfg.key_chunks = "c1_", 8, 64, 1, S, NK
    cfg.out_chunks, cfg.n_oT_steps = 4, 1
    cfg.banks, cfg.score_banks, cfg.pt_buffers = (0, 2, 4, 5, 3), 1, 2
    cfg.scale = 1.0 / 8
    cfg.fin_at = [0, 3, 7]
    cfg.twice, cfg.keep_rows = False, True
    cfg.out_bias, cfg.v_bias, cfg.w_out = w.bo[:, :], None, w.out
    ident = sh.c("ident")
    cfg.stage_heads = lambda i: [i]
    cfg.stage_columns = lambda i: slice(i, i + 1)
    cfg.ctx_last_use = None

    def allocate(ctx, sb, sem):
        cfg.ctx_in = sb("ctx_in", [KC, 2, NK, D])
        cfg.cn = sb("cn", [KC, NK, D])
        cfg.ctxT = sb("ctxT", [128, 2, S])
        cfg.kT = sb("kT", [128, 2, 4, S])
        cfg.qT = sb("qT", [128, 2, 2, 4, T])
        cfg.stats = sb("ctx_stats", [KC, NK, 6])
        cfg.mv = sb("ctx_mean_var", [KC, NK, 2])
        cfg.veps = sb("ctx_var_eps", [KC, NK])
        cfg.rstd = sb("ctx_rstd", [KC, NK])
        cfg.ctx_loaded = [sem(f"ctx_loaded{u}") for u in range(2)]
        cfg.ctx_var, cfg.ctx_rstd, cfg.cn_ready, cfg.chain = sem("ctx_var"), sem("ctx_rstd"), sem("cn_ready"), sem("ctx_chain")

    cfg.allocate = allocate

    def head_operands(par, h):
        return cfg.qT[:, par, h % 2, h // 2, :], cfg.kT[:, par, h // 2, :]

    cfg.head_operands = head_operands
    cfg.wait_weights = lambda eng: eng.wait_ge(sh.w_loaded["c1"], 64)

    def queries(pe, k, bank, b, at, par):
        for m in range(4):
            for c in range(2):
                last = nc.tensor.matmul(bank[:, m * T:(m + 1) * T], w.q[:, c, m * 128:(m + 1) * 128], sh.xnT[:, c, b, :],
                                        start=(c == 0), stop=(c == 1))
        return last

    def transposes(pe, k, bank, b, at, par):
        if k == 1:
            pe.wait_ge(cfg.cn_ready, b + 1)
        for j in range(NK):
            last = nc.tensor.transpose(bank[:, j * KC:(j + 1) * KC], cfg.cn[:, j, (k - 1) * 128:k * 128], ident[:KC, :KC])
        return last

    def keys(pe, k, bank, b, at, par):
        m = k - 3
        if m == 0:
            pe.wait_ge(cfg.sem_side_done, at)
        for c in range(2):
            last = nc.tensor.matmul(bank[:, 0:S], w.kv[:, c, m * 128:(m + 1) * 128], cfg.ctxT[:, c, :], start=(c == 0), stop=(c == 1))
        return last

    def values(pe, k, bank, b, at, par):
        j = k - 7
        for c in range(2):
            last = nc.tensor.matmul(bank[:KC, :], cfg.ctxT[:, c, j * KC:(j + 1) * KC], w.kv[:, c, 512:1024], start=(c == 0), stop=(c == 1))
        return last

    cfg.prep_mm = [queries] + [transposes] * 2 + [keys] * 4 + [values] * 3

    def prep_act(k, bank, b, par):
        if k == 0:
            for half in range(2):
                rows = slice(64 * half, 64 * half + 64)
                last = nc.scalar.copy(cfg.qT[rows, par, half, :, :], bank[rows, 0:4 * T].rearrange("p (m t) -> p m t", m=4))
            return last
        if k < 3:
            c = k - 1
            return nc.scalar.activation(cfg.ctxT[:, c, :], bank[:, 0:S], ACT.Identity,
                                        bias=sh.columns[:, 150 + c:151 + c], scale=sh.columns[:, 148 + c:149 + c])
        if k < 7:
            return nc.scalar.copy(cfg.kT[:, par, k - 3, :], bank[:, 0:S])
        return nc.scalar.copy(cfg.v_at(par, k - 7), bank[:KC, :].rearrange("p (c j d) -> p c j d", c=4, d=64))

    cfg.prep_act = prep_act
    cfg.xnT_act = lambda b, src: nc.scalar.copy(sh.xnT[:, :, b, :], src)

    def context_norm(dve, b, par):
        link = chained(dve, cfg.chain, b * 2)
        dve.wait_ge(cfg.ctx_loaded[par], b * 8 + 16 - 8 * par)
        dve.sem_inc(cfg.passed, 1)
        for j in range(NK):
            last = nc.vector.bn_stats(cfg.stats[:, j, :], cfg.ctx_in[:, par, j, :])
        link(last, cfg.passed)
        for j in range(NK):
            last = nc.vector.bn_aggr(cfg.mv[:, j, :], cfg.stats[:, j, :])
        link(last)
        nc.vector.tensor_scalar(cfg.veps[:, :], cfg.mv[:, :, 1], LN_EPS, None, ALU.add).then_inc(cfg.ctx_var, 1)
        dve.wait_ge(cfg.ctx_rstd, b + 1)
        for j in range(NK):
            last = nc.vector.tensor_scalar(cfg.cn[:, j, :], cfg.ctx_in[:, par, j, :], cfg.mv[:, j, 0:1],
                                           cfg.rstd[:, j:j + 1], ALU.subtract, ALU.mult)
        last.then_inc(cfg.cn_ready, 1)

    def dve_before(dve, ln):
        cfg.passed = ln.passed
        context_norm(dve, 0, 0)
        dve.wait_ge(cfg.sem_side_done, 3)
        cfg.now = 0

    def dve_slot(dve, s, b, par, ln, more):
        if s == 0 and more:
            context_norm(dve, b + 1, par)

    cfg.dve_before, cfg.dve_slot = dve_before, dve_slot

    def pool(eng, plan, ln):
        def power():
            pass

        def of_context(b):
            eng.wait_ge(cfg.ctx_var, b + 1)
            nc.gpsimd.tensor_tensor(cfg.rstd[:, :], cfg.veps[:, :], sh.c("minus_half")[:KC, 0:NK], ALU.pow).then_inc(cfg.ctx_rstd, 1)

        of_context(0)
        of_context(1)
        with eng.Fori(0, B - 2) as b:
            of_context(b + 2)
            norm_power(nc, sh, eng, ln, b + 1)
        norm_power(nc, sh, eng, ln, B - 1)
        norm_power(nc, sh, eng, ln, B)

    cfg.pool = pool

    def sync(sp, plan):
        src = sh.ins["ctx_1024"].rearrange("b (j p) d -> b p j d", p=KC)
        for u in range(2):
            sp.dma_start(cfg.ctx_in[:, u, :, :], src[u]).then_inc(cfg.ctx_loaded[u], 16)
        with sp.Fori(2, B - 1, 2) as b:
            for u in range(2):
                sp.wait_ge(cfg.cn_ready, b + u - 1)
                sp.dma_start(cfg.ctx_in[:, u, :, :], src[b + u]).then_inc(cfg.ctx_loaded[u], 16)

    cfg.sync = sync
    attention(nc, sh, cfg)



def experts_1(nc, sh, w):
    NS = E1 * CAP
    HALF = B * CAP // 2
    NJ = H1 // 128
    with ExitStack() as ctx:
        sb = lambda name, shape, dt=F32: ctx.enter_context(nc.sbuf_tensor("e1_" + name, shape, dt))
        sem = sem_maker(nc, ctx, "e1_")
        ps = sh.ps
        m = Shared()
        m.t, m.r, m.oh1, m.oh2 = sb("t", [T, B, E1]), sb("r", [T, B]), sb("oh1", [T, B, E1]), sb("oh2", [T, B, E1])
        m.m1, m.m2 = sb("m1", [T, B]), sb("m2", [T, B])
        lg = sb("lg", [T, B, E1])
        pos = sb("pos", [T, 2, B])
        held = sb("held", [T, 2, B])
        prob = sb("prob", [T, 2, B])
        ex = sb("ex", [128, 2, E1, B * CAP])
        logits_mm, hot_ready, counts_mm, diff_ready, ediff_ready, chain = (
            sem("logits_mm"), sem("hot_ready"), sem("counts_mm"), sem("diff_ready"), sem("ediff_ready"), sem("chain"))

        wfc, wgt = sb("wfc", [128, 2, 2, H1]), sb("wgt", [128, 2, 2, H1])
        wpj = sb("wpj", [128, 2, NJ, D])
        w_in = [sem(f"w_in{u}") for u in range(2)]

        def load_expert(sp, e, u):
            for dst, name, pat in ((wgt, "w_gate", "e (c p) n -> e p c n"), (wfc, "w_c_fc", "e (c p) n -> e p c n"),
                                   (wpj, "w_c_proj", "e (j p) n -> e p j n")):
                sp.dma_start(dst[:, u, :, :], sh.ins["L1_ffn_" + name].rearrange(pat, p=128)[e]).then_inc(w_in[u], 16)

        with nc.Block() as block:
            @block.sync
            def _(sp):
                load_expert(sp, 0, 0)
                load_expert(sp, 1, 1)

            @block.tensor
            def _(pe):
                pe.wait_ge(sh.w_loaded["router1"], 32)
                for b in range(B):
                    for c in range(2):
                        last = nc.tensor.matmul(ps[:T, 0, b * E1:(b + 1) * E1], sh.xnT[:, c, b, :], w.router[:, c, :],
                                                start=(c == 0), stop=(c == 1))
                last.then_inc(logits_mm, 1)
                pe.wait_ge(hot_ready, 1)
                flat = lambda a: a[:, :, :].rearrange("p b e -> p (b e)")
                nc.tensor.matmul(ps[:T, 1, 0:B * E1], sh.c("upto")[:T, :], flat(m.oh1), start=True, stop=True)
                nc.tensor.matmul(ps[:T, 2, 0:B * E1], sh.c("upto")[:T, :], flat(m.oh2), start=True, stop=False)
                nc.tensor.matmul(ps[:T, 2, 0:B * E1], sh.c("ones")[:T, :], flat(m.oh1), start=False, stop=True).then_inc(counts_mm, 1)

            @block.scalar
            def _(act):
                act.wait_ge(diff_ready, 1)
                nc.scalar.activation(prob[:, 1, :], m.r[:, :], ACT.Exp).then_inc(ediff_ready, 1)

            @block.vector
            def _(dve):
                link = chained(dve, chain, 0)
                dve.wait_ge(sh.w_loaded["router1"], 32)
                dve.wait_ge(logits_mm, 1)
                link(nc.vector.tensor_tensor(lg[:, :, :], ps[:T, 0, 0:B * E1].rearrange("p (b e) -> p b e", e=E1),
                                             mid(w.router_b[:, :], B), ALU.add))
                top_two(nc, link, lg, B, E1, sh.c("count16")[:T, 16 - E1:16], m)
                dve.sem_inc(hot_ready, 1)
                nc.vector.tensor_tensor(m.r[:, :], m.m2[:, :], m.m1[:, :], ALU.subtract).then_inc(diff_ready, 1)
                dve.wait_ge(ediff_ready, 1)
                link(nc.vector.tensor_scalar(prob[:, 0, :], prob[:, 1, :], 1.0, None, ALU.add))
                link(nc.vector.reciprocal(prob[:, 0, :], prob[:, 0, :]))
                link(nc.vector.tensor_tensor(prob[:, 1, :], prob[:, 1, :], prob[:, 0, :], ALU.mult))
                dve.wait_ge(counts_mm, 1)
                for n, hot in enumerate((m.oh1, m.oh2)):
                    link(nc.vector.tensor_tensor(m.t[:, :, :], hot[:, :, :], ps[:T, 1 + n, 0:B * E1].rearrange("p (b e) -> p b e", e=E1), ALU.mult))
                    link(nc.vector.tensor_reduce(pos[:, n, :], m.t[:, :, :], AX.X, ALU.add))
                link(nc.vector.tensor_scalar(pos[:, :, :], pos[:, :, :], -1.0, None, ALU.add))
                link(nc.vector.tensor_scalar(held[:, :, :], pos[:, :, :], float(CAP - 1), None, ALU.min))

        sel = sb("sel", [T, 2, CAP])
        part = sb("part", [T, 2, E1, CAP])
        oneh = sb("oneh", [T, E1, CAP])
        own = sb("own", [T, D])
        oneh_ready, own_ready, slots_mm, slots_ready, sel_chain = (
            sem("oneh_ready"), sem("own_ready"), sem("slots_mm"), sem("slots_ready"), sem("sel_chain"))

        def one_hot(dve, link, at, b, scaled):
            for n in range(2):
                if scaled:
                    last = nc.vector.tensor_scalar(sel[:, n, :], sh.c("slots")[:T, :], at[:, n, b:b + 1] if isinstance(b, int) else at[:, n, bass.ds(b, 1)],
                                                   prob[:, n, b:b + 1] if isinstance(b, int) else prob[:, n, bass.ds(b, 1)], ALU.is_equal, ALU.mult)
                else:
                    last = nc.vector.tensor_scalar(sel[:, n, :], sh.c("slots")[:T, :], at[:, n, b:b + 1] if isinstance(b, int) else at[:, n, bass.ds(b, 1)],
                                                   None, ALU.is_equal)
            link(last)
            for n, hot in enumerate((m.oh1, m.oh2)):
                last = nc.vector.tensor_tensor(part[:, n, :, :], bc(hot[:, b, :], CAP), mid(sel[:, n, :], E1), ALU.mult)
            link(last)

        with nc.Block() as block:
            @block.vector
            def _(dve):
                def step(b, first=False):
                    link = chained(dve, sel_chain, b * 2)
                    one_hot(dve, link, pos, b, False)
                    if not first:
                        dve.wait_ge(slots_mm, b)
                    nc.vector.tensor_tensor(oneh[:, :, :], part[:, 0, :, :], part[:, 1, :, :], ALU.add).then_inc(oneh_ready, 1)

                step(0, True)
                with dve.Fori(1, B) as b:
                    step(b)

            @block.scalar
            def _(act):
                def take(b):
                    act.wait_ge(slots_mm, b + 1)
                    for c in range(2):
                        last = nc.scalar.copy(ex[:, c, :, bass.ds(b * CAP, CAP)], ps[:, c, 0:NS].rearrange("p (e s) -> p e s", e=E1))
                    last.then_inc(slots_ready, 1)

                nc.scalar.copy(own[:, :], sh.XN[:, 0, :]).then_inc(own_ready, 1)
                with act.Fori(0, B - 1) as b:
                    take(b)
                    nc.scalar.copy(own[:, :], sh.XN[:, b + 1, :]).then_inc(own_ready, 1)
                take(B - 1)

            @block.tensor
            def _(pe):
                def step(b, first=False):
                    pe.wait_ge(own_ready, b + 1)
                    pe.wait_ge(oneh_ready, b + 1)
                    if not first:
                        pe.wait_ge(slots_ready, b)
                    for c in range(2):
                        last = nc.tensor.matmul(ps[:, c, 0:NS], own[:, c * 128:(c + 1) * 128],
                                                oneh[:, :, :].rearrange("p e s -> p (e s)"), start=True, stop=True)
                    last.then_inc(slots_mm, 1)

                step(0, True)
                with pe.Fori(1, B) as b:
                    step(b)

        gbuf = sb("gbuf", [128, 2, HALF])
        ubuf = sb("ubuf", [128, 2, 2, HALF])
        hid = sb("hid", [128, 2, 2, HALF])
        g_mm, h_mm, g_taken, u_ready, hid_ready, expert_mm, out_taken, passed = (
            sem("g_mm"), sem("h_mm"), sem("g_taken"), sem("u_ready"), sem("hid_ready"), sem("expert_mm"), sem("out_taken"), sem("passed"))
        with nc.Block() as block:
            @block.sync
            def _(sp):
                with sp.Fori(2, E1 - 1, 2) as e:
                    for u in range(2):
                        sp.wait_ge(expert_mm, e + u - 1)
                        load_expert(sp, e + u, u)

            @block.scalar
            def _(act):
                act.sem_inc(g_taken, 1)
                with act.Fori(0, E1 - 1, 2) as e2:
                    for n in range(2 * NJ):
                        e, j = e2 + n // NJ, n % NJ
                        n_all = e2 * NJ + n
                        act.wait_ge(g_mm, n_all + 1)
                        act.sem_inc(passed, 1)
                        nc.scalar.activation(gbuf[:, :, :], ps[:, 2:4, 0:HALF], ACT.Identity,
                                             bias=sh.columns[:, bass.ds(n_all + 64, 1)]).then_inc(g_taken, 1)
                        act.wait_ge(u_ready, n_all + 2)
                        nc.scalar.activation(hid[:, j % 2, :, :], ubuf[:, j % 2, :, :], ACT.Silu).then_inc(hid_ready, 1)

            @block.vector
            def _(dve):
                dve.sem_inc(u_ready, 1)
                dve.sem_inc(out_taken, 1)
                with dve.Fori(0, E1 - 1, 2) as e2:
                    for n in range(2 * NJ):
                        e, j = e2 + n // NJ, n % NJ
                        n_all = e2 * NJ + n
                        dve.wait_ge(h_mm, n_all + 1)
                        dve.wait_ge(g_taken, n_all + 2)
                        nc.vector.scalar_tensor_tensor(ubuf[:, j % 2, :, :], ps[:, 0:2, 0:HALF], sh.columns[:, bass.ds(n_all, 1)],
                                                       gbuf[:, :, :], ALU.add, ALU.mult).then_inc(u_ready, 1)
                        if j == NJ - 1:
                            dve.wait_ge(expert_mm, e + 1)
                            for mo in range(2):
                                last = nc.vector.tensor_scalar(ex[:, mo, e, :].rearrange("p (a n) -> p a n", a=2),
                                                               ps[:, 4 + 2 * mo:6 + 2 * mo, 0:HALF],
                                                               sh.columns[:, bass.ds(e * 2 + 128 + mo, 1)], None, ALU.add)
                            last.then_inc(out_taken, 1)

            @block.tensor
            def _(pe):
                def hidden_products(e, u, j, n_all):
                    for wt, bank, free, done in ((wgt, 2, g_taken, g_mm), (wfc, 0, u_ready, h_mm)):
                        pe.wait_ge(free, n_all + 1)
                        for half in range(2):
                            for c in range(2):
                                last = nc.tensor.matmul(ps[:, bank + half, 0:HALF], wt[:, u, c, j * 128:(j + 1) * 128],
                                                        ex[:, c, e, half * HALF:(half + 1) * HALF], start=(c == 0), stop=(c == 1))
                        last.then_inc(done, 1)

                def out_products(e, u, j, n_all):
                    pe.wait_ge(hid_ready, n_all + 1)
                    if j == 0:
                        pe.wait_ge(out_taken, e + 1)
                    for mo in range(2):
                        for half in range(2):
                            last = nc.tensor.matmul(ps[:, 4 + 2 * mo + half, 0:HALF], wpj[:, u, j, mo * 128:(mo + 1) * 128],
                                                    hid[:, j % 2, half, :], start=(j == 0), stop=(j == NJ - 1))
                    if j == NJ - 1:
                        last.then_inc(expert_mm, 1)

                with pe.Fori(0, E1 - 1, 2) as e2:
                    for u in range(2):
                        e = e2 + u
                        pe.wait_ge(w_in[u], e2 * 24 + 48)
                        for j in range(NJ):
                            hidden_products(e, u, j, e * NJ + j)
                            if j > 0:
                                out_products(e, u, j - 1, e * NJ + j - 1)
                        out_products(e, u, NJ - 1, e * NJ + NJ - 1)

        CH = [(0, 3), (3, 6), (6, 8)]
        own_ex = sb("own_ex", [128, 2, E1, CAP])
        gT = sb("gT", [3 * CAP, 3, T])
        oS = sb("oS", [3 * CAP, 3, D])
        ohc_ready, ownx_ready, tr_mm, tr_ready, y_mm, x_ready, comb_chain = (
            sem("ohc_ready"), sem("ownx_ready"), sem("tr_mm"), sem("tr_ready"), sem("y_mm"), sem("x_ready"), sem("comb_chain"))
        stored = sem("stored")
        with nc.Block() as block:
            @block.sync
            def _(sp):
                with sp.Fori(0, B) as b:
                    sp.wait_ge(x_ready, b + 1)
                    sp.dma_start(sh.out[b], sh.X[:, b, :]).then_inc(stored, 16)
                sp.wait_ge(stored, 16 * B)

            @block.vector
            def _(dve):
                def matrix(b, first=False):
                    link = chained(dve, comb_chain, b * 2)
                    one_hot(dve, link, held, b, True)
                    if not first:
                        dve.wait_ge(tr_mm, b)
                    nc.vector.tensor_tensor(oneh[:, :, :], part[:, 0, :, :], part[:, 1, :, :], ALU.add).then_inc(ohc_ready, 1)

                def rows(b):
                    dve.wait_ge(y_mm, b + 1)
                    nc.vector.tensor_tensor(sh.X[:, b, :], sh.X[:, b, :], ps[:T, 3, 0:D], ALU.add).then_inc(x_ready, 1)

                matrix(0, True)
                with dve.Fori(0, B - 1) as b:
                    matrix(b + 1)
                    rows(b)
                rows(B - 1)

            @block.gpsimd
            def _(pool):
                def step(b, first=False):
                    if not first:
                        pool.wait_ge(tr_mm, b)
                        pool.sem_inc(passed, 1)
                    for c in range(2):
                        last = nc.gpsimd.tensor_copy(own_ex[:, c, :, :], ex[:, c, :, bass.ds(b * CAP, CAP)])
                    last.then_inc(ownx_ready, 1)

                step(0, True)
                with pool.Fori(1, B) as b:
                    step(b)

            @block.scalar
            def _(act):
                def step(b, first=False):
                    act.wait_ge(tr_mm, b + 1)
                    if not first:
                        act.wait_ge(y_mm, b)
                    nc.scalar.copy(gT[:, 0:2, :], ps[:3 * CAP, 0, 0:2 * T].rearrange("p (q t) -> p q t", q=2))
                    nc.scalar.copy(gT[:2 * CAP, 2, :], ps[:2 * CAP, 0, 2 * T:3 * T])
                    nc.scalar.copy(oS[:, 0:2, :], ps[:3 * CAP, 1, :].rearrange("p (q n) -> p q n", q=2))
                    nc.scalar.copy(oS[:2 * CAP, 2, :], ps[:2 * CAP, 2, 0:D]).then_inc(tr_ready, 1)

                step(0, True)
                with act.Fori(1, B) as b:
                    step(b)

            @block.tensor
            def _(pe):
                ident = sh.c("ident")

                def transposes(b):
                    pe.wait_ge(ohc_ready, b + 1)
                    pe.wait_ge(ownx_ready, b + 1)
                    for q, (lo, hi) in enumerate(CH):
                        n = (hi - lo) * CAP
                        nc.tensor.transpose(ps[:n, 0, q * T:(q + 1) * T], oneh[:, lo:hi, :].rearrange("p e s -> p (e s)"), ident[:T, :T])
                        for c in range(2):
                            last = nc.tensor.transpose(ps[:n, 1 + q // 2, q % 2 * D + c * 128:q % 2 * D + (c + 1) * 128],
                                                       own_ex[:, c, lo:hi, :].rearrange("p e s -> p (e s)"), ident)
                    last.then_inc(tr_mm, 1)

                def product(b, first=False):
                    pe.wait_ge(tr_ready, b + 1)
                    if not first:
                        pe.wait_ge(x_ready, b)
                    for q, (lo, hi) in enumerate(CH):
                        n = (hi - lo) * CAP
                        last = nc.tensor.matmul(ps[:T, 3, 0:D], gT[:n, q, :], oS[:n, q, :], start=(q == 0), stop=(q == 2))
                    last.then_inc(y_mm, 1)

                transposes(0)
                product(0, True)
                with pe.Fori(1, B) as b:
                    transposes(b)
                    product(b)


def decoder(nc, ins, consts_in, out):
    with ExitStack() as ctx:
        sb = lambda name, shape, dt=F32: ctx.enter_context(nc.sbuf_tensor(name, shape, dt))
        sem = lambda name: ctx.enter_context(nc.semaphore(name))
        sh = Shared()
        sh.ins, sh.consts_in, sh.out = ins, consts_in, out
        sh.const = sb("const", [128, N_CONST])
        sh.c = lambda name: sh.const[:, CONSTS[name][0]:CONSTS[name][0] + CONSTS[name][1]]
        sh.X = sb("X", [T, B, D])
        sh.xnT = sb("xnT", [128, 2, B, T])
        sh.columns = sb("columns", [128, 160])
        sh.ps = ctx.enter_context(nc.psum_tensor("ps", [128, 8, 512], F32))
        sh.const_loaded, sh.x_loaded, stored = sem("const_loaded"), sem("x_loaded"), sem("stored")
        sh.w_loaded = {}
        sh.early_loads = []

        def early(name, dst, src):
            if name not in sh.w_loaded:
                sh.w_loaded[name] = sem("loaded_" + name)
            sh.early_loads.append((dst, src, name))

        sh.early = early
        layer0 = ExitStack()
        s0 = lambda name, shape, dt=F32: layer0.enter_context(nc.sbuf_tensor(name, shape, dt))
        wo0 = s0("wo0", [128, 2, D])
        bo0 = s0("bo0", [T, D])
        early("wo0", wo0[:, :, :], ins["L0_attn_Wo"].rearrange("(c p) n -> p c n", p=128))
        early("wo0", bo0[:, :], ins["L0_attn_bo"].partition_broadcast(T))
        w0 = Shared()
        w0.bv, w0.bo = sh.columns[:, 156:158], s0("c0_bo", [T, D])
        early("c0", w0.bo[:, :], ins["L0_xattn_b_O"].partition_broadcast(T))
        w0.n_loads = 5
        w0.bk, w0.bq_scaled = sh.columns[:, 154:156], sh.columns[:, 158:160]
        w0.wq, w0.wk, w0.wv, w0.wo = (s0("c0_w" + n, [128, 2, D]) for n in "qkvo")
        for n, t in (("Q", w0.wq), ("K", w0.wk), ("V", w0.wv), ("O", w0.wo)):
            early("c0", t[:, :, :], ins["L0_xattn_W_" + n].rearrange("(c p) n -> p c n", p=128))
        with nc.sbuf_tensor("attnT", [128, 2, B, T], F32) as attnT:
            sh.attnT = attnT
            linear_attention(nc, sh)
            L = T // B
            permuted = attnT[:, :, :, :].rearrange("p c b l -> p c l b")
            with nc.Block() as block:
                @block.tensor
                def _(pe):
                    pe.wait_ge(sh.w_loaded["wo0"], 32)

                @block.vector
                def _(dve):
                    dve.wait_ge(sh.w_loaded["wo0"], 32)
            add_and_norm(nc, sh, "ao_", lambda i: permuted[:, :, bass.ds(i * L, L), :], wo0, bo0[:, :])
        bias_columns(nc, sh)
        weights = Shared()

        def load_now(name, dst, src):
            if name not in sh.w_loaded:
                sh.w_loaded[name] = sem("loaded_" + name)
            sh.now.append((dst, src, name))

        def issue():
            with nc.Block() as block:
                @block.sync
                def _(sp):
                    for dst, src, name in sh.now:
                        sp.dma_start(dst, src).then_inc(sh.w_loaded[name], 16)
            sh.now = []

        sh.now = []
        with layer0:
            e0 = Shared()
            e0.gate, e0.gate_b = s0("e0_gate", [128, 2, E0]), s0("e0_gate_b", [T, E0])
            e0.gates, e0.up, e0.down = (s0("e0_gates", [128, E0 + 1, 2, I0]), s0("e0_up", [128, E0 + 1, 2, I0]),
                                        s0("e0_down", [128, E0 + 1, D]))
            load_now("gate0", e0.gate[:, :, :], ins["L0_ffn_gate_w"].rearrange("(c p) n -> p c n", p=128))
            load_now("gate0", e0.gate_b[:, :], ins["L0_ffn_gate_b"].partition_broadcast(T))
            for dst, name in ((e0.gates, "wg"), (e0.up, "wu")):
                load_now("experts0", dst[:, 0:E0, :, :], ins["L0_ffn_experts_" + name].rearrange("e (c p) n -> p e c n", p=128))
                load_now("experts0", dst[:, E0, :, :], ins["L0_ffn_shared_" + name].rearrange("(c p) n -> p c n", p=128))
            load_now("experts0", e0.down[:, 0:E0, :], ins["L0_ffn_experts_wd"].rearrange("e p n -> p e n"))
            load_now("experts0", e0.down[:, E0, :], ins["L0_ffn_shared_wd"])
            issue()
            context_attention_0(nc, sh, w0)
            experts_0(nc, sh, e0)
            add_and_norm(nc, sh, "ea_", lambda i: sh.xnT[:, :, i, :])
        s1, c1, e1 = Shared(), Shared(), Shared()
        e1.router, e1.router_b = sb("e1_router", [128, 2, E1]), sb("e1_router_b", [T, E1])
        sh.XN = sb("XN", [T, B, D])
        attentions1 = ctx.enter_context(ExitStack())
        sa = lambda name, shape, dt=F32: attentions1.enter_context(nc.sbuf_tensor(name, shape, dt))
        s1.qkv, s1.out = sa("s1_qkv", [128, 2, 3072]), sa("s1_out", [128, 8, D])
        load_now("s1", s1.qkv[:, :, :], ins["L1_attn_W_qkv"].rearrange("(c p) n -> p c n", p=128))
        load_now("s1", s1.out[:, :, :], ins["L1_attn_W_out"].rearrange("(c p) n -> p c n", p=128))
        c1.q, c1.kv, c1.out, c1.bo = (sa("c1_q", [128, 2, 512]), sa("c1_kv", [128, 2, 1024]), sa("c1_out", [128, 4, D]),
                                      sa("c1_bo", [T, D]))
        load_now("c1", c1.q[:, :, :], ins["L1_xattn_Wq"].rearrange("(c p) n -> p c n", p=128))
        load_now("c1", c1.kv[:, :, :], ins["L1_xattn_Wkv"].rearrange("(c p) n -> p c n", p=128))
        load_now("c1", c1.out[:, :, :], ins["L1_xattn_Wout"].rearrange("(c p) n -> p c n", p=128))
        load_now("c1", c1.bo[:, :], ins["L1_xattn_bout"].partition_broadcast(T))
        load_now("router1", e1.router[:, :, :], ins["L1_ffn_router_w"].rearrange("(c p) n -> p c n", p=128))
        load_now("router1", e1.router_b[:, :], ins["L1_ffn_router_b"].partition_broadcast(T))
        issue()
        self_attention_1(nc, sh, s1)
        context_attention_1(nc, sh, c1)
        attentions1.close()
        experts_1(nc, sh, e1)


_INS = ["x", "ctx_1024"] + ["L0_attn_" + n for n in ("Wq", "bq", "Wk", "bk", "Wv", "bv", "Wo", "bo")] \
    + ["L0_xattn_" + n for n in ("W_Q", "b_Q", "W_K", "b_K", "W_V", "b_V", "W_O", "b_O")] \
    + ["L0_ffn_" + n for n in ("gate_w", "gate_b", "shared_wg", "shared_wu", "shared_wd", "experts_wg", "experts_wu", "experts_wd")] \
    + ["L1_attn_W_qkv", "L1_attn_W_out"] \
    + ["L1_xattn_" + n for n in ("g1", "b1", "g2", "b2", "Wq", "Wkv", "Wout", "bout")] \
    + ["L1_ffn_" + n for n in ("router_w", "router_b", "w_c_fc", "b_c_fc", "w_gate", "b_gate", "w_c_proj", "b_c_proj")]


def kernel(**inputs):
    import numpy as _np
    import concourse.bacc as _bacc
    from concourse import mybir as _mybir
    from concourse.bass_utils import run_bass_kernel_spmd as _run

    nc = _bacc.Bacc("TRN2", target_bir_lowering=False, num_devices=1)
    arrays, ins = {}, {}
    for name in _INS:
        a = _np.ascontiguousarray(inputs[name])
        arrays["in_" + name] = a
        ins[name] = nc.dram_tensor("in_" + name, a.shape, _mybir.dt.from_np(a.dtype), kind="ExternalInput").ap()
    arrays["in_consts"] = CONST_ARRAY
    consts_in = nc.dram_tensor("in_consts", CONST_ARRAY.shape, _mybir.dt.float32, kind="ExternalInput").ap()
    out = nc.dram_tensor("out", (B, T, D), _mybir.dt.float32, kind="ExternalOutput").ap()
    decoder(nc, ins, consts_in, out)
    r = _run(nc, [arrays], core_ids=[0])
    return r.results[0]["out"]
```

```python
import concourse.bass as bass
import concourse.mybir as mybir
import numpy as np
from contextlib import ExitStack

B, T, D = 16, 112, 256
S, KC, NK = 375, 125, 3
F32, BF16 = mybir.dt.float32, mybir.dt.bfloat16
ALU = mybir.AluOpType
ACT = mybir.ActivationFunctionType
AX = mybir.AxisListType
LN_EPS = 1e-5
HA, DA = 16, 16
E0, I0 = 16, 128
E1, H1 = 8, 1024
CAP = int(1.2 * 2 * T // E1)
FAR = 3.0e38

CONSTS = {}


def constant_columns():
    parts = []

    def put(name, a):
        a = np.asarray(a, np.float32)
        full = np.zeros((128, a.shape[1]), np.float32)
        full[: a.shape[0]] = a
        CONSTS[name] = (sum(x.shape[1] for x in parts), a.shape[1])
        parts.append(full)

    angle = (np.pi / 2 * np.arange(1, T + 1, dtype=np.float32) / T).astype(np.float32)
    put("ident", np.eye(128))
    put("block16", np.kron(np.eye(8), np.ones((16, 16))))
    put("head16", np.kron(np.eye(8), np.ones((16, 1))))
    put("sincos", np.stack([np.sin(angle), np.cos(angle)], 1))
    put("sincosT", np.tile(np.concatenate([np.sin(angle), np.cos(angle)]), (128, 1)))
    put("count16", np.tile(np.arange(16, 0, -1), (T, 1)))
    put("slots", np.tile(np.arange(CAP), (T, 1)))
    put("upto", np.triu(np.ones((T, T))))
    put("ones", np.ones((T, T)))
    put("minus_half", -0.5 * np.ones((128, 4)))
    pick = np.zeros((48, E0 * 128))
    for e in range(E0):
        for part in range(3):
            pick[part * 16 + e, e * 128:(e + 1) * 128] = 1
    put("pick", pick)
    return np.concatenate(parts, 1)


CONST_ARRAY = constant_columns()
N_CONST = CONSTS["pick"][0]


def bc(ap, n):
    return ap.unsqueeze(len(ap.shape)).broadcast_to(list(ap.shape) + [n])


def mid(ap, n):
    return ap.unsqueeze(1).broadcast_to([ap.shape[0], n, ap.shape[1]])


def chained(eng, sem, base):
    count = [0]

    def link(ins, apart=None):
        count[0] += 1
        ins.then_inc(sem, 1)
        eng.wait_ge(sem, base + count[0])
        if apart is not None:
            eng.sem_inc(apart, 1)
        return count[0]

    return link


class Shared:
    pass


def sem_maker(nc, ctx, prefix):
    held = []

    def give_back():
        nc.clear_and_free_semaphores(held)
        nc.all_engine_barrier()

    ctx.callback(give_back)

    def sem(name):
        held.append(nc.alloc_semaphore(name=prefix + name))
        return held[-1]

    return sem



LN_LINKS = 5


def norm_rows(nc, sh, dve, link, ln, x, out, n=T, nth=None):
    dve.sem_inc(ln.passed, 1)
    link(nc.vector.bn_stats(ln.stats[:n, :], x), ln.passed)
    link(nc.vector.bn_aggr(ln.mv[:n, :], ln.stats[:n, :]))
    nc.vector.tensor_scalar(ln.veps[:n, :], ln.mv[:n, 1:2], LN_EPS, None, ALU.add).then_inc(ln.var_ready, 1)
    dve.wait_ge(ln.rstd_ready, nth)
    return nc.vector.tensor_scalar(out, x, ln.mv[:n, 0:1], ln.rstd[:n, :], ALU.subtract, ALU.mult)


def norm_power(nc, sh, pool, ln, nth, n=T):
    pool.wait_ge(ln.var_ready, nth)
    nc.gpsimd.tensor_tensor(ln.rstd[:n, :], ln.veps[:n, :], sh.c("minus_half")[:n, 0:1],
                            ALU.pow).then_inc(ln.rstd_ready, 1)


def norm_memory(nc, ctx, prefix, sem):
    ln = Shared()
    ln.stats = ctx.enter_context(nc.sbuf_tensor(prefix + "stats", [128, 6], F32))
    ln.mv = ctx.enter_context(nc.sbuf_tensor(prefix + "mean_var", [128, 2], F32))
    ln.veps = ctx.enter_context(nc.sbuf_tensor(prefix + "var_eps", [128, 1], F32))
    ln.rstd = ctx.enter_context(nc.sbuf_tensor(prefix + "rstd", [128, 1], F32))
    ln.var_ready = sem("var_ready")
    ln.passed = sem("passed")
    ln.rstd_ready = sem("rstd_ready")
    return ln



def linear_attention(nc, sh):
    with ExitStack() as ctx:
        sb = lambda name, shape, dt=F32: ctx.enter_context(nc.sbuf_tensor("la_" + name, shape, dt))
        sem = sem_maker(nc, ctx, "la_")
        ps = sh.ps
        w = sb("wqkv", [128, 2, 3 * D])
        bias = sb("bias", [T, 2 * D])
        bv = sb("bv", [1, D])
        stats = sb("stats", [T, B, 6])
        mv = sb("mean_var", [T, B, 2])
        veps = sb("var_eps", [T, B])
        rstd = sb("rstd", [T, B])
        shift = sb("shift", [T, B])
        xn = sb("xn", [T, D])
        xnTs = sb("xnTs", [128, 2, T])
        qk = sb("qk", [T, 2 * D])
        mx = sb("mx", [T, 32])
        rs = sb("rs", [T, 32])
        rs_sc = sb("rs_sc", [T, 2, 16])
        k = sb("k", [T, D])
        ck = sb("ck", [T, D])
        q_sc = sb("q_sc", [T, 2, D])
        vsc = sb("vsc", [T, 2, 2, 129])
        kvm = sb("kvm", [128, 4, 2, 136])
        qT = sb("qT", [128, 2, 2, T])
        cqT = sb("cqT", [128, 2, 2, T])
        zr = sb("zr", [T, 2, 2, 8])
        t1 = sb("t1", [T, 2, 2, 128])
        at = sb("at", [T, D])
        P_QK, P_V, P_KV, P_O, P_Q, P_A = 0, 1, 2, 4, 6, 7
        x_stats, var_ready, rstd_ready, rows_ready = sem("x_stats"), sem("var_ready"), sem("rstd_ready"), sem("rows_ready")
        xn_ready, xnT_mm, xnT_ready = sem("xn_ready"), sem("xnT_mm"), sem("xnT_ready")
        qkv_mm, vsc_ready, shifted, exp_done = sem("qkv_mm"), sem("vsc_ready"), sem("shifted"), sem("exp_done")
        k_ready, ck_ready, q_ready = sem("k_ready"), sem("ck_ready"), sem("q_ready")
        k_mm, kvm_k_ready, ck_mm, kvm_ck_ready = sem("k_mm"), sem("kvm_k_ready"), sem("ck_mm"), sem("kvm_ck_ready")
        q_mm, qT_ready, cqT_ready = sem("q_mm"), sem("qT_ready"), sem("cqT_ready")
        out_mm, at_ready, aT_mm, aT_ready = sem("out_mm"), sem("at_ready"), sem("aT_mm"), sem("aT_ready")
        chain1, chain2, passed, loaded = sem("chain1"), sem("chain2"), sem("passed"), sem("loaded")
        sin_col, cos_col = sh.c("sincos")[:T, 0:1], sh.c("sincos")[:T, 1:2]
        factors_T = sh.c("sincosT").rearrange("p (s t) -> p s t", s=2)
        LINKS1, LINKS2 = 6, 3
        block = ctx.enter_context(nc.Block())

        def steps(eng, step):
            step(-3, False, False, False, True)
            step(-2, False, False, True, True)
            step(-1, False, True, True, True)
            with eng.Fori(0, B - 3) as i:
                step(i, True, True, True, True)
            step(B - 3, True, True, True, False)
            step(B - 2, True, True, False, False)
            step(B - 1, True, False, False, False)

        @block.sync
        def _(sp):
            sp.dma_start(sh.X[:, :, :], sh.ins["x"].rearrange("b t d -> t b d")).then_inc(sh.x_loaded, 16)
            sp.dma_start(sh.const[:, :], sh.consts_in[:, 0:N_CONST]).then_inc(sh.const_loaded, 16)
            for j, name in enumerate(("Wq", "Wk", "Wv")):
                sp.dma_start(w[:, :, j * D:(j + 1) * D],
                             sh.ins["L0_attn_" + name].rearrange("(c p) n -> p c n", p=128)).then_inc(loaded, 16)
            for j, name in enumerate(("bq", "bk")):
                sp.dma_start(bias[:, j * D:(j + 1) * D],
                             sh.ins["L0_attn_" + name].partition_broadcast(T)).then_inc(loaded, 16)
            sp.dma_start(bv[:, :], sh.ins["L0_attn_bv"].partition_broadcast(1)).then_inc(loaded, 16)
            for dst, src, name in sh.early_loads:
                sp.dma_start(dst, src).then_inc(sh.w_loaded[name], 16)

        @block.gpsimd
        def _(pool):
            pool.wait_ge(sh.const_loaded, 16)
            pool.wait_ge(var_ready, 1)
            nc.gpsimd.tensor_tensor(rstd[:, :], veps[:, :], sh.c("minus_half")[:T, 0:1].broadcast_to([T, B]),
                                    ALU.pow).then_inc(rstd_ready, 1)

            def step(i, result, keys, products, rows):
                if keys:
                    pool.wait_ge(qT_ready, i + 2)
                    nc.gpsimd.tensor_tensor(cqT[:, :, :, :], factors_T.unsqueeze(2).broadcast_to([128, 2, 2, T]),
                                            qT[:, :, :, :], ALU.subtract).then_inc(cqT_ready, 1)
                if products:
                    pool.wait_ge(k_ready, i + 3)
                    pool.sem_inc(passed, 1)
                    nc.gpsimd.tensor_scalar(ck[:, :], k[:, :], -1.0, 1.0, ALU.mult, ALU.add).then_inc(ck_ready, 1)

            steps(pool, step)

        @block.scalar
        def _(act):
            act.wait_ge(sh.const_loaded, 16)
            for c in range(2):
                nc.scalar.copy(vsc[:, c, :, 128], sh.c("sincos")[:T, :])
            act.wait_ge(sh.x_loaded, 16)
            act.wait_ge(rows_ready, 1)

            def step(i, result, keys, products, rows):
                if products:
                    act.wait_ge(xnT_mm, i + 3)
                    nc.scalar.copy(xnTs[:, :, :], ps[:, P_V, 256:256 + 2 * T].rearrange("p (c t) -> p c t", c=2)).then_inc(xnT_ready, 1)
                if rows:
                    act.sem_inc(passed, 1)
                    nc.scalar.activation(xn[:, :], sh.X[:, i + 3, :], ACT.Identity, bias=shift[:, i + 3:i + 4] if isinstance(i, int)
                                         else shift[:, bass.ds(i + 3, 1)], scale=rstd[:, i + 3:i + 4] if isinstance(i, int)
                                         else rstd[:, bass.ds(i + 3, 1)]).then_inc(xn_ready, 1)
                if keys:
                    act.wait_ge(q_mm, i + 2)
                    nc.scalar.copy(qT[:, :, :, :], ps[:, P_Q, 0:4 * T].rearrange("p (s c t) -> p s c t", s=2, c=2)).then_inc(qT_ready, 1)
                if products:
                    act.wait_ge(shifted, i + 3)
                    nc.scalar.activation(qk[:, :], qk[:, :], ACT.Exp).then_inc(exp_done, 1)
                    if keys:
                        act.wait_ge(ck_mm, i + 2)
                    vv = ps[:T, P_V, 0:D].rearrange("p (c n) -> p c n", c=2)
                    nc.scalar.mul(vsc[:, :, 0, 0:128], vv, sin_col)
                    nc.scalar.mul(vsc[:, :, 1, 0:128], vv, cos_col).then_inc(vsc_ready, 1)
                if result:
                    act.wait_ge(aT_mm, i + 1)
                    nc.scalar.copy(sh.attnT[:, :, i, :], ps[:, P_A, 0:2 * T].rearrange("p (c t) -> p c t", c=2)).then_inc(aT_ready, 1)

            steps(act, step)

        @block.vector
        def _(dve):
            dve.wait_ge(sh.x_loaded, 16)
            for b in range(B):
                nc.vector.bn_stats(stats[:, b, :], sh.X[:, b, :]).then_inc(x_stats, 1)
            for b in range(B):
                dve.wait_ge(x_stats, b + 1)
                nc.vector.bn_aggr(mv[:, b, :], stats[:, b, :]).then_inc(x_stats, 1)
            dve.wait_ge(x_stats, 2 * B)
            nc.vector.tensor_scalar(veps[:, :], mv[:, :, 1], LN_EPS, None, ALU.add).then_inc(var_ready, 1)
            dve.wait_ge(rstd_ready, 1)
            nc.vector.scalar_tensor_tensor(shift[:, :], mv[:, :, 0], -1.0, rstd[:, :], ALU.mult, ALU.mult).then_inc(rows_ready, 1)
            dve.wait_ge(sh.const_loaded, 16)
            dve.wait_ge(loaded, 96)

            def masked(r):
                for c in range(2):
                    nc.vector.tensor_tensor(kvm[:, 2 * r + c, :, 0:128],
                                            ps[:, P_KV + c, 0:258].rearrange("p (s n) -> p s n", s=2)[:, :, 0:128],
                                            mid(sh.c("block16"), 2), ALU.mult)
                sums = ps[:, P_KV:P_KV + 2, 0:258].rearrange("p c (s n) -> p c s n", s=2)[:, :, :, 128]
                return nc.vector.tensor_tensor(kvm[:, 2 * r:2 * r + 2, :, 128:136], bc(sums, 8),
                                               sh.c("head16").unsqueeze(1).unsqueeze(1).broadcast_to([128, 2, 2, 8]), ALU.mult)

            def step(i, result, keys, products, rows):
                if result:
                    link = chained(dve, chain2, i * LINKS2)
                    dve.wait_ge(out_mm, i + 1)
                    o = ps[:T, P_O:P_O + 2, 0:272].rearrange("p r (c n) -> p r c n", c=2)
                    link(nc.vector.tensor_scalar(zr[:, :, :, :], o[:, :, :, 128:136], 1e-6, None, ALU.max))
                    link(nc.vector.reciprocal(zr[:, :, :, :], zr[:, :, :, :]))
                    for r in range(2):
                        last = nc.vector.tensor_tensor(t1[:, r, :, :].rearrange("p c (h d) -> p c h d", d=DA),
                                                       o[:, r, :, 0:128].rearrange("p c (h d) -> p c h d", d=DA),
                                                       bc(zr[:, r, :, :], DA), ALU.mult)
                    assert link(last) == LINKS2
                    nc.vector.tensor_tensor(at[:, :].rearrange("p (c n) -> p c n", c=2),
                                            t1[:, 0, :, :], t1[:, 1, :, :], ALU.add).then_inc(at_ready, 1)
                if keys:
                    dve.wait_ge(k_mm, i + 2)
                    masked(0).then_inc(kvm_k_ready, 1)
                if products:
                    link = chained(dve, chain1, (i + 2) * LINKS1)
                    dve.wait_ge(qkv_mm, i + 3)
                    link(nc.vector.tensor_tensor(qk[:, :], ps[:T, P_QK, :], bias[:, :], ALU.add))
                    q3 = qk[:, :].rearrange("p (g d) -> p g d", d=DA)
                    link(nc.vector.tensor_reduce(mx[:, :], q3, AX.X, ALU.max))
                    nc.vector.tensor_tensor(q3, q3, bc(mx[:, :], DA), ALU.subtract).then_inc(shifted, 1)
                if keys:
                    dve.wait_ge(ck_mm, i + 2)
                    masked(1).then_inc(kvm_ck_ready, 1)
                if products:
                    dve.wait_ge(exp_done, i + 3)
                    link(nc.vector.tensor_reduce(rs[:, :], q3, AX.X, ALU.add))
                    link(nc.vector.reciprocal(rs[:, :], rs[:, :]))
                    nc.vector.tensor_scalar(rs_sc[:, 0, :], rs[:, 0:16], sin_col, None, ALU.mult)
                    link(nc.vector.tensor_scalar(rs_sc[:, 1, :], rs[:, 0:16], cos_col, None, ALU.mult))
                    nc.vector.tensor_tensor(k[:, :].rearrange("p (g d) -> p g d", d=DA), q3[:, 16:32, :],
                                            bc(rs[:, 16:32], DA), ALU.mult).then_inc(k_ready, 1)
                    n = link(nc.vector.tensor_tensor(q_sc[:, :, :].rearrange("p s (g d) -> p s g d", d=DA),
                                                     q3[:, 0:16, :].unsqueeze(1).broadcast_to([T, 2, 16, DA]),
                                                     bc(rs_sc[:, :, :], DA), ALU.mult))
                    nc.vector.sem_inc(q_ready, 1)
                    assert n == LINKS1

            steps(dve, step)

        @block.tensor
        def _(pe):
            pe.wait_ge(sh.const_loaded, 16)
            pe.wait_ge(loaded, 96)
            ident = sh.c("ident")

            def key_products(rows):
                for c in range(2):
                    last = nc.tensor.matmul(ps[:, P_KV + c, 0:258], rows[:, c * 128:(c + 1) * 128],
                                            vsc[:, c, :, :].rearrange("p s n -> p (s n)"), start=True, stop=True)
                return last

            def step(i, result, keys, products, rows):
                if result:
                    for r, q in enumerate((qT, cqT)):
                        pe.wait_ge((kvm_k_ready, kvm_ck_ready)[r], i + 1)
                        pe.wait_ge((qT_ready, cqT_ready)[r], i + 1)
                        for c in range(2):
                            for s in range(2):
                                last = nc.tensor.matmul(ps[:T, P_O + r, c * 136:(c + 1) * 136], q[:, s, c, :],
                                                        kvm[:, 2 * r + c, s, :], start=(s == 0), stop=(s == 1))
                    last.then_inc(out_mm, 1)
                if products:
                    pe.wait_ge(xn_ready, i + 3)
                    if keys:
                        pe.wait_ge(vsc_ready, i + 2)
                    for c in range(2):
                        last = nc.tensor.transpose(ps[:, P_V, 256 + c * T:256 + (c + 1) * T], xn[:, c * 128:(c + 1) * 128],
                                                   ident[:T, :T])
                    last.then_inc(xnT_mm, 1)
                if keys:
                    pe.wait_ge(k_ready, i + 2)
                    pe.wait_ge(vsc_ready, i + 2)
                    key_products(k).then_inc(k_mm, 1)
                    pe.wait_ge(q_ready, i + 2)
                    for s in range(2):
                        for c in range(2):
                            at_col = (2 * s + c) * T
                            last = nc.tensor.transpose(ps[:, P_Q, at_col:at_col + T], q_sc[:, s, c * 128:(c + 1) * 128], ident[:T, :T])
                    last.then_inc(q_mm, 1)
                if products:
                    pe.wait_ge(xnT_ready, i + 3)
                    for c in range(2):
                        nc.tensor.matmul(ps[:T, P_QK, :], xnTs[:, c, :], w[:, c, 0:2 * D], start=(c == 0), stop=(c == 1))
                    nc.tensor.matmul(ps[:T, P_V, 0:D], sh.c("ones")[0:1, :T], bv[:, :], start=True, stop=False)
                    for c in range(2):
                        last = nc.tensor.matmul(ps[:T, P_V, 0:D], xnTs[:, c, :], w[:, c, 2 * D:3 * D], start=False, stop=(c == 1))
                    last.then_inc(qkv_mm, 1)
                if keys:
                    pe.wait_ge(ck_ready, i + 2)
                    pe.wait_ge(kvm_k_ready, i + 2)
                    key_products(ck).then_inc(ck_mm, 1)
                if result:
                    pe.wait_ge(at_ready, i + 1)
                    if not products:
                        pe.wait_ge(aT_ready, i)
                    for c in range(2):
                        last = nc.tensor.transpose(ps[:, P_A, c * T:(c + 1) * T], at[:, c * 128:(c + 1) * 128], ident[:T, :T])
                    last.then_inc(aT_mm, 1)

            steps(pe, step)



def add_and_norm(nc, sh, tag, gather, weight=None, bias=None):
    PAIRS = B // 2
    with ExitStack() as ctx:
        sb = lambda name, shape, dt=F32: ctx.enter_context(nc.sbuf_tensor(tag + name, shape, dt))
        sem = sem_maker(nc, ctx, tag)
        ps = sh.ps
        own = sb("own", [128, 2, 2, 2 * T])
        xn = sb("xn", [T, 2, 2, D])
        stats, mv = sb("stats", [T, 2, 6]), sb("mean_var", [T, 2, 2])
        veps, minus_mean = sb("var_eps", [T, 2, 2]), sb("minus_mean", [T, 2, 2])
        rstd, shift = sb("rstd", [T, 2, 2]), sb("shift", [T, 2, 2])
        own_ready, y_mm, added, var_ready, shift_ready = (
            sem("own_ready"), sem("y_mm"), sem("added"), sem("var_ready"), sem("shift_ready"))
        xn_ready, xnT_mm, xnT_ready = sem("xn_ready"), sem("xnT_mm"), sem("xnT_ready")
        chain, rstd_done, passed, passed2 = sem("chain"), sem("rstd_done"), sem("passed"), sem("passed2")
        LINKS = 3 + (bias is not None)
        P_Y, P_XT = 0, 2
        block = ctx.enter_context(nc.Block())

        def steps(eng, step):
            for u in range(2):
                step(u, u, False, True)
            with eng.Fori(1, PAIRS // 2 - 1) as g:
                for u in range(2):
                    step(2 * g + u, u, True, True)
            for u in range(2):
                step(PAIRS - 2 + u, u, True, False)

        @block.gpsimd
        def _(pool):
            def step(p, u, later, more):
                pool.wait_ge(var_ready, p + 1)
                if later:
                    pool.wait_ge(xn_ready, p - 1)
                nc.gpsimd.tensor_tensor(rstd[:, u, :], veps[:, u, :], sh.c("minus_half")[:T, 0:2], ALU.pow).then_inc(rstd_done, 1)
                pool.wait_ge(rstd_done, p + 1)
                nc.gpsimd.tensor_tensor(shift[:, u, :], minus_mean[:, u, :], rstd[:, u, :], ALU.mult).then_inc(shift_ready, 1)

            steps(pool, step)

        @block.scalar
        def _(act):
            def copy_in(p, u):
                src = gather(p)
                dst = own[:, u, :, :].rearrange("p c (a b) -> p c a b", b=src.shape[3])
                nc.scalar.copy(dst, src).then_inc(own_ready, 1)

            def copy_out(p, u):
                act.wait_ge(xnT_mm, p + 1)
                nc.scalar.copy(sh.xnT[:, :, bass.ds(2 * p, 2), :].rearrange("p c j t -> p j c t"),
                               ps[:, P_XT + u, 0:4 * T].rearrange("p (j c t) -> p j c t", j=2, c=2)).then_inc(xnT_ready, 1)

            def step(p, u, later, more):
                if more:
                    act.wait_ge(y_mm, p + 1)
                    copy_in(p + 2, u)
                act.wait_ge(shift_ready, p + 1)
                act.sem_inc(passed, 1)
                for j in range(2):
                    last = nc.scalar.activation(xn[:, u, j, :], sh.X[:, 2 * p + j, :], ACT.Identity,
                                                bias=shift[:, u, j:j + 1], scale=rstd[:, u, j:j + 1])
                last.then_inc(xn_ready, 1)
                if later or u:
                    copy_out(p - 1, 1 - u)

            copy_in(0, 0)
            copy_in(1, 1)
            steps(act, step)
            copy_out(PAIRS - 1, 1)

        @block.vector
        def _(dve):
            def step(p, u, later, more):
                link = chained(dve, chain, p * LINKS)
                x = sh.X[:, bass.ds(2 * p, 2), :]
                dve.wait_ge(y_mm, p + 1)
                link(nc.vector.tensor_tensor(x, x, ps[:T, P_Y + u, :].rearrange("p (j d) -> p j d", j=2), ALU.add))
                nc.vector.sem_inc(added, 1)
                if bias is not None:
                    link(nc.vector.tensor_tensor(x, x, mid(bias, 2), ALU.add))
                dve.sem_inc(passed2, 1)
                nc.vector.bn_stats(stats[:, 0, :], sh.X[:, 2 * p, :])
                link(nc.vector.bn_stats(stats[:, 1, :], sh.X[:, 2 * p + 1, :]), passed2)
                nc.vector.bn_aggr(mv[:, 0, :], stats[:, 0, :])
                n = link(nc.vector.bn_aggr(mv[:, 1, :], stats[:, 1, :]), passed2)
                assert n == LINKS
                if later:
                    dve.wait_ge(shift_ready, p - 1)
                nc.vector.tensor_scalar(minus_mean[:, u, :], mv[:, :, 0], -1.0, None, ALU.mult)
                nc.vector.tensor_scalar(veps[:, u, :], mv[:, :, 1], LN_EPS, None, ALU.add).then_inc(var_ready, 1)

            steps(dve, step)

        @block.tensor
        def _(pe):
            ident = sh.c("ident")

            def product(p, u):
                pe.wait_ge(own_ready, p + 1)
                for j in range(2):
                    for c in range(2):
                        rows = own[:, u, c, j * T:(j + 1) * T]
                        if weight is None:
                            last = nc.tensor.transpose(ps[:T, P_Y + u, j * D + c * 128:j * D + (c + 1) * 128], rows, ident)
                        else:
                            last = nc.tensor.matmul(ps[:T, P_Y + u, j * D:(j + 1) * D], rows, weight[:, c, :],
                                                    start=(c == 0), stop=(c == 1))
                last.then_inc(y_mm, 1)

            def step(p, u, later, more):
                if more:
                    pe.wait_ge(added, p + 1)
                    product(p + 2, u)
                pe.wait_ge(xn_ready, p + 1)
                if later:
                    pe.wait_ge(xnT_ready, p - 1)
                for j in range(2):
                    for c in range(2):
                        at_col = (2 * j + c) * T
                        last = nc.tensor.transpose(ps[:, P_XT + u, at_col:at_col + T], xn[:, u, j, c * 128:(c + 1) * 128],
                                                   ident[:T, :T])
                last.then_inc(xnT_mm, 1)

            product(0, 0)
            product(1, 1)
            steps(pe, step)


def bias_columns(nc, sh):
    with ExitStack() as ctx:
        sem = sem_maker(nc, ctx, "bc_")
        rows = [ctx.enter_context(nc.sbuf_tensor(f"bc_rows{n}", [128, 128], F32)) for n in range(2)]
        rows_loaded, cols_mm = sem("rows_loaded"), sem("cols_mm")
        made = sem("made")
        block = ctx.enter_context(nc.Block())
        ident = sh.c("ident")
        small = [("L1_ffn_b_c_proj", 16), ("L1_xattn_g1", 2), ("L1_xattn_b1", 2), ("L1_xattn_g2", 2),
                 ("L1_xattn_b2", 2), ("L0_xattn_b_Q", 2), ("L0_xattn_b_K", 2), ("L0_xattn_b_V", 2)]

        @block.sync
        def _(sp):
            for n, name in enumerate(("L1_ffn_b_c_fc", "L1_ffn_b_gate")):
                sp.dma_start(rows[0][64 * n:64 * n + 64, :],
                             sh.ins[name].rearrange("e o (j p) -> (e o j) p", p=128)).then_inc(rows_loaded, 16)
            at = 0
            for name, n in small:
                src = sh.ins[name]
                src = src.rearrange("e o (j p) -> (e o j) p", p=128) if n == 16 else src.rearrange("(j p) -> j p", p=128)
                sp.dma_start(rows[1][at:at + n, :], src).then_inc(rows_loaded, 16)
                at += n

        @block.tensor
        def _(pe):
            pe.wait_ge(rows_loaded, 16 * (2 + len(small)))
            nc.tensor.transpose(sh.ps[:, 0, 0:128], rows[0][:, :], ident)
            nc.tensor.transpose(sh.ps[:, 0, 128:158], rows[1][:30, :], ident[:30, :30]).then_inc(cols_mm, 1)

        @block.vector
        def _(dve):
            dve.wait_ge(cols_mm, 1)
            nc.vector.tensor_copy(sh.columns[:, 0:158], sh.ps[:, 0, 0:158]).then_inc(made, 1)
            dve.wait_ge(made, 1)
            nc.vector.tensor_scalar(sh.columns[:, 158:160], sh.columns[:, 152:154], 0.25, None, ALU.mult)



class Plan:

    def __init__(self, n_prep, n_fin, fin_at, n_slots):
        self.n_prep, self.n_fin = n_prep, n_fin
        full = [("prep", k) for k in range(n_prep)]
        for k, at in enumerate(fin_at):
            full.insert(at, ("fin", k))
        assert full[-1][0] == "prep"
        self.full, self.n_slots = full, n_slots
        self.only_prep = [s for s in full if s[0] == "prep"]
        self.only_fin = [s for s in full if s[0] == "fin"]

    def base(self, b):
        return self.n_prep - self.n_fin + b * (self.n_prep + self.n_fin)

    def prep_end(self, b):
        return self.n_prep if isinstance(b, int) and b == 0 else self.n_prep * 2 + (b - 1) * (self.n_prep + self.n_fin)

    def slots(self, steps):
        n = self.n_slots
        cut = [round(s * len(steps) / n) for s in range(n + 1)]
        return [[(p, *steps[p]) for p in range(cut[s], cut[s + 1])] for s in range(n)]


def attention(nc, sh, cfg):
    with ExitStack() as ctx:
        tag = cfg.tag
        sb = lambda name, shape, dt=F32: ctx.enter_context(nc.sbuf_tensor(tag + name, shape, dt))
        sem = sem_maker(nc, ctx, tag)
        ps = sh.ps
        H, dh, HS, KT, NC = cfg.heads, cfg.dh, cfg.per_stage, cfg.keys, cfg.key_chunks
        KCH = KT // NC
        NS = H // HS
        HD = H * dh
        NF = cfg.out_chunks
        ln = norm_memory(nc, ctx, tag, sem)
        v = sb("v", [KCH, 2, NC, NF, (128 // dh) * (128 + dh)])
        cfg.v_at = lambda par, k: v[:, par, k, :, :].rearrange("p c (j x) -> p c j x", x=128 + dh)[:, :, :, 0:dh]
        cfg.allocate(ctx, sb, sem)
        cleared = sem("cleared")
        probs = sb("probs", [T, 2, HS, KT])
        pT = sb("pT", [KCH, 2, HS * NC * T])
        negmax = sb("negmax", [T, 2, H])
        sums = sb("sums", [T, 2, H])
        inv = sb("inv", [T, H])
        inv_wide = sb("inv_wide", [T, H, dh])
        invT = sb("invT", [128, NF, T])
        oT = sb("oT", [128, NF, T])
        y = sb("y", [T, D])
        xn = sb("xn", [T, D])
        scores_mm, max_done, exp_done = sem("scores_mm"), sem("max_done"), sem("exp_done")
        pT_mm, pT_ready, o_mm, o_ready, inv_ready = (
            sem("pT_mm"), sem("pT_ready"), sem("o_mm"), sem("o_ready"), sem("inv_ready"))
        side_mm, side_done, xn_ready = sem("side_mm"), sem("side_done"), sem("xn_ready")
        chain_i, chain_o, chain_x = sem("chain_i"), sem("chain_o"), sem("chain_x")
        cfg.sem_side_done = side_done
        n_prep = len(cfg.prep_mm)
        n_fin = cfg.n_oT_steps + 2
        plan = Plan(n_prep, n_fin, cfg.fin_at, NS + 2)
        BANK_S, BANK_PT, BANK_O, BANK_SIDE, N_SIDE = cfg.banks
        s_banks = cfg.score_banks
        n_ptb = cfg.pt_buffers
        YSTEP = cfg.n_oT_steps
        block = ctx.enter_context(nc.Block())

        def scores_bank(par, x):
            if s_banks == 1:
                return ps[:T, BANK_S + par, x * KT:(x + 1) * KT]
            return ps[:T, BANK_S + par * s_banks + x, 0:KT]

        def scores_all(par):
            if s_banks == 1:
                return ps[:T, BANK_S + par, 0:HS * KT].rearrange("p (h k) -> p h k", h=HS)
            return ps[:T, BANK_S + par * s_banks:BANK_S + (par + 1) * s_banks, 0:KT]

        per_bank = HS if s_banks == 1 else 1
        pt_banks = HS // per_bank

        def pT_psum(par, x, k):
            bank = BANK_PT + (par % n_ptb) * pt_banks + x // per_bank
            col = (x % per_bank * NC + k) * T
            return ps[:KCH, bank, col:col + T]

        def pT_psum_all(par):
            bank = BANK_PT + (par % n_ptb) * pt_banks
            return ps[:KCH, bank:bank + pt_banks, 0:per_bank * NC * T]

        hpc = 128 // dh
        c_per_bank = NF if NF * T <= 512 else 4

        @block.sync
        def _(sp):
            cfg.sync(sp, plan)

        @block.gpsimd
        def _(pool):
            for u in range(2):
                nc.gpsimd.memset(v[:, u, :, :, :], 0.0).then_inc(cleared, 1)
            if dh == 64:
                nc.gpsimd.memset(cfg.qT[:, :, :, :, :], 0.0).then_inc(cleared, 1)
            cfg.pool(pool, plan, ln)

        @block.scalar
        def _(act):
            def side(p, kind, k, base, b, par):
                act.wait_ge(side_mm, base + p + 1)
                bank = BANK_SIDE + p % N_SIDE
                if kind == "prep":
                    last = cfg.prep_act(k, ps[:, bank, :], b + 1, par)
                elif k < cfg.n_oT_steps:
                    n = NF // cfg.n_oT_steps
                    last = nc.scalar.copy(invT[:, k * n:(k + 1) * n, :], ps[:, bank, 0:n * T].rearrange("p (c t) -> p c t", c=n))
                elif k == YSTEP:
                    last = nc.scalar.copy(y[:, :], ps[:T, bank, 0:D])
                else:
                    last = cfg.xnT_act(b - 1, ps[:, bank, 0:2 * T].rearrange("p (c t) -> p c t", c=2))
                last.then_inc(side_done, 1)

            def exps(b, par, i):
                act.wait_ge(max_done, b * NS + i + 1)
                for x, h in enumerate(cfg.stage_heads(i)):
                    last = nc.scalar.activation(probs[:, i % 2, x, :], scores_bank(i % 2, x), ACT.Exp,
                                                bias=negmax[:, par, h:h + 1], scale=cfg.scale,
                                                accum_out=sums[:, par, h:h + 1])
                last.then_inc(exp_done, 1)

            def iteration(b, par, steps, base):
                for s, todo in enumerate(plan.slots(steps)):
                    for p, kind, k in todo:
                        side(p, kind, k, base, b, 1 - par)
                    if s < NS:
                        exps(b, par, s)

            cfg.wait_weights(act)
            act.wait_ge(cleared, 2 + (dh == 64))
            for p, (kind, k) in enumerate(plan.only_prep):
                side(p, kind, k, 0, -1, 0)
            iteration(0, 0, plan.only_prep, plan.n_prep)
            with act.Fori(1, B - 2, 2) as b:
                iteration(b, 1, plan.full, plan.base(b))
                iteration(b + 1, 0, plan.full, plan.base(b + 1))
            iteration(B - 1, 1, plan.only_fin, plan.base(B - 1))
            for p, (kind, k) in enumerate(plan.only_fin):
                side(p, kind, k, plan.base(B - 1) + plan.n_fin, B, None)

        @block.vector
        def _(dve):
            LINKS_X = 3 + (cfg.out_bias is not None) + 3 * cfg.twice

            def residual(b, base, p):
                link = chained(dve, chain_x, b * LINKS_X)
                dve.wait_ge(side_done, base + p + 1)
                n = link(nc.vector.tensor_tensor(sh.X[:, b, :], sh.X[:, b, :], y[:, :], ALU.add))
                if cfg.out_bias is not None:
                    n = link(nc.vector.tensor_tensor(sh.X[:, b, :], sh.X[:, b, :], cfg.out_bias, ALU.add))
                if cfg.twice:
                    link(norm_rows(nc, sh, dve, link, ln, sh.X[:, b, :], xn[:, :], nth=b * 2 + 1))
                    norm_rows(nc, sh, dve, link, ln, xn[:, :], xn[:, :], nth=b * 2 + 2).then_inc(xn_ready, 1)
                else:
                    norm_rows(nc, sh, dve, link, ln, sh.X[:, b, :], xn[:, :], nth=b + 1).then_inc(xn_ready, 1)
                    if cfg.keep_rows:
                        nc.vector.tensor_scalar(sh.XN[:, b, :], sh.X[:, b, :], ln.mv[:T, 0:1], ln.rstd[:T, :],
                                                ALU.subtract, ALU.mult)

            def inverse_sums(b, par):
                dve.wait_ge(exp_done, b * NS + NS)
                nc.vector.reciprocal(inv[:, :], sums[:, par, :]).then_inc(chain_i, 1)
                dve.wait_ge(chain_i, b + 1)
                nc.vector.tensor_copy(inv_wide[:, :, :], bc(inv[:, :], dh)).then_inc(inv_ready, 1)

            def scale_heads(b, base, p):
                dve.wait_ge(side_done, base + p + 1)
                dve.wait_ge(o_mm, b + 1)
                for n in range(NF // c_per_bank):
                    cs = slice(n * c_per_bank, (n + 1) * c_per_bank)
                    last = nc.vector.tensor_tensor(oT[:, cs, :], invT[:, cs, :],
                                                   ps[:, BANK_O + n, 0:c_per_bank * T].rearrange("p (c t) -> p c t", t=T), ALU.mult)
                if cfg.v_bias is not None:
                    last.then_inc(chain_o, 1)
                    dve.wait_ge(chain_o, b + 1)
                    for c in range(NF):
                        last = nc.vector.tensor_scalar(oT[:, c, :], oT[:, c, :], cfg.v_bias[:, c:c + 1], None, ALU.add)
                last.then_inc(o_ready, 1)

            def iteration(b, par, steps, base):
                slots = plan.slots(steps)
                due = None
                for s in range(NS + 2):
                    for p, kind, k in slots[s]:
                        if (kind, k) == ("fin", YSTEP - 1):
                            scale_heads(b - 1, base, p)
                    if s < NS:
                        dve.wait_ge(scores_mm, b * NS + s + 1)
                        nc.vector.tensor_reduce(negmax[:, par, cfg.stage_columns(s)], scores_all(s % 2),
                                                AX.X, ALU.max, negate=True).then_inc(max_done, 1)
                    if 1 <= s <= NS:
                        dve.wait_ge(pT_mm, b * NS + s)
                        nc.vector.tensor_copy(pT[:, (s - 1) % 2, :].rearrange("p (n k) -> p n k", n=pt_banks),
                                              pT_psum_all((s - 1) % 2)).then_inc(pT_ready, 1)
                    if due is not None:
                        residual(b - 1, base, due)
                        due = None
                    for p, kind, k in slots[s]:
                        if (kind, k) == ("fin", YSTEP):
                            due = p
                    if cfg.dve_slot:
                        cfg.dve_slot(dve, s, b, 1 - par, ln, steps is not plan.only_fin)
                if due is not None:
                    residual(b - 1, base, due)
                inverse_sums(b, par)

            cfg.wait_weights(dve)
            if cfg.dve_before:
                cfg.dve_before(dve, ln)
            iteration(0, 0, plan.only_prep, plan.n_prep)
            with dve.Fori(1, B - 2, 2) as b:
                iteration(b, 1, plan.full, plan.base(b))
                iteration(b + 1, 0, plan.full, plan.base(b + 1))
            iteration(B - 1, 1, plan.only_fin, plan.base(B - 1))
            scale_heads(B - 1, plan.base(B - 1) + plan.n_fin, YSTEP - 1)
            residual(B - 1, plan.base(B - 1) + plan.n_fin, YSTEP)

        @block.tensor
        def _(pe):
            ident = sh.c("ident")

            def side(p, kind, k, base, b, par):
                if p < N_SIDE:
                    if not (isinstance(base, int) and base == 0):
                        pe.wait_ge(side_done, base)
                else:
                    pe.wait_ge(side_done, base + p - N_SIDE + 1)
                bank = BANK_SIDE + p % N_SIDE
                if kind == "prep":
                    last = cfg.prep_mm[k](pe, k, ps[:, bank, :], b + 1, base + p, par)
                elif k < cfg.n_oT_steps:
                    pe.wait_ge(inv_ready, b)
                    n = NF // cfg.n_oT_steps
                    for c in range(n):
                        f = k * n + c
                        last = nc.tensor.transpose(ps[:, bank, c * T:(c + 1) * T], inv_wide[:, f * hpc:(f + 1) * hpc, :].rearrange("p h d -> p (h d)"), ident[:T, :T])
                elif k == YSTEP:
                    pe.wait_ge(o_ready, b)
                    for c in range(NF):
                        last = nc.tensor.matmul(ps[:T, bank, 0:D], oT[:, c, :], cfg.w_out[:, c, :],
                                                start=(c == 0), stop=(c == NF - 1))
                else:
                    pe.wait_ge(xn_ready, b)
                    for c in range(2):
                        last = nc.tensor.transpose(ps[:, bank, c * T:(c + 1) * T], xn[:, c * 128:(c + 1) * 128], ident[:T, :T])
                last.then_inc(side_mm, 1)

            steps_at = {}

            def order(steps):
                steps_at.clear()
                steps_at.update({s: p for p, s in enumerate(steps)})

            cfg.steps_at = steps_at

            def stage_scores(b, par, i):
                for x, h in enumerate(cfg.stage_heads(i)):
                    q, kk = cfg.head_operands(par, h)
                    last = nc.tensor.matmul(scores_bank(i % 2, x), q, kk, start=True, stop=True)
                last.then_inc(scores_mm, 1)

            def stage_transposes(b, i):
                pe.wait_ge(exp_done, b * NS + i + 1)
                if not (isinstance(b, int) and b == 0 and i < n_ptb):
                    pe.wait_ge(pT_ready, b * NS + i + 1 - n_ptb)
                for x in range(HS):
                    for k in range(NC):
                        last = nc.tensor.transpose(pT_psum(i, x, k), probs[:, i % 2, x, k * KCH:(k + 1) * KCH], ident[:T, :T])
                last.then_inc(pT_mm, 1)

            def stage_values(b, par, i):
                pe.wait_ge(pT_ready, b * NS + i + 1)
                if i == 0 and not (isinstance(b, int) and b == 0):
                    pe.wait_ge(o_ready, b)
                for x, h in enumerate(cfg.stage_heads(i)):
                    c, j = h // hpc, h % hpc
                    bank, col = BANK_O + c // c_per_bank, c % c_per_bank * T
                    for k in range(NC):
                        at = (x * NC + k) * T
                        last = nc.tensor.matmul(ps[:, bank, col:col + T], v[:, par, k, c, j * 128:(j + 1) * 128], pT[:, i % 2, at:at + T],
                                                start=(j == 0 and k == 0), stop=(j == hpc - 1 and k == NC - 1))
                if i == NS - 1:
                    last.then_inc(o_mm, 1)

            def iteration(b, par, steps, base):
                order(steps)
                pe.wait_ge(side_done, plan.prep_end(b))
                if dh == 16:
                    pe.wait_ge(cfg.q_ready, b + 1)
                for s, todo in enumerate(plan.slots(steps)):
                    if s < NS:
                        stage_scores(b, par, s)
                    for p, kind, k in todo:
                        side(p, kind, k, base, b, 1 - par)
                    if 1 <= s <= NS:
                        stage_transposes(b, s - 1)
                    if s >= 2:
                        stage_values(b, par, s - 2)

            cfg.wait_weights(pe)
            order(plan.only_prep)
            for p, (kind, k) in enumerate(plan.only_prep):
                side(p, kind, k, 0, -1, 0)
            iteration(0, 0, plan.only_prep, plan.n_prep)
            with pe.Fori(1, B - 2, 2) as b:
                iteration(b, 1, plan.full, plan.base(b))
                iteration(b + 1, 0, plan.full, plan.base(b + 1))
            iteration(B - 1, 1, plan.only_fin, plan.base(B - 1))
            for p, (kind, k) in enumerate(plan.only_fin):
                side(p, kind, k, plan.base(B - 1) + plan.n_fin, B, None)


def load_context(nc, sh, cfg, sp, plan):
    src = sh.ins["ctx_1024"].rearrange("b (j p) d -> b p j d", p=KC)

    def load(b, u):
        sp.dma_start(cfg.ctx_in[:, u, :, :], src[b]).then_inc(cfg.ctx_loaded[u], 16)

    load(0, 0)
    load(1, 1)
    sp.wait_ge(cfg.sem_side_done, cfg.ctx_last_use + 1)
    load(2, 0)
    sp.wait_ge(cfg.sem_side_done, plan.n_prep + cfg.ctx_last_use + 1)
    load(3, 1)
    at = plan.full.index(("prep", cfg.ctx_last_use))
    with sp.Fori(4, B - 1, 2) as b:
        for u in range(2):
            sp.wait_ge(cfg.sem_side_done, plan.base(b + u - 3) + at + 1)
            load(b + u, u)



def context_attention_0(nc, sh, w):
    cfg = Shared()
    cfg.tag, cfg.heads, cfg.dh, cfg.per_stage, cfg.keys, cfg.key_chunks = "c0_", 16, 16, 2, S, NK
    cfg.out_chunks, cfg.n_oT_steps = 2, 1
    cfg.banks, cfg.score_banks, cfg.pt_buffers = (0, 4, 6, 7, 1), 2, 1
    cfg.scale = 1.0
    cfg.fin_at = [0, 4, 8]
    cfg.twice = cfg.keep_rows = False
    cfg.out_bias, cfg.v_bias, cfg.w_out = w.bo[:, :], w.bv, w.wo
    cfg.dve_slot = None
    cfg.dve_before = None
    cfg.norm_nth = None
    ident = sh.c("ident")

    cfg.stage_heads = lambda i: [2 * i, 2 * i + 1]
    cfg.stage_columns = lambda i: slice(2 * i, 2 * i + 2)

    def allocate(ctx, sb, sem):
        cfg.ctx_in = sb("ctx_in", [KC, 2, NK, D])
        cfg.ctxT = sb("ctxT", [128, 2, S])
        cfg.kT = sb("kT", [128, 2, 2, S])
        cfg.q_all = sb("q_all", [128, 2, T])
        cfg.qT = sb("qT", [128, 2, 2, 8, T])
        cfg.q_ready = sem("q_ready")
        cfg.ctx_loaded = [sem(f"ctx_loaded{u}") for u in range(2)]

    cfg.allocate = allocate

    def head_operands(par, h):
        return cfg.qT[:, par, h // 8, h % 8, :], cfg.kT[:, par, h // 8, :]

    cfg.head_operands = head_operands

    def wait_weights(eng):
        eng.wait_ge(sh.w_loaded["c0"], w.n_loads * 16)

    cfg.wait_weights = wait_weights

    def transposes(pe, k, bank, b, at, par):
        if k == 1:
            pe.wait_ge(cfg.ctx_loaded[par], b * 8 + 16 - 8 * par)
        for j in range(NK):
            last = nc.tensor.transpose(bank[:, j * KC:(j + 1) * KC], cfg.ctx_in[:, par, j, (k - 1) * 128:k * 128], ident[:KC, :KC])
        return last

    def keys(pe, k, bank, b, at, par):
        m = k - 3
        if m == 0:
            pe.wait_ge(cfg.sem_side_done, at)
        for c in range(2):
            last = nc.tensor.matmul(bank[:, 0:S], w.wk[:, c, m * 128:(m + 1) * 128], cfg.ctxT[:, c, :], start=(c == 0), stop=(c == 1))
        return last

    def values(pe, k, bank, b, at, par):
        for j in ((0, 1) if k == 5 else (2,)):
            for c in range(2):
                last = nc.tensor.matmul(bank[:KC, j % 2 * D:(j % 2 + 1) * D], cfg.ctxT[:, c, j * KC:(j + 1) * KC],
                                        w.wv[:, c, :], start=(c == 0), stop=(c == 1))
        return last

    def queries(pe, k, bank, b, at, par):
        for m in range(2):
            for c in range(2):
                last = nc.tensor.matmul(bank[:, m * T:(m + 1) * T], w.wq[:, c, m * 128:(m + 1) * 128], sh.xnT[:, c, b, :],
                                        start=(c == 0), stop=(c == 1))
        return last

    cfg.prep_mm = [queries, transposes, transposes, keys, keys, values, values]
    cfg.ctx_last_use = 2

    def prep_act(k, bank, b, par):
        if k == 0:
            for m in range(2):
                last = nc.scalar.activation(cfg.q_all[:, m, :], bank[:, m * T:(m + 1) * T], ACT.Identity,
                                            bias=w.bq_scaled[:, m:m + 1], scale=0.25)
            return last
        if k < 3:
            return nc.scalar.copy(cfg.ctxT[:, k - 1, :], bank[:, 0:S])
        if k < 5:
            return nc.scalar.activation(cfg.kT[:, par, k - 3, :], bank[:, 0:S], ACT.Identity, bias=w.bk[:, k - 3:k - 2])
        if k == 5:
            for j in range(2):
                last = nc.scalar.copy(cfg.v_at(par, j), bank[:KC, j * D:(j + 1) * D].rearrange("p (c j d) -> p c j d", c=2, d=16))
            return last
        return nc.scalar.copy(cfg.v_at(par, 2), bank[:KC, 0:D].rearrange("p (c j d) -> p c j d", c=2, d=16))

    cfg.prep_act = prep_act
    cfg.xnT_act = lambda b, src: nc.scalar.copy(sh.xnT[:, :, b, :], src)

    cfg.sync = lambda sp, plan: load_context(nc, sh, cfg, sp, plan)

    def pool(eng, plan, ln):
        at = plan.full.index(("prep", 0))

        def masked_queries(par, side_steps):
            eng.wait_ge(cfg.sem_side_done, side_steps)
            for m in range(2):
                last = nc.gpsimd.tensor_tensor(cfg.qT[:, par, m, :, :], mid(cfg.q_all[:, m, :], 8), bc(sh.c("head16"), T), ALU.mult)
            last.then_inc(cfg.q_ready, 1)

        masked_queries(0, 1)
        masked_queries(1, plan.n_prep + 1)
        with eng.Fori(1, B - 2, 2) as b:
            for u in range(2):
                masked_queries(u, plan.base(b + u) + at + 1)
                norm_power(nc, sh, eng, ln, b + u)
        norm_power(nc, sh, eng, ln, B - 1)
        norm_power(nc, sh, eng, ln, B)

    cfg.pool = pool
    attention(nc, sh, cfg)




def top_two(nc, link, v, n, width, count, m):
    for best, hot in ((m.m1, m.oh1), (m.m2, m.oh2)):
        link(nc.vector.tensor_reduce(best[:, :], v[:, :, :], AX.X, ALU.max))
        link(nc.vector.tensor_tensor(m.t[:, :, :], v[:, :, :], bc(best[:, :], width), ALU.is_equal))
        link(nc.vector.tensor_tensor(m.t[:, :, :], m.t[:, :, :], mid(count, n), ALU.mult))
        link(nc.vector.tensor_reduce(m.r[:, :], m.t[:, :, :], AX.X, ALU.max))
        link(nc.vector.tensor_tensor(hot[:, :, :], m.t[:, :, :], bc(m.r[:, :], width), ALU.is_equal))
        if best is m.m1:
            link(nc.vector.scalar_tensor_tensor(v[:, :, :], hot[:, :, :], -FAR, v[:, :, :], ALU.mult, ALU.add))


def experts_0(nc, sh, w):
    NE = E0 + 1
    G = 4
    GT = G * T
    with ExitStack() as ctx:
        sb = lambda name, shape, dt=F32: ctx.enter_context(nc.sbuf_tensor("e0_" + name, shape, dt))
        sem = sem_maker(nc, ctx, "e0_")
        ps = sh.ps
        wT = sb("wT", [48, B, T], BF16)
        pick = sb("pick", [48, E0 * 128], BF16)
        with ExitStack() as gates:
            gb = lambda name, shape, dt=F32: gates.enter_context(nc.sbuf_tensor("e0_" + name, shape, dt))
            m = Shared()
            m.t, m.r, m.oh1, m.oh2 = gb("t", [T, B, E0]), gb("r", [T, B]), gb("oh1", [T, B, E0]), gb("oh2", [T, B, E0])
            m.m1, m.m2 = gb("m1", [T, B]), gb("m2", [T, B])
            v = gb("v", [T, B, E0])
            high, middle = gb("high", [T, B, E0], BF16), gb("middle", [T, B, E0], BF16)
            parts = gb("parts", [T, B, 3, E0])
            pick32 = gb("pick32", [48, E0 * 128])
            logits_mm, logit_ready, exp_done, parts_ready, wT_mm = (
                sem("logits_mm"), sem("logit_ready"), sem("exp_done"), sem("parts_ready"), sem("wT_mm"))
            chain, pick_loaded = sem("gate_chain"), sem("pick_loaded")
            with nc.Block() as block:
                @block.sync
                def _(sp):
                    sp.dma_start(pick32[:, :], sh.consts_in[0:48, N_CONST:N_CONST + E0 * 128]).then_inc(pick_loaded, 16)

                @block.gpsimd
                def _(pool):
                    pool.wait_ge(pick_loaded, 16)
                    nc.gpsimd.tensor_copy(pick[:, :], pick32[:, :])

                @block.tensor
                def _(pe):
                    pe.wait_ge(sh.w_loaded["gate0"], 32)
                    for b in range(B):
                        for c in range(2):
                            last = nc.tensor.matmul(ps[:T, 0, b * E0:(b + 1) * E0], sh.xnT[:, c, b, :], w.gate[:, c, :],
                                                    start=(c == 0), stop=(c == 1))
                    last.then_inc(logits_mm, 1)
                    pe.wait_ge(parts_ready, 1)
                    for g in range(B // G):
                        for u in range(G):
                            last = nc.tensor.transpose(ps[:48, 1 + g, u * T:(u + 1) * T],
                                                       parts[:, g * G + u, :, :].rearrange("p k e -> p (k e)"), sh.c("ident")[:T, :T])
                        last.then_inc(wT_mm, 1)

                @block.scalar
                def _(act):
                    act.wait_ge(logit_ready, 1)
                    nc.scalar.activation(v[:, :, :], v[:, :, :], ACT.Exp, scale=-1.0).then_inc(exp_done, 1)
                    for g in range(B // G):
                        act.wait_ge(wT_mm, g + 1)
                        nc.scalar.copy(wT[:, g * G:(g + 1) * G, :], ps[:48, 1 + g, 0:GT].rearrange("p (b t) -> p b t", b=G))

                @block.vector
                def _(dve):
                    link = chained(dve, chain, 0)
                    dve.wait_ge(sh.w_loaded["gate0"], 32)
                    dve.wait_ge(logits_mm, 1)
                    nc.vector.tensor_tensor(v[:, :, :], ps[:T, 0, 0:B * E0].rearrange("p (b e) -> p b e", e=E0),
                                            mid(w.gate_b[:, :], B), ALU.add).then_inc(logit_ready, 1)
                    dve.wait_ge(exp_done, 1)
                    link(nc.vector.tensor_scalar(v[:, :, :], v[:, :, :], 1.0, None, ALU.add))
                    link(nc.vector.reciprocal(v[:, :, :], v[:, :, :]))
                    top_two(nc, link, v, B, E0, sh.c("count16")[:T, :], m)
                    link(nc.vector.tensor_tensor(m.r[:, :], m.m1[:, :], m.m2[:, :], ALU.add))
                    link(nc.vector.reciprocal(m.r[:, :], m.r[:, :]))
                    link(nc.vector.tensor_tensor(m.m1[:, :], m.m1[:, :], m.r[:, :], ALU.mult))
                    link(nc.vector.tensor_tensor(m.m2[:, :], m.m2[:, :], m.r[:, :], ALU.mult))
                    link(nc.vector.tensor_tensor(m.oh1[:, :, :], m.oh1[:, :, :], bc(m.m1[:, :], E0), ALU.mult))
                    link(nc.vector.tensor_tensor(m.oh2[:, :, :], m.oh2[:, :, :], bc(m.m2[:, :], E0), ALU.mult))
                    link(nc.vector.tensor_tensor(v[:, :, :], m.oh1[:, :, :], m.oh2[:, :, :], ALU.add))
                    link(nc.vector.tensor_copy(high[:, :, :], v[:, :, :]))
                    link(nc.vector.tensor_tensor(v[:, :, :], v[:, :, :], high[:, :, :], ALU.subtract))
                    link(nc.vector.tensor_copy(middle[:, :, :], v[:, :, :]))
                    nc.vector.tensor_copy(parts[:, :, 0, :], high[:, :, :])
                    nc.vector.tensor_copy(parts[:, :, 1, :], middle[:, :, :])
                    nc.vector.tensor_tensor(parts[:, :, 2, :], v[:, :, :], middle[:, :, :], ALU.subtract).then_inc(parts_ready, 1)

        act_out = sb("act_out", [128, 2, GT])
        gated = sb("gated", [128, 2, GT])
        hidden = sb("hidden", [128, 2, GT])
        gate_mm, up_mm, silu_done, hidden_ready, sum_mm, sum_taken = (
            sem("gate_mm"), sem("up_mm"), sem("silu_done"), sem("hidden_ready"), sem("sum_mm"), sem("sum_taken"))
        chain = sem("chain")
        with nc.Block() as block:
            @block.scalar
            def _(act):
                with act.Fori(0, B // G) as g:
                    for e in range(NE):
                        act.wait_ge(gate_mm, g * NE + e + 1)
                        nc.scalar.activation(act_out[:, e % 2, :], ps[:, 3 * (e % 2), 0:GT], ACT.Silu).then_inc(silu_done, 1)

            @block.vector
            def _(dve):
                dve.sem_inc(sum_taken, 1)
                with dve.Fori(0, B // G) as g:
                    for e in range(NE):
                        par = e % 2
                        dve.wait_ge(silu_done, g * NE + e + 1)
                        dve.wait_ge(up_mm, g * NE + e + 1)
                        if e < E0:
                            nc.vector.tensor_tensor(gated[:, par, :], act_out[:, par, :], ps[:, 3 * par + 1, 0:GT], ALU.mult).then_inc(chain, 1)
                            dve.wait_ge(chain, g * E0 + e + 1)
                            nc.vector.tensor_tensor(hidden[:, par, :], gated[:, par, :], ps[:, 3 * par + 2, 0:GT], ALU.mult).then_inc(hidden_ready, 1)
                        else:
                            nc.vector.tensor_tensor(hidden[:, par, :], act_out[:, par, :], ps[:, 3 * par + 1, 0:GT], ALU.mult).then_inc(hidden_ready, 1)
                    dve.wait_ge(sum_mm, g + 1)
                    x = sh.xnT[:, :, bass.ds(g * G, G), :].rearrange("p c b t -> p c (b t)")
                    nc.vector.tensor_tensor(x, x, ps[:, 6:8, 0:GT], ALU.add).then_inc(sum_taken, 1)

            @block.tensor
            def _(pe):
                pe.wait_ge(sh.w_loaded["experts0"], 16 * 6)

                def down(g, e):
                    pe.wait_ge(hidden_ready, g * NE + e + 1)
                    if e == 0:
                        pe.wait_ge(sum_taken, g + 1)
                    for mo in range(2):
                        last = nc.tensor.matmul(ps[:, 6 + mo, 0:GT], w.down[:, e, mo * 128:(mo + 1) * 128], hidden[:, e % 2, :],
                                                start=(e == 0), stop=(e == NE - 1))
                    return last

                with pe.Fori(0, B // G) as g:
                    x = sh.xnT[:, :, bass.ds(g * G, G), :].rearrange("p c b t -> p c (b t)")
                    for e in range(NE):
                        bank = 3 * (e % 2)
                        for c in range(2):
                            last = nc.tensor.matmul(ps[:, bank, 0:GT], w.gates[:, e, c, :], x[:, c, :], start=(c == 0), stop=(c == 1))
                        last.then_inc(gate_mm, 1)
                        for c in range(2):
                            last = nc.tensor.matmul(ps[:, bank + 1, 0:GT], w.up[:, e, c, :], x[:, c, :], start=(c == 0), stop=(c == 1))
                        if e < E0:
                            last = nc.tensor.matmul(ps[:, bank + 2, 0:GT], pick[:, e * 128:(e + 1) * 128],
                                                    wT[:, bass.ds(g * G, G), :].rearrange("p b t -> p (b t)"), start=True, stop=True)
                        last.then_inc(up_mm, 1)
                        if e > 0:
                            down(g, e - 1)
                    down(g, NE - 1).then_inc(sum_mm, 1)



def self_attention_1(nc, sh, w):
    cfg = Shared()
    cfg.tag, cfg.heads, cfg.dh, cfg.per_stage, cfg.keys, cfg.key_chunks = "s1_", 16, 64, 4, T, 1
    cfg.out_chunks, cfg.n_oT_steps = 8, 2
    cfg.banks, cfg.score_banks, cfg.pt_buffers = (0, 2, 4, 6, 2), 1, 2
    cfg.scale = 1.0 / 8
    cfg.fin_at = [0, 1, 4, 8]
    cfg.twice, cfg.keep_rows = True, False
    cfg.out_bias = cfg.v_bias = None
    cfg.w_out = w.out
    cfg.dve_slot = cfg.dve_before = None
    cfg.stage_heads = lambda i: [4 * i + x for x in range(4)]
    cfg.stage_columns = lambda i: slice(4 * i, 4 * i + 4)
    wv = w.qkv[:, :, :].rearrange("p c (n j) -> p c j n", j=3)

    def allocate(ctx, sb, sem):
        cfg.kT = sb("kT", [128, 2, 8, T])
        cfg.qT = sb("qT", [128, 2, 2, 8, T])
        cfg.own = sb("own", [128, 2, T])

    cfg.allocate = allocate

    def head_operands(par, h):
        return cfg.qT[:, par, h % 2, h // 2, :], cfg.kT[:, par, h // 2, :]

    cfg.head_operands = head_operands
    cfg.wait_weights = lambda eng: eng.wait_ge(sh.w_loaded["s1"], 32)

    def queries_keys(pe, k, bank, b, at, par):
        for u in range(4):
            n = k % 2 * 4 + u
            for c in range(2):
                last = nc.tensor.matmul(bank[:, u * T:(u + 1) * T], wv[:, c, k // 2, n * 128:(n + 1) * 128], sh.xnT[:, c, b, :],
                                        start=(c == 0), stop=(c == 1))
        return last

    def values(pe, k, bank, b, at, par):
        if k == 4:
            pe.wait_ge(cfg.sem_side_done, at - 1)
        for c in range(2):
            last = nc.tensor.matmul(bank[:T, :], cfg.own[:, c, :], wv[:, c, 2, (k - 4) * 512:(k - 3) * 512],
                                    start=(c == 0), stop=(c == 1))
        return last

    cfg.prep_mm = [queries_keys] * 4 + [values] * 2

    def prep_act(k, bank, b, par):
        if k < 4:
            pairs, src = slice(k % 2 * 4, k % 2 * 4 + 4), bank[:, 0:4 * T].rearrange("p (u t) -> p u t", u=4)
            if k >= 2:
                return nc.scalar.copy(cfg.kT[:, par, pairs, :], src)
            for half in range(2):
                rows = slice(64 * half, 64 * half + 64)
                last = nc.scalar.copy(cfg.qT[rows, par, half, pairs, :], src[rows])
            if k == 0:
                last = nc.scalar.copy(cfg.own[:, :, :], sh.xnT[:, :, b, :])
            return last
        return nc.scalar.copy(cfg.v_at(par, 0)[:, (k - 4) * 4:(k - 3) * 4], bank[:T, :].rearrange("p (c j d) -> p c j d", c=4, d=64))

    cfg.prep_act = prep_act

    def xnT_act(b, src):
        for c in range(2):
            last = nc.scalar.activation(sh.xnT[:, c, b, :], src[:, c, :], ACT.Identity,
                                        bias=sh.columns[:, 146 + c:147 + c], scale=sh.columns[:, 144 + c:145 + c])
        return last

    cfg.xnT_act = xnT_act
    cfg.sync = lambda sp, plan: None

    def pool(eng, plan, ln):
        with eng.Fori(0, B) as b:
            norm_power(nc, sh, eng, ln, b * 2 + 1)
            norm_power(nc, sh, eng, ln, b * 2 + 2)

    cfg.pool = pool
    attention(nc, sh, cfg)



def context_attention_1(nc, sh, w):
    cfg = Shared()
    cfg.tag, cfg.heads, cfg.dh, cfg.per_stage, cfg.keys, cfg.key_chunks = "c1_", 8, 64, 1, S, NK
    cfg.out_chunks, cfg.n_oT_steps = 4, 1
    cfg.banks, cfg.score_banks, cfg.pt_buffers = (0, 2, 4, 5, 3), 1, 2
    cfg.scale = 1.0 / 8
    cfg.fin_at = [0, 3, 7]
    cfg.twice, cfg.keep_rows = False, True
    cfg.out_bias, cfg.v_bias, cfg.w_out = w.bo[:, :], None, w.out
    ident = sh.c("ident")
    cfg.stage_heads = lambda i: [i]
    cfg.stage_columns = lambda i: slice(i, i + 1)
    cfg.ctx_last_use = None

    def allocate(ctx, sb, sem):
        cfg.ctx_in = sb("ctx_in", [KC, 2, NK, D])
        cfg.cn = sb("cn", [KC, NK, D])
        cfg.ctxT = sb("ctxT", [128, 2, S])
        cfg.kT = sb("kT", [128, 2, 4, S])
        cfg.qT = sb("qT", [128, 2, 2, 4, T])
        cfg.stats = sb("ctx_stats", [KC, NK, 6])
        cfg.mv = sb("ctx_mean_var", [KC, NK, 2])
        cfg.veps = sb("ctx_var_eps", [KC, NK])
        cfg.rstd = sb("ctx_rstd", [KC, NK])
        cfg.ctx_loaded = [sem(f"ctx_loaded{u}") for u in range(2)]
        cfg.ctx_var, cfg.ctx_rstd, cfg.cn_ready, cfg.chain = sem("ctx_var"), sem("ctx_rstd"), sem("cn_ready"), sem("ctx_chain")

    cfg.allocate = allocate

    def head_operands(par, h):
        return cfg.qT[:, par, h % 2, h // 2, :], cfg.kT[:, par, h // 2, :]

    cfg.head_operands = head_operands
    cfg.wait_weights = lambda eng: eng.wait_ge(sh.w_loaded["c1"], 64)

    def queries(pe, k, bank, b, at, par):
        for m in range(4):
            for c in range(2):
                last = nc.tensor.matmul(bank[:, m * T:(m + 1) * T], w.q[:, c, m * 128:(m + 1) * 128], sh.xnT[:, c, b, :],
                                        start=(c == 0), stop=(c == 1))
        return last

    def transposes(pe, k, bank, b, at, par):
        if k == 1:
            pe.wait_ge(cfg.cn_ready, b + 1)
        for j in range(NK):
            last = nc.tensor.transpose(bank[:, j * KC:(j + 1) * KC], cfg.cn[:, j, (k - 1) * 128:k * 128], ident[:KC, :KC])
        return last

    def keys(pe, k, bank, b, at, par):
        m = k - 3
        if m == 0:
            pe.wait_ge(cfg.sem_side_done, at)
        for c in range(2):
            last = nc.tensor.matmul(bank[:, 0:S], w.kv[:, c, m * 128:(m + 1) * 128], cfg.ctxT[:, c, :], start=(c == 0), stop=(c == 1))
        return last

    def values(pe, k, bank, b, at, par):
        j = k - 7
        for c in range(2):
            last = nc.tensor.matmul(bank[:KC, :], cfg.ctxT[:, c, j * KC:(j + 1) * KC], w.kv[:, c, 512:1024], start=(c == 0), stop=(c == 1))
        return last

    cfg.prep_mm = [queries] + [transposes] * 2 + [keys] * 4 + [values] * 3

    def prep_act(k, bank, b, par):
        if k == 0:
            for half in range(2):
                rows = slice(64 * half, 64 * half + 64)
                last = nc.scalar.copy(cfg.qT[rows, par, half, :, :], bank[rows, 0:4 * T].rearrange("p (m t) -> p m t", m=4))
            return last
        if k < 3:
            c = k - 1
            return nc.scalar.activation(cfg.ctxT[:, c, :], bank[:, 0:S], ACT.Identity,
                                        bias=sh.columns[:, 150 + c:151 + c], scale=sh.columns[:, 148 + c:149 + c])
        if k < 7:
            return nc.scalar.copy(cfg.kT[:, par, k - 3, :], bank[:, 0:S])
        return nc.scalar.copy(cfg.v_at(par, k - 7), bank[:KC, :].rearrange("p (c j d) -> p c j d", c=4, d=64))

    cfg.prep_act = prep_act
    cfg.xnT_act = lambda b, src: nc.scalar.copy(sh.xnT[:, :, b, :], src)

    def context_norm(dve, b, par):
        link = chained(dve, cfg.chain, b * 2)
        dve.wait_ge(cfg.ctx_loaded[par], b * 8 + 16 - 8 * par)
        dve.sem_inc(cfg.passed, 1)
        for j in range(NK):
            last = nc.vector.bn_stats(cfg.stats[:, j, :], cfg.ctx_in[:, par, j, :])
        link(last, cfg.passed)
        for j in range(NK):
            last = nc.vector.bn_aggr(cfg.mv[:, j, :], cfg.stats[:, j, :])
        link(last)
        nc.vector.tensor_scalar(cfg.veps[:, :], cfg.mv[:, :, 1], LN_EPS, None, ALU.add).then_inc(cfg.ctx_var, 1)
        dve.wait_ge(cfg.ctx_rstd, b + 1)
        for j in range(NK):
            last = nc.vector.tensor_scalar(cfg.cn[:, j, :], cfg.ctx_in[:, par, j, :], cfg.mv[:, j, 0:1],
                                           cfg.rstd[:, j:j + 1], ALU.subtract, ALU.mult)
        last.then_inc(cfg.cn_ready, 1)

    def dve_before(dve, ln):
        cfg.passed = ln.passed
        context_norm(dve, 0, 0)
        dve.wait_ge(cfg.sem_side_done, 3)
        cfg.now = 0

    def dve_slot(dve, s, b, par, ln, more):
        if s == 0 and more:
            context_norm(dve, b + 1, par)

    cfg.dve_before, cfg.dve_slot = dve_before, dve_slot

    def pool(eng, plan, ln):
        def power():
            pass

        def of_context(b):
            eng.wait_ge(cfg.ctx_var, b + 1)
            nc.gpsimd.tensor_tensor(cfg.rstd[:, :], cfg.veps[:, :], sh.c("minus_half")[:KC, 0:NK], ALU.pow).then_inc(cfg.ctx_rstd, 1)

        of_context(0)
        of_context(1)
        with eng.Fori(0, B - 2) as b:
            of_context(b + 2)
            norm_power(nc, sh, eng, ln, b + 1)
        norm_power(nc, sh, eng, ln, B - 1)
        norm_power(nc, sh, eng, ln, B)

    cfg.pool = pool

    def sync(sp, plan):
        src = sh.ins["ctx_1024"].rearrange("b (j p) d -> b p j d", p=KC)
        for u in range(2):
            sp.dma_start(cfg.ctx_in[:, u, :, :], src[u]).then_inc(cfg.ctx_loaded[u], 16)
        with sp.Fori(2, B - 1, 2) as b:
            for u in range(2):
                sp.wait_ge(cfg.cn_ready, b + u - 1)
                sp.dma_start(cfg.ctx_in[:, u, :, :], src[b + u]).then_inc(cfg.ctx_loaded[u], 16)

    cfg.sync = sync
    attention(nc, sh, cfg)



def experts_1(nc, sh, w):
    NS = E1 * CAP
    HALF = B * CAP // 2
    NJ = H1 // 128
    with ExitStack() as ctx:
        sb = lambda name, shape, dt=F32: ctx.enter_context(nc.sbuf_tensor("e1_" + name, shape, dt))
        sem = sem_maker(nc, ctx, "e1_")
        ps = sh.ps
        m = Shared()
        m.t, m.r, m.oh1, m.oh2 = sb("t", [T, B, E1]), sb("r", [T, B]), sb("oh1", [T, B, E1]), sb("oh2", [T, B, E1])
        m.m1, m.m2 = sb("m1", [T, B]), sb("m2", [T, B])
        lg = sb("lg", [T, B, E1])
        pos = sb("pos", [T, 2, B])
        held = sb("held", [T, 2, B])
        prob = sb("prob", [T, 2, B])
        ex = sb("ex", [128, 2, E1, B * CAP])
        logits_mm, hot_ready, counts_mm, diff_ready, ediff_ready, chain = (
            sem("logits_mm"), sem("hot_ready"), sem("counts_mm"), sem("diff_ready"), sem("ediff_ready"), sem("chain"))

        wfc, wgt = sb("wfc", [128, 2, 2, H1]), sb("wgt", [128, 2, 2, H1])
        wpj = sb("wpj", [128, 2, NJ, D])
        w_in = [sem(f"w_in{u}") for u in range(2)]

        def load_expert(sp, e, u):
            for dst, name, pat in ((wgt, "w_gate", "e (c p) n -> e p c n"), (wfc, "w_c_fc", "e (c p) n -> e p c n"),
                                   (wpj, "w_c_proj", "e (j p) n -> e p j n")):
                sp.dma_start(dst[:, u, :, :], sh.ins["L1_ffn_" + name].rearrange(pat, p=128)[e]).then_inc(w_in[u], 16)

        with nc.Block() as block:
            @block.sync
            def _(sp):
                load_expert(sp, 0, 0)
                load_expert(sp, 1, 1)

            @block.tensor
            def _(pe):
                pe.wait_ge(sh.w_loaded["router1"], 32)
                for b in range(B):
                    for c in range(2):
                        last = nc.tensor.matmul(ps[:T, 0, b * E1:(b + 1) * E1], sh.xnT[:, c, b, :], w.router[:, c, :],
                                                start=(c == 0), stop=(c == 1))
                last.then_inc(logits_mm, 1)
                pe.wait_ge(hot_ready, 1)
                flat = lambda a: a[:, :, :].rearrange("p b e -> p (b e)")
                nc.tensor.matmul(ps[:T, 1, 0:B * E1], sh.c("upto")[:T, :], flat(m.oh1), start=True, stop=True)
                nc.tensor.matmul(ps[:T, 2, 0:B * E1], sh.c("upto")[:T, :], flat(m.oh2), start=True, stop=False)
                nc.tensor.matmul(ps[:T, 2, 0:B * E1], sh.c("ones")[:T, :], flat(m.oh1), start=False, stop=True).then_inc(counts_mm, 1)

            @block.scalar
            def _(act):
                act.wait_ge(diff_ready, 1)
                nc.scalar.activation(prob[:, 1, :], m.r[:, :], ACT.Exp).then_inc(ediff_ready, 1)

            @block.vector
            def _(dve):
                link = chained(dve, chain, 0)
                dve.wait_ge(sh.w_loaded["router1"], 32)
                dve.wait_ge(logits_mm, 1)
                link(nc.vector.tensor_tensor(lg[:, :, :], ps[:T, 0, 0:B * E1].rearrange("p (b e) -> p b e", e=E1),
                                             mid(w.router_b[:, :], B), ALU.add))
                top_two(nc, link, lg, B, E1, sh.c("count16")[:T, 16 - E1:16], m)
                dve.sem_inc(hot_ready, 1)
                nc.vector.tensor_tensor(m.r[:, :], m.m2[:, :], m.m1[:, :], ALU.subtract).then_inc(diff_ready, 1)
                dve.wait_ge(ediff_ready, 1)
                link(nc.vector.tensor_scalar(prob[:, 0, :], prob[:, 1, :], 1.0, None, ALU.add))
                link(nc.vector.reciprocal(prob[:, 0, :], prob[:, 0, :]))
                link(nc.vector.tensor_tensor(prob[:, 1, :], prob[:, 1, :], prob[:, 0, :], ALU.mult))
                dve.wait_ge(counts_mm, 1)
                for n, hot in enumerate((m.oh1, m.oh2)):
                    link(nc.vector.tensor_tensor(m.t[:, :, :], hot[:, :, :], ps[:T, 1 + n, 0:B * E1].rearrange("p (b e) -> p b e", e=E1), ALU.mult))
                    link(nc.vector.tensor_reduce(pos[:, n, :], m.t[:, :, :], AX.X, ALU.add))
                link(nc.vector.tensor_scalar(pos[:, :, :], pos[:, :, :], -1.0, None, ALU.add))
                link(nc.vector.tensor_scalar(held[:, :, :], pos[:, :, :], float(CAP - 1), None, ALU.min))

        sel = sb("sel", [T, 2, CAP])
        part = sb("part", [T, 2, E1, CAP])
        oneh = sb("oneh", [T, E1, CAP])
        own = sb("own", [T, D])
        oneh_ready, own_ready, slots_mm, slots_ready, sel_chain = (
            sem("oneh_ready"), sem("own_ready"), sem("slots_mm"), sem("slots_ready"), sem("sel_chain"))

        def one_hot(dve, link, at, b, scaled):
            for n in range(2):
                if scaled:
                    last = nc.vector.tensor_scalar(sel[:, n, :], sh.c("slots")[:T, :], at[:, n, b:b + 1] if isinstance(b, int) else at[:, n, bass.ds(b, 1)],
                                                   prob[:, n, b:b + 1] if isinstance(b, int) else prob[:, n, bass.ds(b, 1)], ALU.is_equal, ALU.mult)
                else:
                    last = nc.vector.tensor_scalar(sel[:, n, :], sh.c("slots")[:T, :], at[:, n, b:b + 1] if isinstance(b, int) else at[:, n, bass.ds(b, 1)],
                                                   None, ALU.is_equal)
            link(last)
            for n, hot in enumerate((m.oh1, m.oh2)):
                last = nc.vector.tensor_tensor(part[:, n, :, :], bc(hot[:, b, :], CAP), mid(sel[:, n, :], E1), ALU.mult)
            link(last)

        with nc.Block() as block:
            @block.vector
            def _(dve):
                def step(b, first=False):
                    link = chained(dve, sel_chain, b * 2)
                    one_hot(dve, link, pos, b, False)
                    if not first:
                        dve.wait_ge(slots_mm, b)
                    nc.vector.tensor_tensor(oneh[:, :, :], part[:, 0, :, :], part[:, 1, :, :], ALU.add).then_inc(oneh_ready, 1)

                step(0, True)
                with dve.Fori(1, B) as b:
                    step(b)

            @block.scalar
            def _(act):
                def take(b):
                    act.wait_ge(slots_mm, b + 1)
                    for c in range(2):
                        last = nc.scalar.copy(ex[:, c, :, bass.ds(b * CAP, CAP)], ps[:, c, 0:NS].rearrange("p (e s) -> p e s", e=E1))
                    last.then_inc(slots_ready, 1)

                nc.scalar.copy(own[:, :], sh.XN[:, 0, :]).then_inc(own_ready, 1)
                with act.Fori(0, B - 1) as b:
                    take(b)
                    nc.scalar.copy(own[:, :], sh.XN[:, b + 1, :]).then_inc(own_ready, 1)
                take(B - 1)

            @block.tensor
            def _(pe):
                def step(b, first=False):
                    pe.wait_ge(own_ready, b + 1)
                    pe.wait_ge(oneh_ready, b + 1)
                    if not first:
                        pe.wait_ge(slots_ready, b)
                    for c in range(2):
                        last = nc.tensor.matmul(ps[:, c, 0:NS], own[:, c * 128:(c + 1) * 128],
                                                oneh[:, :, :].rearrange("p e s -> p (e s)"), start=True, stop=True)
                    last.then_inc(slots_mm, 1)

                step(0, True)
                with pe.Fori(1, B) as b:
                    step(b)

        gbuf = sb("gbuf", [128, 2, HALF])
        ubuf = sb("ubuf", [128, 2, 2, HALF])
        hid = sb("hid", [128, 2, 2, HALF])
        g_mm, h_mm, g_taken, u_ready, hid_ready, expert_mm, out_taken, passed = (
            sem("g_mm"), sem("h_mm"), sem("g_taken"), sem("u_ready"), sem("hid_ready"), sem("expert_mm"), sem("out_taken"), sem("passed"))
        with nc.Block() as block:
            @block.sync
            def _(sp):
                with sp.Fori(2, E1 - 1, 2) as e:
                    for u in range(2):
                        sp.wait_ge(expert_mm, e + u - 1)
                        load_expert(sp, e + u, u)

            @block.scalar
            def _(act):
                act.sem_inc(g_taken, 1)
                with act.Fori(0, E1 - 1, 2) as e2:
                    for n in range(2 * NJ):
                        e, j = e2 + n // NJ, n % NJ
                        n_all = e2 * NJ + n
                        act.wait_ge(g_mm, n_all + 1)
                        act.sem_inc(passed, 1)
                        nc.scalar.activation(gbuf[:, :, :], ps[:, 2:4, 0:HALF], ACT.Identity,
                                             bias=sh.columns[:, bass.ds(n_all + 64, 1)]).then_inc(g_taken, 1)
                        act.wait_ge(u_ready, n_all + 2)
                        nc.scalar.activation(hid[:, j % 2, :, :], ubuf[:, j % 2, :, :], ACT.Silu).then_inc(hid_ready, 1)

            @block.vector
            def _(dve):
                dve.sem_inc(u_ready, 1)
                dve.sem_inc(out_taken, 1)
                with dve.Fori(0, E1 - 1, 2) as e2:
                    for n in range(2 * NJ):
                        e, j = e2 + n // NJ, n % NJ
                        n_all = e2 * NJ + n
                        dve.wait_ge(h_mm, n_all + 1)
                        dve.wait_ge(g_taken, n_all + 2)
                        nc.vector.scalar_tensor_tensor(ubuf[:, j % 2, :, :], ps[:, 0:2, 0:HALF], sh.columns[:, bass.ds(n_all, 1)],
                                                       gbuf[:, :, :], ALU.add, ALU.mult).then_inc(u_ready, 1)
                        if j == NJ - 1:
                            dve.wait_ge(expert_mm, e + 1)
                            for mo in range(2):
                                last = nc.vector.tensor_scalar(ex[:, mo, e, :].rearrange("p (a n) -> p a n", a=2),
                                                               ps[:, 4 + 2 * mo:6 + 2 * mo, 0:HALF],
                                                               sh.columns[:, bass.ds(e * 2 + 128 + mo, 1)], None, ALU.add)
                            last.then_inc(out_taken, 1)

            @block.tensor
            def _(pe):
                def hidden_products(e, u, j, n_all):
                    for wt, bank, free, done in ((wgt, 2, g_taken, g_mm), (wfc, 0, u_ready, h_mm)):
                        pe.wait_ge(free, n_all + 1)
                        for half in range(2):
                            for c in range(2):
                                last = nc.tensor.matmul(ps[:, bank + half, 0:HALF], wt[:, u, c, j * 128:(j + 1) * 128],
                                                        ex[:, c, e, half * HALF:(half + 1) * HALF], start=(c == 0), stop=(c == 1))
                        last.then_inc(done, 1)

                def out_products(e, u, j, n_all):
                    pe.wait_ge(hid_ready, n_all + 1)
                    if j == 0:
                        pe.wait_ge(out_taken, e + 1)
                    for mo in range(2):
                        for half in range(2):
                            last = nc.tensor.matmul(ps[:, 4 + 2 * mo + half, 0:HALF], wpj[:, u, j, mo * 128:(mo + 1) * 128],
                                                    hid[:, j % 2, half, :], start=(j == 0), stop=(j == NJ - 1))
                    if j == NJ - 1:
                        last.then_inc(expert_mm, 1)

                with pe.Fori(0, E1 - 1, 2) as e2:
                    for u in range(2):
                        e = e2 + u
                        pe.wait_ge(w_in[u], e2 * 24 + 48)
                        for j in range(NJ):
                            hidden_products(e, u, j, e * NJ + j)
                            if j > 0:
                                out_products(e, u, j - 1, e * NJ + j - 1)
                        out_products(e, u, NJ - 1, e * NJ + NJ - 1)

        CH = [(0, 3), (3, 6), (6, 8)]
        own_ex = sb("own_ex", [128, 2, E1, CAP])
        gT = sb("gT", [3 * CAP, 3, T])
        oS = sb("oS", [3 * CAP, 3, D])
        ohc_ready, ownx_ready, tr_mm, tr_ready, y_mm, x_ready, comb_chain = (
            sem("ohc_ready"), sem("ownx_ready"), sem("tr_mm"), sem("tr_ready"), sem("y_mm"), sem("x_ready"), sem("comb_chain"))
        stored = sem("stored")
        with nc.Block() as block:
            @block.sync
            def _(sp):
                with sp.Fori(0, B) as b:
                    sp.wait_ge(x_ready, b + 1)
                    sp.dma_start(sh.out[b], sh.X[:, b, :]).then_inc(stored, 16)
                sp.wait_ge(stored, 16 * B)

            @block.vector
            def _(dve):
                def matrix(b, first=False):
                    link = chained(dve, comb_chain, b * 2)
                    one_hot(dve, link, held, b, True)
                    if not first:
                        dve.wait_ge(tr_mm, b)
                    nc.vector.tensor_tensor(oneh[:, :, :], part[:, 0, :, :], part[:, 1, :, :], ALU.add).then_inc(ohc_ready, 1)

                def rows(b):
                    dve.wait_ge(y_mm, b + 1)
                    nc.vector.tensor_tensor(sh.X[:, b, :], sh.X[:, b, :], ps[:T, 3, 0:D], ALU.add).then_inc(x_ready, 1)

                matrix(0, True)
                with dve.Fori(0, B - 1) as b:
                    matrix(b + 1)
                    rows(b)
                rows(B - 1)

            @block.gpsimd
            def _(pool):
                def step(b, first=False):
                    if not first:
                        pool.wait_ge(tr_mm, b)
                        pool.sem_inc(passed, 1)
                    for c in range(2):
                        last = nc.gpsimd.tensor_copy(own_ex[:, c, :, :], ex[:, c, :, bass.ds(b * CAP, CAP)])
                    last.then_inc(ownx_ready, 1)

                step(0, True)
                with pool.Fori(1, B) as b:
                    step(b)

            @block.scalar
            def _(act):
                def step(b, first=False):
                    act.wait_ge(tr_mm, b + 1)
                    if not first:
                        act.wait_ge(y_mm, b)
                    nc.scalar.copy(gT[:, 0:2, :], ps[:3 * CAP, 0, 0:2 * T].rearrange("p (q t) -> p q t", q=2))
                    nc.scalar.copy(gT[:2 * CAP, 2, :], ps[:2 * CAP, 0, 2 * T:3 * T])
                    nc.scalar.copy(oS[:, 0:2, :], ps[:3 * CAP, 1, :].rearrange("p (q n) -> p q n", q=2))
                    nc.scalar.copy(oS[:2 * CAP, 2, :], ps[:2 * CAP, 2, 0:D]).then_inc(tr_ready, 1)

                step(0, True)
                with act.Fori(1, B) as b:
                    step(b)

            @block.tensor
            def _(pe):
                ident = sh.c("ident")

                def transposes(b):
                    pe.wait_ge(ohc_ready, b + 1)
                    pe.wait_ge(ownx_ready, b + 1)
                    for q, (lo, hi) in enumerate(CH):
                        n = (hi - lo) * CAP
                        nc.tensor.transpose(ps[:n, 0, q * T:(q + 1) * T], oneh[:, lo:hi, :].rearrange("p e s -> p (e s)"), ident[:T, :T])
                        for c in range(2):
                            last = nc.tensor.transpose(ps[:n, 1 + q // 2, q % 2 * D + c * 128:q % 2 * D + (c + 1) * 128],
                                                       own_ex[:, c, lo:hi, :].rearrange("p e s -> p (e s)"), ident)
                    last.then_inc(tr_mm, 1)

                def product(b, first=False):
                    pe.wait_ge(tr_ready, b + 1)
                    if not first:
                        pe.wait_ge(x_ready, b)
                    for q, (lo, hi) in enumerate(CH):
                        n = (hi - lo) * CAP
                        last = nc.tensor.matmul(ps[:T, 3, 0:D], gT[:n, q, :], oS[:n, q, :], start=(q == 0), stop=(q == 2))
                    last.then_inc(y_mm, 1)

                transposes(0)
                product(0, True)
                with pe.Fori(1, B) as b:
                    transposes(b)
                    product(b)


def decoder(nc, ins, consts_in, out):
    with ExitStack() as ctx:
        sb = lambda name, shape, dt=F32: ctx.enter_context(nc.sbuf_tensor(name, shape, dt))
        sem = lambda name: ctx.enter_context(nc.semaphore(name))
        sh = Shared()
        sh.ins, sh.consts_in, sh.out = ins, consts_in, out
        sh.const = sb("const", [128, N_CONST])
        sh.c = lambda name: sh.const[:, CONSTS[name][0]:CONSTS[name][0] + CONSTS[name][1]]
        sh.X = sb("X", [T, B, D])
        sh.xnT = sb("xnT", [128, 2, B, T])
        sh.columns = sb("columns", [128, 160])
        sh.ps = ctx.enter_context(nc.psum_tensor("ps", [128, 8, 512], F32))
        sh.const_loaded, sh.x_loaded, stored = sem("const_loaded"), sem("x_loaded"), sem("stored")
        sh.w_loaded = {}
        sh.early_loads = []

        def early(name, dst, src):
            if name not in sh.w_loaded:
                sh.w_loaded[name] = sem("loaded_" + name)
            sh.early_loads.append((dst, src, name))

        sh.early = early
        layer0 = ExitStack()
        s0 = lambda name, shape, dt=F32: layer0.enter_context(nc.sbuf_tensor(name, shape, dt))
        wo0 = s0("wo0", [128, 2, D])
        bo0 = s0("bo0", [T, D])
        early("wo0", wo0[:, :, :], ins["L0_attn_Wo"].rearrange("(c p) n -> p c n", p=128))
        early("wo0", bo0[:, :], ins["L0_attn_bo"].partition_broadcast(T))
        w0 = Shared()
        w0.bv, w0.bo = sh.columns[:, 156:158], s0("c0_bo", [T, D])
        early("c0", w0.bo[:, :], ins["L0_xattn_b_O"].partition_broadcast(T))
        w0.n_loads = 5
        w0.bk, w0.bq_scaled = sh.columns[:, 154:156], sh.columns[:, 158:160]
        w0.wq, w0.wk, w0.wv, w0.wo = (s0("c0_w" + n, [128, 2, D]) for n in "qkvo")
        for n, t in (("Q", w0.wq), ("K", w0.wk), ("V", w0.wv), ("O", w0.wo)):
            early("c0", t[:, :, :], ins["L0_xattn_W_" + n].rearrange("(c p) n -> p c n", p=128))
        with nc.sbuf_tensor("attnT", [128, 2, B, T], F32) as attnT:
            sh.attnT = attnT
            linear_attention(nc, sh)
            L = T // B
            permuted = attnT[:, :, :, :].rearrange("p c b l -> p c l b")
            with nc.Block() as block:
                @block.tensor
                def _(pe):
                    pe.wait_ge(sh.w_loaded["wo0"], 32)

                @block.vector
                def _(dve):
                    dve.wait_ge(sh.w_loaded["wo0"], 32)
            add_and_norm(nc, sh, "ao_", lambda p: permuted[:, :, bass.ds(2 * p * L, 2 * L), :], wo0, bo0[:, :])
        bias_columns(nc, sh)
        weights = Shared()

        def load_now(name, dst, src):
            if name not in sh.w_loaded:
                sh.w_loaded[name] = sem("loaded_" + name)
            sh.now.append((dst, src, name))

        def issue():
            with nc.Block() as block:
                @block.sync
                def _(sp):
                    for dst, src, name in sh.now:
                        sp.dma_start(dst, src).then_inc(sh.w_loaded[name], 16)
            sh.now = []

        sh.now = []
        with layer0:
            e0 = Shared()
            e0.gate, e0.gate_b = s0("e0_gate", [128, 2, E0]), s0("e0_gate_b", [T, E0])
            e0.gates, e0.up, e0.down = (s0("e0_gates", [128, E0 + 1, 2, I0]), s0("e0_up", [128, E0 + 1, 2, I0]),
                                        s0("e0_down", [128, E0 + 1, D]))
            load_now("gate0", e0.gate[:, :, :], ins["L0_ffn_gate_w"].rearrange("(c p) n -> p c n", p=128))
            load_now("gate0", e0.gate_b[:, :], ins["L0_ffn_gate_b"].partition_broadcast(T))
            for dst, name in ((e0.gates, "wg"), (e0.up, "wu")):
                load_now("experts0", dst[:, 0:E0, :, :], ins["L0_ffn_experts_" + name].rearrange("e (c p) n -> p e c n", p=128))
                load_now("experts0", dst[:, E0, :, :], ins["L0_ffn_shared_" + name].rearrange("(c p) n -> p c n", p=128))
            load_now("experts0", e0.down[:, 0:E0, :], ins["L0_ffn_experts_wd"].rearrange("e p n -> p e n"))
            load_now("experts0", e0.down[:, E0, :], ins["L0_ffn_shared_wd"])
            issue()
            context_attention_0(nc, sh, w0)
            experts_0(nc, sh, e0)
            add_and_norm(nc, sh, "ea_", lambda p: sh.xnT[:, :, bass.ds(2 * p, 2), :])
        s1, c1, e1 = Shared(), Shared(), Shared()
        e1.router, e1.router_b = sb("e1_router", [128, 2, E1]), sb("e1_router_b", [T, E1])
        sh.XN = sb("XN", [T, B, D])
        attentions1 = ctx.enter_context(ExitStack())
        sa = lambda name, shape, dt=F32: attentions1.enter_context(nc.sbuf_tensor(name, shape, dt))
        s1.qkv, s1.out = sa("s1_qkv", [128, 2, 3072]), sa("s1_out", [128, 8, D])
        load_now("s1", s1.qkv[:, :, :], ins["L1_attn_W_qkv"].rearrange("(c p) n -> p c n", p=128))
        load_now("s1", s1.out[:, :, :], ins["L1_attn_W_out"].rearrange("(c p) n -> p c n", p=128))
        c1.q, c1.kv, c1.out, c1.bo = (sa("c1_q", [128, 2, 512]), sa("c1_kv", [128, 2, 1024]), sa("c1_out", [128, 4, D]),
                                      sa("c1_bo", [T, D]))
        load_now("c1", c1.q[:, :, :], ins["L1_xattn_Wq"].rearrange("(c p) n -> p c n", p=128))
        load_now("c1", c1.kv[:, :, :], ins["L1_xattn_Wkv"].rearrange("(c p) n -> p c n", p=128))
        load_now("c1", c1.out[:, :, :], ins["L1_xattn_Wout"].rearrange("(c p) n -> p c n", p=128))
        load_now("c1", c1.bo[:, :], ins["L1_xattn_bout"].partition_broadcast(T))
        load_now("router1", e1.router[:, :, :], ins["L1_ffn_router_w"].rearrange("(c p) n -> p c n", p=128))
        load_now("router1", e1.router_b[:, :], ins["L1_ffn_router_b"].partition_broadcast(T))
        issue()
        self_attention_1(nc, sh, s1)
        context_attention_1(nc, sh, c1)
        attentions1.close()
        experts_1(nc, sh, e1)


_INS = ["x", "ctx_1024"] + ["L0_attn_" + n for n in ("Wq", "bq", "Wk", "bk", "Wv", "bv", "Wo", "bo")] \
    + ["L0_xattn_" + n for n in ("W_Q", "b_Q", "W_K", "b_K", "W_V", "b_V", "W_O", "b_O")] \
    + ["L0_ffn_" + n for n in ("gate_w", "gate_b", "shared_wg", "shared_wu", "shared_wd", "experts_wg", "experts_wu", "experts_wd")] \
    + ["L1_attn_W_qkv", "L1_attn_W_out"] \
    + ["L1_xattn_" + n for n in ("g1", "b1", "g2", "b2", "Wq", "Wkv", "Wout", "bout")] \
    + ["L1_ffn_" + n for n in ("router_w", "router_b", "w_c_fc", "b_c_fc", "w_gate", "b_gate", "w_c_proj", "b_c_proj")]


def kernel(**inputs):
    import numpy as _np
    import concourse.bacc as _bacc
    from concourse import mybir as _mybir
    from concourse.bass_utils import run_bass_kernel_spmd as _run

    nc = _bacc.Bacc("TRN2", target_bir_lowering=False, num_devices=1)
    arrays, ins = {}, {}
    for name in _INS:
        a = _np.ascontiguousarray(inputs[name])
        arrays["in_" + name] = a
        ins[name] = nc.dram_tensor("in_" + name, a.shape, _mybir.dt.from_np(a.dtype), kind="ExternalInput").ap()
    arrays["in_consts"] = CONST_ARRAY
    consts_in = nc.dram_tensor("in_consts", CONST_ARRAY.shape, _mybir.dt.float32, kind="ExternalInput").ap()
    out = nc.dram_tensor("out", (B, T, D), _mybir.dt.float32, kind="ExternalOutput").ap()
    decoder(nc, ins, consts_in, out)
    r = _run(nc, [arrays], core_ids=[0])
    return r.results[0]["out"]
```

```python
import concourse.bass as bass
import concourse.mybir as mybir
import numpy as np
from contextlib import ExitStack

B, T, D = 16, 112, 256
S, KC, NK = 375, 125, 3
F32, BF16, F32R = mybir.dt.float32, mybir.dt.bfloat16, mybir.dt.float32r
ALU = mybir.AluOpType
ACT = mybir.ActivationFunctionType
AX = mybir.AxisListType
LN_EPS = 1e-5
HA, DA = 16, 16
E0, I0 = 16, 128
E1, H1 = 8, 1024
CAP = int(1.2 * 2 * T // E1)
FAR = 3.0e38

CONSTS = {}


def constant_columns():
    parts = []

    def put(name, a):
        a = np.asarray(a, np.float32)
        full = np.zeros((128, a.shape[1]), np.float32)
        full[: a.shape[0]] = a
        CONSTS[name] = (sum(x.shape[1] for x in parts), a.shape[1])
        parts.append(full)

    angle = (np.pi / 2 * np.arange(1, T + 1, dtype=np.float32) / T).astype(np.float32)
    put("ident", np.eye(128))
    put("block16", np.kron(np.eye(8), np.ones((16, 16))))
    put("head16", np.kron(np.eye(8), np.ones((16, 1))))
    put("sincos", np.stack([np.sin(angle), np.cos(angle)], 1))
    put("sincosT", np.tile(np.concatenate([np.sin(angle), np.cos(angle)]), (128, 1)))
    put("count16", np.tile(np.arange(16, 0, -1), (T, 1)))
    put("slots", np.tile(np.arange(CAP), (T, 1)))
    put("upto", np.triu(np.ones((T, T))))
    put("ones", np.ones((T, T)))
    put("minus_half", -0.5 * np.ones((128, 4)))
    pick = np.zeros((48, E0 * 128))
    for e in range(E0):
        for part in range(3):
            pick[part * 16 + e, e * 128:(e + 1) * 128] = 1
    put("pick", pick)
    return np.concatenate(parts, 1)


CONST_ARRAY = constant_columns()
N_CONST = CONSTS["pick"][0]


def bc(ap, n):
    return ap.unsqueeze(len(ap.shape)).broadcast_to(list(ap.shape) + [n])


def mid(ap, n):
    return ap.unsqueeze(1).broadcast_to([ap.shape[0], n, ap.shape[1]])


def chained(eng, sem, base):
    count = [0]

    def link(ins, apart=None):
        count[0] += 1
        ins.then_inc(sem, 1)
        eng.wait_ge(sem, base + count[0])
        if apart is not None:
            eng.sem_inc(apart, 1)
        return count[0]

    return link


class Shared:
    pass


def sem_maker(nc, ctx, prefix):
    held = []

    def give_back():
        nc.clear_and_free_semaphores(held)
        nc.all_engine_barrier()

    ctx.callback(give_back)

    def sem(name):
        held.append(nc.alloc_semaphore(name=prefix + name))
        return held[-1]

    return sem



def norm_power(nc, sh, pool, ln, nth, n=T):
    pool.wait_ge(ln.var_ready, nth)
    nc.gpsimd.tensor_tensor(ln.rstd[:n, :], ln.veps[:n, :], sh.c("minus_half")[:n, 0:1],
                            ALU.pow).then_inc(ln.rstd_ready, 1)


def norm_memory(nc, ctx, prefix, sem):
    ln = Shared()
    ln.stats = ctx.enter_context(nc.sbuf_tensor(prefix + "stats", [128, 6], F32))
    ln.mv = ctx.enter_context(nc.sbuf_tensor(prefix + "mean_var", [128, 2], F32))
    ln.veps = ctx.enter_context(nc.sbuf_tensor(prefix + "var_eps", [128, 1], F32))
    ln.rstd = ctx.enter_context(nc.sbuf_tensor(prefix + "rstd", [128, 1], F32))
    ln.var_ready = sem("var_ready")
    ln.passed = sem("passed")
    ln.rstd_ready = sem("rstd_ready")
    return ln



def linear_attention(nc, sh):
    with ExitStack() as ctx:
        sb = lambda name, shape, dt=F32: ctx.enter_context(nc.sbuf_tensor("la_" + name, shape, dt))
        sem = sem_maker(nc, ctx, "la_")
        ps = sh.ps
        w = sb("wqkv", [128, 2, 3 * D])
        bias = sb("bias", [T, 2 * D])
        bv = sb("bv", [1, D])
        stats = sb("stats", [T, B, 6])
        mv = sb("mean_var", [T, B, 2])
        veps = sb("var_eps", [T, B])
        rstd = sb("rstd", [T, B])
        shift = sb("shift", [T, B])
        xn = sb("xn", [T, D])
        xnTs = sb("xnTs", [128, 2, T])
        qk = sb("qk", [T, 2 * D])
        mx = sb("mx", [T, 32])
        rs = sb("rs", [T, 32])
        rs_sc = sb("rs_sc", [T, 2, 16])
        k = sb("k", [T, D])
        ck = sb("ck", [T, D])
        q_sc = sb("q_sc", [T, 2, D])
        vsc = sb("vsc", [T, 2, 2, 129])
        kvm = sb("kvm", [128, 4, 2, 136])
        qT = sb("qT", [128, 2, 2, T])
        cqT = sb("cqT", [128, 2, 2, T])
        zr = sb("zr", [T, 2, 2, 8])
        t1 = sb("t1", [T, 2, 2, 128])
        at = sb("at", [T, D])
        P_QK, P_V, P_KV, P_O, P_Q, P_A = 0, 1, 2, 4, 6, 7
        x_stats, var_ready, rstd_ready, rows_ready = sem("x_stats"), sem("var_ready"), sem("rstd_ready"), sem("rows_ready")
        xn_ready, xnT_mm, xnT_ready = sem("xn_ready"), sem("xnT_mm"), sem("xnT_ready")
        qkv_mm, vsc_ready, shifted, exp_done = sem("qkv_mm"), sem("vsc_ready"), sem("shifted"), sem("exp_done")
        k_ready, ck_ready, q_ready = sem("k_ready"), sem("ck_ready"), sem("q_ready")
        k_mm, kvm_k_ready, ck_mm, kvm_ck_ready = sem("k_mm"), sem("kvm_k_ready"), sem("ck_mm"), sem("kvm_ck_ready")
        q_mm, qT_ready, cqT_ready = sem("q_mm"), sem("qT_ready"), sem("cqT_ready")
        out_mm, at_ready, aT_mm, aT_ready = sem("out_mm"), sem("at_ready"), sem("aT_mm"), sem("aT_ready")
        chain1, chain2, passed, loaded = sem("chain1"), sem("chain2"), sem("passed"), sem("loaded")
        sin_col, cos_col = sh.c("sincos")[:T, 0:1], sh.c("sincos")[:T, 1:2]
        factors_T = sh.c("sincosT").rearrange("p (s t) -> p s t", s=2)
        LINKS1, LINKS2 = 6, 3
        block = ctx.enter_context(nc.Block())

        def steps(eng, step):
            step(-3, False, False, False, True)
            step(-2, False, False, True, True)
            step(-1, False, True, True, True)
            with eng.Fori(0, B - 3) as i:
                step(i, True, True, True, True)
            step(B - 3, True, True, True, False)
            step(B - 2, True, True, False, False)
            step(B - 1, True, False, False, False)

        @block.sync
        def _(sp):
            sp.dma_start(sh.X[:, :, :], sh.ins["x"].rearrange("b t d -> t b d")).then_inc(sh.x_loaded, 16)
            sp.dma_start(sh.const[:, :], sh.consts_in[:, 0:N_CONST]).then_inc(sh.const_loaded, 16)
            for j, name in enumerate(("Wq", "Wk", "Wv")):
                sp.dma_start(w[:, :, j * D:(j + 1) * D],
                             sh.ins["L0_attn_" + name].rearrange("(c p) n -> p c n", p=128)).then_inc(loaded, 16)
            for j, name in enumerate(("bq", "bk")):
                sp.dma_start(bias[:, j * D:(j + 1) * D],
                             sh.ins["L0_attn_" + name].partition_broadcast(T)).then_inc(loaded, 16)
            sp.dma_start(bv[:, :], sh.ins["L0_attn_bv"].partition_broadcast(1)).then_inc(loaded, 16)
            for dst, src, name in sh.early_loads:
                sp.dma_start(dst, src).then_inc(sh.w_loaded[name], 16)

        @block.gpsimd
        def _(pool):
            pool.wait_ge(sh.const_loaded, 16)
            pool.wait_ge(var_ready, 1)
            nc.gpsimd.tensor_tensor(rstd[:, :], veps[:, :], sh.c("minus_half")[:T, 0:1].broadcast_to([T, B]),
                                    ALU.pow).then_inc(rstd_ready, 1)

            def step(i, result, keys, products, rows):
                if keys:
                    pool.wait_ge(qT_ready, i + 2)
                    nc.gpsimd.tensor_tensor(cqT[:, :, :, :], factors_T.unsqueeze(2).broadcast_to([128, 2, 2, T]),
                                            qT[:, :, :, :], ALU.subtract).then_inc(cqT_ready, 1)
                if products:
                    pool.wait_ge(k_ready, i + 3)
                    pool.sem_inc(passed, 1)
                    nc.gpsimd.tensor_scalar(ck[:, :], k[:, :], -1.0, 1.0, ALU.mult, ALU.add).then_inc(ck_ready, 1)

            steps(pool, step)

        @block.scalar
        def _(act):
            act.wait_ge(sh.const_loaded, 16)
            for c in range(2):
                nc.scalar.copy(vsc[:, c, :, 128], sh.c("sincos")[:T, :])
            act.wait_ge(sh.x_loaded, 16)
            act.wait_ge(rows_ready, 1)

            def step(i, result, keys, products, rows):
                if products:
                    act.wait_ge(xnT_mm, i + 3)
                    nc.scalar.copy(xnTs[:, :, :], ps[:, P_V, 256:256 + 2 * T].rearrange("p (c t) -> p c t", c=2)).then_inc(xnT_ready, 1)
                if rows:
                    act.sem_inc(passed, 1)
                    nc.scalar.activation(xn[:, :], sh.X[:, i + 3, :], ACT.Identity, bias=shift[:, i + 3:i + 4] if isinstance(i, int)
                                         else shift[:, bass.ds(i + 3, 1)], scale=rstd[:, i + 3:i + 4] if isinstance(i, int)
                                         else rstd[:, bass.ds(i + 3, 1)]).then_inc(xn_ready, 1)
                if keys:
                    act.wait_ge(q_mm, i + 2)
                    nc.scalar.copy(qT[:, :, :, :], ps[:, P_Q, 0:4 * T].rearrange("p (s c t) -> p s c t", s=2, c=2)).then_inc(qT_ready, 1)
                if products:
                    act.wait_ge(shifted, i + 3)
                    nc.scalar.activation(qk[:, :], qk[:, :], ACT.Exp).then_inc(exp_done, 1)
                    if keys:
                        act.wait_ge(ck_mm, i + 2)
                    vv = ps[:T, P_V, 0:D].rearrange("p (c n) -> p c n", c=2)
                    nc.scalar.mul(vsc[:, :, 0, 0:128], vv, sin_col)
                    nc.scalar.mul(vsc[:, :, 1, 0:128], vv, cos_col).then_inc(vsc_ready, 1)
                if result:
                    act.wait_ge(aT_mm, i + 1)
                    nc.scalar.copy(sh.attnT[:, :, i, :], ps[:, P_A, 0:2 * T].rearrange("p (c t) -> p c t", c=2)).then_inc(aT_ready, 1)

            steps(act, step)

        @block.vector
        def _(dve):
            dve.wait_ge(sh.x_loaded, 16)
            for b in range(B):
                nc.vector.bn_stats(stats[:, b, :], sh.X[:, b, :]).then_inc(x_stats, 1)
            for b in range(B):
                dve.wait_ge(x_stats, b + 1)
                nc.vector.bn_aggr(mv[:, b, :], stats[:, b, :]).then_inc(x_stats, 1)
            dve.wait_ge(x_stats, 2 * B)
            nc.vector.tensor_scalar(veps[:, :], mv[:, :, 1], LN_EPS, None, ALU.add).then_inc(var_ready, 1)
            dve.wait_ge(rstd_ready, 1)
            nc.vector.scalar_tensor_tensor(shift[:, :], mv[:, :, 0], -1.0, rstd[:, :], ALU.mult, ALU.mult).then_inc(rows_ready, 1)
            dve.wait_ge(sh.const_loaded, 16)
            dve.wait_ge(loaded, 96)

            def masked(r):
                for c in range(2):
                    nc.vector.tensor_tensor(kvm[:, 2 * r + c, :, 0:128],
                                            ps[:, P_KV + c, 0:258].rearrange("p (s n) -> p s n", s=2)[:, :, 0:128],
                                            mid(sh.c("block16"), 2), ALU.mult)
                sums = ps[:, P_KV:P_KV + 2, 0:258].rearrange("p c (s n) -> p c s n", s=2)[:, :, :, 128]
                return nc.vector.tensor_tensor(kvm[:, 2 * r:2 * r + 2, :, 128:136], bc(sums, 8),
                                               sh.c("head16").unsqueeze(1).unsqueeze(1).broadcast_to([128, 2, 2, 8]), ALU.mult)

            def step(i, result, keys, products, rows):
                if result:
                    link = chained(dve, chain2, i * LINKS2)
                    dve.wait_ge(out_mm, i + 1)
                    o = ps[:T, P_O:P_O + 2, 0:272].rearrange("p r (c n) -> p r c n", c=2)
                    link(nc.vector.tensor_scalar(zr[:, :, :, :], o[:, :, :, 128:136], 1e-6, None, ALU.max))
                    link(nc.vector.reciprocal(zr[:, :, :, :], zr[:, :, :, :]))
                    for r in range(2):
                        last = nc.vector.tensor_tensor(t1[:, r, :, :].rearrange("p c (h d) -> p c h d", d=DA),
                                                       o[:, r, :, 0:128].rearrange("p c (h d) -> p c h d", d=DA),
                                                       bc(zr[:, r, :, :], DA), ALU.mult)
                    assert link(last) == LINKS2
                    nc.vector.tensor_tensor(at[:, :].rearrange("p (c n) -> p c n", c=2),
                                            t1[:, 0, :, :], t1[:, 1, :, :], ALU.add).then_inc(at_ready, 1)
                if keys:
                    dve.wait_ge(k_mm, i + 2)
                    masked(0).then_inc(kvm_k_ready, 1)
                if products:
                    link = chained(dve, chain1, (i + 2) * LINKS1)
                    dve.wait_ge(qkv_mm, i + 3)
                    link(nc.vector.tensor_tensor(qk[:, :], ps[:T, P_QK, :], bias[:, :], ALU.add))
                    q3 = qk[:, :].rearrange("p (g d) -> p g d", d=DA)
                    link(nc.vector.tensor_reduce(mx[:, :], q3, AX.X, ALU.max))
                    nc.vector.tensor_tensor(q3, q3, bc(mx[:, :], DA), ALU.subtract).then_inc(shifted, 1)
                if keys:
                    dve.wait_ge(ck_mm, i + 2)
                    masked(1).then_inc(kvm_ck_ready, 1)
                if products:
                    dve.wait_ge(exp_done, i + 3)
                    link(nc.vector.tensor_reduce(rs[:, :], q3, AX.X, ALU.add))
                    link(nc.vector.reciprocal(rs[:, :], rs[:, :]))
                    nc.vector.tensor_scalar(rs_sc[:, 0, :], rs[:, 0:16], sin_col, None, ALU.mult)
                    link(nc.vector.tensor_scalar(rs_sc[:, 1, :], rs[:, 0:16], cos_col, None, ALU.mult))
                    nc.vector.tensor_tensor(k[:, :].rearrange("p (g d) -> p g d", d=DA), q3[:, 16:32, :],
                                            bc(rs[:, 16:32], DA), ALU.mult).then_inc(k_ready, 1)
                    n = link(nc.vector.tensor_tensor(q_sc[:, :, :].rearrange("p s (g d) -> p s g d", d=DA),
                                                     q3[:, 0:16, :].unsqueeze(1).broadcast_to([T, 2, 16, DA]),
                                                     bc(rs_sc[:, :, :], DA), ALU.mult))
                    nc.vector.sem_inc(q_ready, 1)
                    assert n == LINKS1

            steps(dve, step)

        @block.tensor
        def _(pe):
            pe.wait_ge(sh.const_loaded, 16)
            pe.wait_ge(loaded, 96)
            ident = sh.c("ident")

            def key_products(rows):
                for c in range(2):
                    last = nc.tensor.matmul(ps[:, P_KV + c, 0:258], rows[:, c * 128:(c + 1) * 128],
                                            vsc[:, c, :, :].rearrange("p s n -> p (s n)"), start=True, stop=True)
                return last

            def step(i, result, keys, products, rows):
                if result:
                    for r, q in enumerate((qT, cqT)):
                        pe.wait_ge((kvm_k_ready, kvm_ck_ready)[r], i + 1)
                        pe.wait_ge((qT_ready, cqT_ready)[r], i + 1)
                        for c in range(2):
                            for s in range(2):
                                last = nc.tensor.matmul(ps[:T, P_O + r, c * 136:(c + 1) * 136], q[:, s, c, :],
                                                        kvm[:, 2 * r + c, s, :], start=(s == 0), stop=(s == 1))
                    last.then_inc(out_mm, 1)
                if products:
                    pe.wait_ge(xn_ready, i + 3)
                    if keys:
                        pe.wait_ge(vsc_ready, i + 2)
                    for c in range(2):
                        last = nc.tensor.transpose(ps[:, P_V, 256 + c * T:256 + (c + 1) * T], xn[:, c * 128:(c + 1) * 128],
                                                   ident[:T, :T])
                    last.then_inc(xnT_mm, 1)
                if keys:
                    pe.wait_ge(k_ready, i + 2)
                    pe.wait_ge(vsc_ready, i + 2)
                    key_products(k).then_inc(k_mm, 1)
                    pe.wait_ge(q_ready, i + 2)
                    for s in range(2):
                        for c in range(2):
                            at_col = (2 * s + c) * T
                            last = nc.tensor.transpose(ps[:, P_Q, at_col:at_col + T], q_sc[:, s, c * 128:(c + 1) * 128], ident[:T, :T])
                    last.then_inc(q_mm, 1)
                if products:
                    pe.wait_ge(xnT_ready, i + 3)
                    for c in range(2):
                        nc.tensor.matmul(ps[:T, P_QK, :], xnTs[:, c, :], w[:, c, 0:2 * D], start=(c == 0), stop=(c == 1))
                    nc.tensor.matmul(ps[:T, P_V, 0:D], sh.c("ones")[0:1, :T], bv[:, :], start=True, stop=False)
                    for c in range(2):
                        last = nc.tensor.matmul(ps[:T, P_V, 0:D], xnTs[:, c, :], w[:, c, 2 * D:3 * D], start=False, stop=(c == 1))
                    last.then_inc(qkv_mm, 1)
                if keys:
                    pe.wait_ge(ck_ready, i + 2)
                    pe.wait_ge(kvm_k_ready, i + 2)
                    key_products(ck).then_inc(ck_mm, 1)
                if result:
                    pe.wait_ge(at_ready, i + 1)
                    if not products:
                        pe.wait_ge(aT_ready, i)
                    for c in range(2):
                        last = nc.tensor.transpose(ps[:, P_A, c * T:(c + 1) * T], at[:, c * 128:(c + 1) * 128], ident[:T, :T])
                    last.then_inc(aT_mm, 1)

            steps(pe, step)



def add_and_norm(nc, sh, tag, gather, weight=None, bias=None):
    PAIRS = B // 2
    with ExitStack() as ctx:
        sb = lambda name, shape, dt=F32: ctx.enter_context(nc.sbuf_tensor(tag + name, shape, dt))
        sem = sem_maker(nc, ctx, tag)
        ps = sh.ps
        own = sb("own", [128, 2, 2, 2 * T])
        xn = sb("xn", [T, 2, 2, D])
        stats, mv = sb("stats", [T, 2, 6]), sb("mean_var", [T, 2, 2])
        veps, minus_mean = sb("var_eps", [T, 2, 2]), sb("minus_mean", [T, 2, 2])
        rstd, shift = sb("rstd", [T, 2, 2]), sb("shift", [T, 2, 2])
        own_ready, y_mm, added, var_ready, shift_ready = (
            sem("own_ready"), sem("y_mm"), sem("added"), sem("var_ready"), sem("shift_ready"))
        xn_ready, xnT_mm, xnT_ready = sem("xn_ready"), sem("xnT_mm"), sem("xnT_ready")
        chain, rstd_done, passed, passed2 = sem("chain"), sem("rstd_done"), sem("passed"), sem("passed2")
        LINKS = 3 + (bias is not None)
        P_Y, P_XT = 0, 2
        block = ctx.enter_context(nc.Block())

        def steps(eng, step):
            for u in range(2):
                step(u, u, False, True)
            with eng.Fori(1, PAIRS // 2 - 1) as g:
                for u in range(2):
                    step(2 * g + u, u, True, True)
            for u in range(2):
                step(PAIRS - 2 + u, u, True, False)

        @block.gpsimd
        def _(pool):
            def step(p, u, later, more):
                pool.wait_ge(var_ready, p + 1)
                if later:
                    pool.wait_ge(xn_ready, p - 1)
                nc.gpsimd.tensor_tensor(rstd[:, u, :], veps[:, u, :], sh.c("minus_half")[:T, 0:2], ALU.pow).then_inc(rstd_done, 1)
                pool.wait_ge(rstd_done, p + 1)
                nc.gpsimd.tensor_tensor(shift[:, u, :], minus_mean[:, u, :], rstd[:, u, :], ALU.mult).then_inc(shift_ready, 1)

            steps(pool, step)

        @block.scalar
        def _(act):
            def copy_in(p, u):
                src = gather(p)
                dst = own[:, u, :, :].rearrange("p c (a b) -> p c a b", b=src.shape[3])
                nc.scalar.copy(dst, src).then_inc(own_ready, 1)

            def copy_out(p, u):
                act.wait_ge(xnT_mm, p + 1)
                nc.scalar.copy(sh.xnT[:, :, bass.ds(2 * p, 2), :].rearrange("p c j t -> p j c t"),
                               ps[:, P_XT + u, 0:4 * T].rearrange("p (j c t) -> p j c t", j=2, c=2)).then_inc(xnT_ready, 1)

            def step(p, u, later, more):
                if more:
                    act.wait_ge(y_mm, p + 1)
                    copy_in(p + 2, u)
                act.wait_ge(shift_ready, p + 1)
                act.sem_inc(passed, 1)
                for j in range(2):
                    last = nc.scalar.activation(xn[:, u, j, :], sh.X[:, 2 * p + j, :], ACT.Identity,
                                                bias=shift[:, u, j:j + 1], scale=rstd[:, u, j:j + 1])
                last.then_inc(xn_ready, 1)
                if later or u:
                    copy_out(p - 1, 1 - u)

            copy_in(0, 0)
            copy_in(1, 1)
            steps(act, step)
            copy_out(PAIRS - 1, 1)

        @block.vector
        def _(dve):
            def step(p, u, later, more):
                link = chained(dve, chain, p * LINKS)
                x = sh.X[:, bass.ds(2 * p, 2), :]
                dve.wait_ge(y_mm, p + 1)
                link(nc.vector.tensor_tensor(x, x, ps[:T, P_Y + u, :].rearrange("p (j d) -> p j d", j=2), ALU.add))
                nc.vector.sem_inc(added, 1)
                if bias is not None:
                    link(nc.vector.tensor_tensor(x, x, mid(bias, 2), ALU.add))
                dve.sem_inc(passed2, 1)
                nc.vector.bn_stats(stats[:, 0, :], sh.X[:, 2 * p, :])
                link(nc.vector.bn_stats(stats[:, 1, :], sh.X[:, 2 * p + 1, :]), passed2)
                nc.vector.bn_aggr(mv[:, 0, :], stats[:, 0, :])
                n = link(nc.vector.bn_aggr(mv[:, 1, :], stats[:, 1, :]), passed2)
                assert n == LINKS
                if later:
                    dve.wait_ge(shift_ready, p - 1)
                nc.vector.tensor_scalar(minus_mean[:, u, :], mv[:, :, 0], -1.0, None, ALU.mult)
                nc.vector.tensor_scalar(veps[:, u, :], mv[:, :, 1], LN_EPS, None, ALU.add).then_inc(var_ready, 1)

            steps(dve, step)

        @block.tensor
        def _(pe):
            ident = sh.c("ident")

            def product(p, u):
                pe.wait_ge(own_ready, p + 1)
                for j in range(2):
                    for c in range(2):
                        rows = own[:, u, c, j * T:(j + 1) * T]
                        if weight is None:
                            last = nc.tensor.transpose(ps[:T, P_Y + u, j * D + c * 128:j * D + (c + 1) * 128], rows, ident)
                        else:
                            last = nc.tensor.matmul(ps[:T, P_Y + u, j * D:(j + 1) * D], rows, weight[:, c, :],
                                                    start=(c == 0), stop=(c == 1))
                last.then_inc(y_mm, 1)

            def step(p, u, later, more):
                if more:
                    pe.wait_ge(added, p + 1)
                    product(p + 2, u)
                pe.wait_ge(xn_ready, p + 1)
                if later:
                    pe.wait_ge(xnT_ready, p - 1)
                for j in range(2):
                    for c in range(2):
                        at_col = (2 * j + c) * T
                        last = nc.tensor.transpose(ps[:, P_XT + u, at_col:at_col + T], xn[:, u, j, c * 128:(c + 1) * 128],
                                                   ident[:T, :T])
                last.then_inc(xnT_mm, 1)

            product(0, 0)
            product(1, 1)
            steps(pe, step)


def load_bias_rows(sh, rows):
    for n, name in enumerate(("L1_ffn_b_c_fc", "L1_ffn_b_gate")):
        sh.early("bias_rows", rows[0][64 * n:64 * n + 64, :], sh.ins[name].rearrange("e o (j p) -> (e o j) p", p=128))
    at = 0
    for name, n in [("L1_ffn_b_c_proj", 16), ("L1_xattn_g1", 2), ("L1_xattn_b1", 2), ("L1_xattn_g2", 2),
                    ("L1_xattn_b2", 2), ("L0_xattn_b_Q", 2), ("L0_xattn_b_K", 2), ("L0_xattn_b_V", 2)]:
        src = sh.ins[name]
        src = src.rearrange("e o (j p) -> (e o j) p", p=128) if n == 16 else src.rearrange("(j p) -> j p", p=128)
        sh.early("bias_rows", rows[1][at:at + n, :], src)
        at += n
    sh.bias_loads = 10


def bias_columns(nc, sh, rows):
    with ExitStack() as ctx:
        sem = sem_maker(nc, ctx, "bc_")
        cols_mm, made = sem("cols_mm"), sem("made")
        block = ctx.enter_context(nc.Block())
        ident = sh.c("ident")

        @block.tensor
        def _(pe):
            pe.wait_ge(sh.w_loaded["bias_rows"], 16 * sh.bias_loads)
            nc.tensor.transpose(sh.ps[:, 0, 0:128], rows[0][:, :], ident)
            nc.tensor.transpose(sh.ps[:, 0, 128:158], rows[1][:30, :], ident[:30, :30]).then_inc(cols_mm, 1)

        @block.vector
        def _(dve):
            dve.wait_ge(cols_mm, 1)
            nc.vector.tensor_copy(sh.columns[:, 0:158], sh.ps[:, 0, 0:158]).then_inc(made, 1)
            dve.wait_ge(made, 1)
            nc.vector.tensor_scalar(sh.columns[:, 158:160], sh.columns[:, 152:154], 0.25, None, ALU.mult)



class Plan:

    def __init__(self, n_prep, n_fin, fin_at, n_slots, slot_of):
        self.slot_of = slot_of
        self.n_prep, self.n_fin = n_prep, n_fin
        full = [("prep", k) for k in range(n_prep)]
        for k, at in enumerate(fin_at):
            full.insert(at, ("fin", k))
        assert full[-1][0] == "prep"
        self.full, self.n_slots = full, n_slots
        self.only_prep = [s for s in full if s[0] == "prep"]
        self.only_fin = [s for s in full if s[0] == "fin"]

    def base(self, b):
        return self.n_prep - self.n_fin + b * (self.n_prep + self.n_fin)

    def prep_end(self, b):
        return self.n_prep if isinstance(b, int) and b == 0 else self.n_prep * 2 + (b - 1) * (self.n_prep + self.n_fin)

    def slots(self, steps):
        n = self.n_slots
        if self.slot_of is not None:
            where = dict(zip(self.full, self.slot_of))
            return [[(p, *step) for p, step in enumerate(steps) if where[step] == s] for s in range(n)]
        cut = [round(s * len(steps) / n) for s in range(n + 1)]
        return [[(p, *steps[p]) for p in range(cut[s], cut[s + 1])] for s in range(n)]


def attention(nc, sh, cfg):
    with ExitStack() as ctx:
        tag = cfg.tag
        sb = lambda name, shape, dt=F32: ctx.enter_context(nc.sbuf_tensor(tag + name, shape, dt))
        sem = sem_maker(nc, ctx, tag)
        ps = sh.ps
        H, dh, HS, KT, NC = cfg.heads, cfg.dh, cfg.per_stage, cfg.keys, cfg.key_chunks
        KCH = KT // NC
        NS = H // HS
        HD = H * dh
        NF = cfg.out_chunks
        ln = norm_memory(nc, ctx, tag, sem)
        v = sb("v", [KCH, 2, NC, NF, (128 // dh) * (128 + dh)])
        cfg.v_at = lambda par, k: v[:, par, k, :, :].rearrange("p c (j x) -> p c j x", x=128 + dh)[:, :, :, 0:dh]
        cfg.allocate(ctx, sb, sem)
        q_cleared, v_cleared = sem("q_cleared"), sem("v_cleared")
        probs = sb("probs", [T, 2, HS, KT])
        pT = sb("pT", [KCH, 2, HS * NC * T])
        negmax = sb("negmax", [T, 2, H])
        sums = sb("sums", [T, 2, H])
        inv = sb("inv", [T, H])
        inv_wide = sb("inv_wide", [T, H, dh])
        invT = sb("invT", [128, NF, T])
        oT = sb("oT", [128, NF, T])
        y = sb("y", [T, D])
        xn = sb("xn", [T, D])
        scores_mm, max_done, exp_done = sem("scores_mm"), sem("max_done"), sem("exp_done")
        pT_mm, pT_ready, o_mm, o_ready, inv_ready = (
            sem("pT_mm"), sem("pT_ready"), sem("o_mm"), sem("o_ready"), sem("inv_ready"))
        side_mm, side_done, xn_ready = sem("side_mm"), sem("side_done"), sem("xn_ready")
        chain_i, chain_o, chain_x = sem("chain_i"), sem("chain_o"), sem("chain_x")
        cfg.sem_side_done = side_done
        n_prep = len(cfg.prep_mm)
        n_fin = cfg.n_oT_steps + 2
        plan = Plan(n_prep, n_fin, cfg.fin_at, NS + 2, cfg.slot_of)
        BANK_S, BANK_PT, BANK_O, BANK_SIDE, N_SIDE = cfg.banks
        s_banks = cfg.score_banks
        n_ptb = cfg.pt_buffers
        YSTEP = cfg.n_oT_steps
        block = ctx.enter_context(nc.Block())

        def scores_bank(par, x):
            if s_banks == 1:
                return ps[:T, BANK_S + par, x * KT:(x + 1) * KT]
            return ps[:T, BANK_S + par * s_banks + x, 0:KT]

        def scores_all(par):
            if s_banks == 1:
                return ps[:T, BANK_S + par, 0:HS * KT].rearrange("p (h k) -> p h k", h=HS)
            return ps[:T, BANK_S + par * s_banks:BANK_S + (par + 1) * s_banks, 0:KT]

        per_bank = HS if s_banks == 1 else 1
        pt_banks = HS // per_bank

        def pT_psum(par, x, k):
            bank = BANK_PT + (par % n_ptb) * pt_banks + x // per_bank
            col = (x % per_bank * NC + k) * T
            return ps[:KCH, bank, col:col + T]

        def pT_psum_all(par):
            bank = BANK_PT + (par % n_ptb) * pt_banks
            return ps[:KCH, bank:bank + pt_banks, 0:per_bank * NC * T]

        hpc = 128 // dh
        c_per_bank = NF if NF * T <= 512 else 4

        @block.sync
        def _(sp):
            cfg.sync(sp, plan)

        @block.gpsimd
        def _(pool):
            if dh == 64:
                nc.gpsimd.memset(cfg.qT[:, :, :, :, :], 0.0).then_inc(q_cleared, 1)
            cfg.pool(pool, plan, ln)

        @block.scalar
        def _(act):
            def side(p, kind, k, base, b, par):
                act.wait_ge(side_mm, base + p + 1)
                bank = BANK_SIDE + p % N_SIDE
                if kind == "prep":
                    last = cfg.prep_act(k, ps[:, bank, :], b + 1, par)
                elif k < cfg.n_oT_steps:
                    n = NF // cfg.n_oT_steps
                    last = nc.scalar.copy(invT[:, k * n:(k + 1) * n, :], ps[:, bank, 0:n * T].rearrange("p (c t) -> p c t", c=n))
                elif k == YSTEP:
                    last = nc.scalar.copy(y[:, :], ps[:T, bank, 0:D])
                else:
                    last = cfg.xnT_act(b - 1, ps[:, bank, 0:2 * T].rearrange("p (c t) -> p c t", c=2))
                last.then_inc(side_done, 1)

            def exps(b, par, i):
                act.wait_ge(max_done, b * NS + i + 1)
                for x, h in enumerate(cfg.stage_heads(i)):
                    last = nc.scalar.activation(probs[:, i % 2, x, :], scores_bank(i % 2, x), ACT.Exp,
                                                bias=negmax[:, par, h:h + 1], scale=cfg.scale,
                                                accum_out=sums[:, par, h:h + 1])
                last.then_inc(exp_done, 1)

            def iteration(b, par, steps, base):
                for s, todo in enumerate(plan.slots(steps)):
                    for p, kind, k in todo:
                        side(p, kind, k, base, b, 1 - par)
                    if s < NS:
                        exps(b, par, s)

            cfg.wait_weights(act)
            if cfg.act_before:
                cfg.act_before(act)
            if dh == 64:
                act.wait_ge(q_cleared, 1)
            for p, (kind, k) in enumerate(plan.only_prep):
                if k == cfg.first_v_step:
                    act.wait_ge(v_cleared, 2)
                side(p, kind, k, 0, -1, 0)
            iteration(0, 0, plan.only_prep, plan.n_prep)
            with act.Fori(1, B - 2, 2) as b:
                iteration(b, 1, plan.full, plan.base(b))
                iteration(b + 1, 0, plan.full, plan.base(b + 1))
            iteration(B - 1, 1, plan.only_fin, plan.base(B - 1))
            for p, (kind, k) in enumerate(plan.only_fin):
                side(p, kind, k, plan.base(B - 1) + plan.n_fin, B, None)

        @block.vector
        def _(dve):
            LINKS_X = 3 + (cfg.out_bias is not None) + 3 * cfg.twice

            def residual(b, base, p):
                link = chained(dve, chain_x, b * LINKS_X)
                x = sh.X[:, b, :]

                def take():
                    dve.wait_ge(side_done, base + p + 1)
                    link(nc.vector.tensor_tensor(x, x, y[:, :], ALU.add))
                    if cfg.out_bias is not None:
                        link(nc.vector.tensor_tensor(x, x, cfg.out_bias, ALU.add))

                def statistics(rows):
                    dve.sem_inc(ln.passed, 1)
                    link(nc.vector.bn_stats(ln.stats[:T, :], rows), ln.passed)
                    n = link(nc.vector.bn_aggr(ln.mv[:T, :], ln.stats[:T, :]))
                    nc.vector.tensor_scalar(ln.veps[:T, :], ln.mv[:T, 1:2], LN_EPS, None, ALU.add).then_inc(ln.var_ready, 1)
                    return n

                def normalised(out, rows, nth):
                    dve.wait_ge(ln.rstd_ready, nth)
                    return nc.vector.tensor_scalar(out, rows, ln.mv[:T, 0:1], ln.rstd[:T, :], ALU.subtract, ALU.mult)

                def take_and_statistics():
                    take()
                    statistics(x)

                def first_norm():
                    link(normalised(xn[:, :], x, b * 2 + 1))
                    assert statistics(xn[:, :]) == LINKS_X

                def second_norm():
                    normalised(xn[:, :], xn[:, :], b * 2 + 2).then_inc(xn_ready, 1)

                def statistics_once():
                    assert statistics(x) == LINKS_X

                def norm():
                    normalised(xn[:, :], x, b + 1).then_inc(xn_ready, 1)
                    if cfg.keep_rows:
                        nc.vector.tensor_scalar(sh.XN[:, b, :], x, ln.mv[:T, 0:1], ln.rstd[:T, :], ALU.subtract, ALU.mult)

                return [take_and_statistics, first_norm, second_norm] if cfg.twice else [take, statistics_once, norm]

            def inverse_sums(b, par):
                dve.wait_ge(exp_done, b * NS + NS)
                nc.vector.reciprocal(inv[:, :], sums[:, par, :]).then_inc(chain_i, 1)
                dve.wait_ge(chain_i, b + 1)
                nc.vector.tensor_copy(inv_wide[:, :, :], bc(inv[:, :], dh)).then_inc(inv_ready, 1)

            def scale_heads(b, base, p):
                dve.wait_ge(side_done, base + p + 1)
                dve.wait_ge(o_mm, b + 1)
                for n in range(NF // c_per_bank):
                    cs = slice(n * c_per_bank, (n + 1) * c_per_bank)
                    last = nc.vector.tensor_tensor(oT[:, cs, :], invT[:, cs, :],
                                                   ps[:, BANK_O + n, 0:c_per_bank * T].rearrange("p (c t) -> p c t", t=T), ALU.mult)
                if cfg.v_bias is not None:
                    last.then_inc(chain_o, 1)
                    dve.wait_ge(chain_o, b + 1)
                    for c in range(NF):
                        last = nc.vector.tensor_scalar(oT[:, c, :], oT[:, c, :], cfg.v_bias[:, c:c + 1], None, ALU.add)
                last.then_inc(o_ready, 1)

            def iteration(b, par, steps, base):
                slots = plan.slots(steps)
                due = []
                for s in range(NS + 2):
                    for p, kind, k in slots[s]:
                        if (kind, k) == ("fin", YSTEP - 1):
                            scale_heads(b - 1, base, p)
                    if s < NS:
                        dve.wait_ge(scores_mm, b * NS + s + 1)
                        nc.vector.tensor_reduce(negmax[:, par, cfg.stage_columns(s)], scores_all(s % 2),
                                                AX.X, ALU.max, negate=True).then_inc(max_done, 1)
                    if 1 <= s <= NS:
                        dve.wait_ge(pT_mm, b * NS + s)
                        nc.vector.tensor_copy(pT[:, (s - 1) % 2, :].rearrange("p (n k) -> p n k", n=pt_banks),
                                              pT_psum_all((s - 1) % 2)).then_inc(pT_ready, 1)
                    if due:
                        due.pop(0)()
                    for p, kind, k in slots[s]:
                        if (kind, k) == ("fin", YSTEP):
                            due = residual(b - 1, base, p)
                    if cfg.dve_slot:
                        cfg.dve_slot(dve, s, b, 1 - par, ln, steps is not plan.only_fin)
                assert not due
                inverse_sums(b, par)

            cfg.wait_weights(dve)
            if cfg.dve_before:
                cfg.dve_before(dve, ln)
            for u in range(2):
                nc.vector.memset(v[:, u, :, :, :], 0.0).then_inc(v_cleared, 1)
            if cfg.dve_before_end:
                cfg.dve_before_end(dve)
            iteration(0, 0, plan.only_prep, plan.n_prep)
            with dve.Fori(1, B - 2, 2) as b:
                iteration(b, 1, plan.full, plan.base(b))
                iteration(b + 1, 0, plan.full, plan.base(b + 1))
            iteration(B - 1, 1, plan.only_fin, plan.base(B - 1))
            scale_heads(B - 1, plan.base(B - 1) + plan.n_fin, YSTEP - 1)
            for piece in residual(B - 1, plan.base(B - 1) + plan.n_fin, YSTEP):
                piece()

        @block.tensor
        def _(pe):
            ident = sh.c("ident")

            def side(p, kind, k, base, b, par):
                if p < N_SIDE:
                    if not (isinstance(base, int) and base == 0):
                        pe.wait_ge(side_done, base)
                else:
                    pe.wait_ge(side_done, base + p - N_SIDE + 1)
                bank = BANK_SIDE + p % N_SIDE
                if kind == "prep":
                    last = cfg.prep_mm[k](pe, k, ps[:, bank, :], b + 1, base + p, par)
                elif k < cfg.n_oT_steps:
                    pe.wait_ge(inv_ready, b)
                    n = NF // cfg.n_oT_steps
                    for c in range(n):
                        f = k * n + c
                        last = nc.tensor.transpose(ps[:, bank, c * T:(c + 1) * T], inv_wide[:, f * hpc:(f + 1) * hpc, :].rearrange("p h d -> p (h d)"), ident[:T, :T])
                elif k == YSTEP:
                    pe.wait_ge(o_ready, b)
                    for c in range(NF):
                        last = nc.tensor.matmul(ps[:T, bank, 0:D], oT[:, c, :], cfg.w_out[:, c, :],
                                                start=(c == 0), stop=(c == NF - 1))
                else:
                    pe.wait_ge(xn_ready, b)
                    for c in range(2):
                        last = nc.tensor.transpose(ps[:, bank, c * T:(c + 1) * T], xn[:, c * 128:(c + 1) * 128], ident[:T, :T])
                last.then_inc(side_mm, 1)

            steps_at = {}

            def order(steps):
                steps_at.clear()
                steps_at.update({s: p for p, s in enumerate(steps)})

            cfg.steps_at = steps_at

            def stage_scores(b, par, i):
                for x, h in enumerate(cfg.stage_heads(i)):
                    q, kk = cfg.head_operands(par, h)
                    last = nc.tensor.matmul(scores_bank(i % 2, x), q, kk, start=True, stop=True)
                last.then_inc(scores_mm, 1)

            def stage_transposes(b, i):
                pe.wait_ge(exp_done, b * NS + i + 1)
                if not (isinstance(b, int) and b == 0 and i < n_ptb):
                    pe.wait_ge(pT_ready, b * NS + i + 1 - n_ptb)
                for x in range(HS):
                    for k in range(NC):
                        last = nc.tensor.transpose(pT_psum(i, x, k), probs[:, i % 2, x, k * KCH:(k + 1) * KCH], ident[:T, :T])
                last.then_inc(pT_mm, 1)

            def stage_values(b, par, i):
                pe.wait_ge(pT_ready, b * NS + i + 1)
                if i == 0 and not (isinstance(b, int) and b == 0):
                    pe.wait_ge(o_ready, b)
                for x, h in enumerate(cfg.stage_heads(i)):
                    c, j = h // hpc, h % hpc
                    bank, col = BANK_O + c // c_per_bank, c % c_per_bank * T
                    for k in range(NC):
                        at = (x * NC + k) * T
                        last = nc.tensor.matmul(ps[:, bank, col:col + T], v[:, par, k, c, j * 128:(j + 1) * 128], pT[:, i % 2, at:at + T],
                                                start=(j == 0 and k == 0), stop=(j == hpc - 1 and k == NC - 1))
                if i == NS - 1:
                    last.then_inc(o_mm, 1)

            def iteration(b, par, steps, base):
                order(steps)
                pe.wait_ge(side_done, plan.prep_end(b))
                if dh == 16:
                    pe.wait_ge(cfg.q_ready, b + 1)
                for s, todo in enumerate(plan.slots(steps)):
                    if s < NS:
                        stage_scores(b, par, s)
                    for p, kind, k in todo:
                        side(p, kind, k, base, b, 1 - par)
                    if 1 <= s <= NS:
                        stage_transposes(b, s - 1)
                    if s >= 2:
                        stage_values(b, par, s - 2)

            cfg.wait_weights(pe)
            order(plan.only_prep)
            for p, (kind, k) in enumerate(plan.only_prep):
                side(p, kind, k, 0, -1, 0)
            iteration(0, 0, plan.only_prep, plan.n_prep)
            with pe.Fori(1, B - 2, 2) as b:
                iteration(b, 1, plan.full, plan.base(b))
                iteration(b + 1, 0, plan.full, plan.base(b + 1))
            iteration(B - 1, 1, plan.only_fin, plan.base(B - 1))
            for p, (kind, k) in enumerate(plan.only_fin):
                side(p, kind, k, plan.base(B - 1) + plan.n_fin, B, None)


def load_context(nc, sh, cfg, sp, plan):
    src = sh.ins["ctx_1024"].rearrange("b (j p) d -> b p j d", p=KC)

    def load(b, u):
        sp.dma_start(cfg.ctx_in[:, u, :, :], src[b]).then_inc(cfg.ctx_loaded[u], 16)

    load(0, 0)
    load(1, 1)
    sp.wait_ge(cfg.sem_side_done, cfg.ctx_last_use + 1)
    load(2, 0)
    sp.wait_ge(cfg.sem_side_done, plan.n_prep + cfg.ctx_last_use + 1)
    load(3, 1)
    at = plan.full.index(("prep", cfg.ctx_last_use))
    with sp.Fori(4, B - 1, 2) as b:
        for u in range(2):
            sp.wait_ge(cfg.sem_side_done, plan.base(b + u - 3) + at + 1)
            load(b + u, u)



def context_attention_0(nc, sh, w):
    cfg = Shared()
    cfg.tag, cfg.heads, cfg.dh, cfg.per_stage, cfg.keys, cfg.key_chunks = "c0_", 16, 16, 2, S, NK
    cfg.out_chunks, cfg.n_oT_steps = 2, 1
    cfg.banks, cfg.score_banks, cfg.pt_buffers = (0, 4, 6, 7, 1), 2, 1
    cfg.scale = 1.0
    cfg.fin_at = [0, 4, 8]
    cfg.slot_of = None
    cfg.twice = cfg.keep_rows = False
    cfg.out_bias, cfg.v_bias, cfg.w_out = w.bo[:, :], w.bv, w.wo
    cfg.dve_slot = None
    cfg.dve_before = cfg.dve_before_end = cfg.act_before = None
    ident = sh.c("ident")

    cfg.stage_heads = lambda i: [2 * i, 2 * i + 1]
    cfg.stage_columns = lambda i: slice(2 * i, 2 * i + 2)

    def allocate(ctx, sb, sem):
        cfg.ctx_in = sb("ctx_in", [KC, 2, NK, D])
        cfg.ctxT = sb("ctxT", [128, 2, S])
        cfg.kT = sb("kT", [128, 2, 2, S])
        cfg.q_all = sb("q_all", [128, 2, T])
        cfg.qT = sb("qT", [128, 2, 2, 8, T])
        cfg.q_ready = sem("q_ready")
        cfg.ctx_loaded = [sem(f"ctx_loaded{u}") for u in range(2)]

    cfg.allocate = allocate

    def head_operands(par, h):
        return cfg.qT[:, par, h // 8, h % 8, :], cfg.kT[:, par, h // 8, :]

    cfg.head_operands = head_operands

    def wait_weights(eng):
        eng.wait_ge(sh.w_loaded["c0"], w.n_loads * 16)

    cfg.wait_weights = wait_weights

    def transposes(pe, k, bank, b, at, par):
        if k == 1:
            pe.wait_ge(cfg.ctx_loaded[par], b * 8 + 16 - 8 * par)
        for j in range(NK):
            last = nc.tensor.transpose(bank[:, j * KC:(j + 1) * KC], cfg.ctx_in[:, par, j, (k - 1) * 128:k * 128], ident[:KC, :KC])
        return last

    def keys(pe, k, bank, b, at, par):
        m = k - 3
        if m == 0:
            pe.wait_ge(cfg.sem_side_done, at)
        for c in range(2):
            last = nc.tensor.matmul(bank[:, 0:S], w.wk[:, c, m * 128:(m + 1) * 128], cfg.ctxT[:, c, :], start=(c == 0), stop=(c == 1))
        return last

    def values(pe, k, bank, b, at, par):
        for j in ((0, 1) if k == 5 else (2,)):
            for c in range(2):
                last = nc.tensor.matmul(bank[:KC, j % 2 * D:(j % 2 + 1) * D], cfg.ctxT[:, c, j * KC:(j + 1) * KC],
                                        w.wv[:, c, :], start=(c == 0), stop=(c == 1))
        return last

    def queries(pe, k, bank, b, at, par):
        for m in range(2):
            for c in range(2):
                last = nc.tensor.matmul(bank[:, m * T:(m + 1) * T], w.wq[:, c, m * 128:(m + 1) * 128], sh.xnT[:, c, b, :],
                                        start=(c == 0), stop=(c == 1))
        return last

    cfg.prep_mm = [queries, transposes, transposes, keys, keys, values, values]
    cfg.first_v_step = 5
    cfg.ctx_last_use = 2

    def prep_act(k, bank, b, par):
        if k == 0:
            for m in range(2):
                last = nc.scalar.activation(cfg.q_all[:, m, :], bank[:, m * T:(m + 1) * T], ACT.Identity,
                                            bias=w.bq_scaled[:, m:m + 1], scale=0.25)
            return last
        if k < 3:
            return nc.scalar.copy(cfg.ctxT[:, k - 1, :], bank[:, 0:S])
        if k < 5:
            return nc.scalar.activation(cfg.kT[:, par, k - 3, :], bank[:, 0:S], ACT.Identity, bias=w.bk[:, k - 3:k - 2])
        if k == 5:
            for j in range(2):
                last = nc.scalar.copy(cfg.v_at(par, j), bank[:KC, j * D:(j + 1) * D].rearrange("p (c j d) -> p c j d", c=2, d=16))
            return last
        return nc.scalar.copy(cfg.v_at(par, 2), bank[:KC, 0:D].rearrange("p (c j d) -> p c j d", c=2, d=16))

    cfg.prep_act = prep_act
    cfg.xnT_act = lambda b, src: nc.scalar.copy(sh.xnT[:, :, b, :], src)

    cfg.sync = lambda sp, plan: load_context(nc, sh, cfg, sp, plan)

    def pool(eng, plan, ln):
        at = plan.full.index(("prep", 0))

        def masked_queries(par, side_steps):
            eng.wait_ge(cfg.sem_side_done, side_steps)
            for m in range(2):
                last = nc.gpsimd.tensor_tensor(cfg.qT[:, par, m, :, :], mid(cfg.q_all[:, m, :], 8), bc(sh.c("head16"), T), ALU.mult)
            last.then_inc(cfg.q_ready, 1)

        masked_queries(0, 1)
        masked_queries(1, plan.n_prep + 1)
        with eng.Fori(1, B - 2, 2) as b:
            for u in range(2):
                masked_queries(u, plan.base(b + u) + at + 1)
                norm_power(nc, sh, eng, ln, b + u)
        norm_power(nc, sh, eng, ln, B - 1)
        norm_power(nc, sh, eng, ln, B)

    cfg.pool = pool
    attention(nc, sh, cfg)




def top_two(nc, link, v, n, width, count, m):
    for best, hot in ((m.m1, m.oh1), (m.m2, m.oh2)):
        link(nc.vector.tensor_reduce(best[:, :], v[:, :, :], AX.X, ALU.max))
        link(nc.vector.tensor_tensor(m.t[:, :, :], v[:, :, :], bc(best[:, :], width), ALU.is_equal))
        link(nc.vector.tensor_tensor(m.t[:, :, :], m.t[:, :, :], mid(count, n), ALU.mult))
        link(nc.vector.tensor_reduce(m.r[:, :], m.t[:, :, :], AX.X, ALU.max))
        link(nc.vector.tensor_tensor(hot[:, :, :], m.t[:, :, :], bc(m.r[:, :], width), ALU.is_equal))
        if best is m.m1:
            link(nc.vector.scalar_tensor_tensor(v[:, :, :], hot[:, :, :], -FAR, v[:, :, :], ALU.mult, ALU.add))


def split_products(nc, out, high, low, start, stop):
    pairs = []
    for (ah, bh), (al, bl) in zip(high, low):
        pairs += [(ah, bh), (ah, bl), (al, bh)]
    for n, (a, b) in enumerate(pairs):
        last = nc.tensor.matmul(out, a, b, start=start and n == 0, stop=stop and n == len(pairs) - 1)
    return last


def experts_0(nc, sh, w):
    NE = E0 + 1
    G = 4
    GT = G * T
    with ExitStack() as ctx:
        sb = lambda name, shape, dt=F32: ctx.enter_context(nc.sbuf_tensor("e0_" + name, shape, dt))
        sem = sem_maker(nc, ctx, "e0_")
        ps = sh.ps
        x_high, x_low = sb("x_high", [128, 2, B, T], F32R), sb("x_low", [128, 2, B, T], F32R)
        w_high, w_low = sb("w_high", [128, NE, 3, D], F32R), sb("w_low", [128, NE, 3, D], F32R)
        STAGED = 4
        staged = sb("staged", [128, STAGED, 3, D])
        w_loaded = [sem(f"w_loaded{n}") for n in range(STAGED)]
        x_rounded, w_rounded, w_split, w_split_late = sem("x_rounded"), sem("w_rounded"), sem("w_split"), sem("w_split_late")
        POOL_E = 12
        wT = sb("wT", [48, B, T], BF16)
        pick = sb("pick", [48, E0 * 128], BF16)
        with ExitStack() as gates:
            gb = lambda name, shape, dt=F32: gates.enter_context(nc.sbuf_tensor("e0_" + name, shape, dt))
            m = Shared()
            m.t, m.r, m.oh1, m.oh2 = gb("t", [T, B, E0]), gb("r", [T, B]), gb("oh1", [T, B, E0]), gb("oh2", [T, B, E0])
            m.m1, m.m2 = gb("m1", [T, B]), gb("m2", [T, B])
            v = gb("v", [T, B, E0])
            high, middle = gb("high", [T, B, E0], BF16), gb("middle", [T, B, E0], BF16)
            parts = gb("parts", [T, B, 3, E0])
            HP = E0 * 64
            pick32 = gb("pick32", [48, HP])
            logits_mm, logit_ready, exp_done, parts_ready, wT_mm = (
                sem("logits_mm"), sem("logit_ready"), sem("exp_done"), sem("parts_ready"), sem("wT_mm"))
            chain, pick_loaded, pick_half = sem("gate_chain"), sem("pick_loaded"), sem("pick_half")
            with nc.Block() as block:
                @block.sync
                def _(sp):
                    for n in range(2):
                        if n:
                            sp.wait_ge(pick_half, 1)
                        sp.dma_start(pick32[:, :], sh.consts_in[0:48, N_CONST + n * HP:N_CONST + (n + 1) * HP]).then_inc(pick_loaded, 16)
                    for e in range(NE):
                        if e >= STAGED:
                            split, at = (w_split, e - STAGED) if e - STAGED < POOL_E else (w_split_late, e - STAGED - POOL_E)
                            sp.wait_ge(split, at + 1)
                        for n, name in enumerate(("wg", "wu", "wd")):
                            src = sh.ins["L0_ffn_experts_" + name][e] if e < E0 else sh.ins["L0_ffn_shared_" + name]
                            if n < 2:
                                src = src.rearrange("(c p) n -> p c n", p=128)
                                dst = staged[:, e % STAGED, n, :].rearrange("p (c n) -> p c n", c=2)
                            else:
                                dst = staged[:, e % STAGED, n, :]
                            sp.dma_start(dst, src).then_inc(w_loaded[e % STAGED], 16)

                @block.gpsimd
                def _(pool):
                    for e in range(POOL_E):
                        pool.wait_ge(w_rounded, e + 1)
                        nc.gpsimd.tensor_tensor(w_low[:, e, :, :], staged[:, e % STAGED, :, :], w_high[:, e, :, :].bitcast(F32),
                                                ALU.subtract).then_inc(w_split, 1)

                @block.tensor
                def _(pe):
                    pe.wait_ge(sh.w_loaded["gate0"], 32)
                    for b in range(B):
                        for c in range(2):
                            last = nc.tensor.matmul(ps[:T, 0, b * E0:(b + 1) * E0], sh.xnT[:, c, b, :], w.gate[:, c, :],
                                                    start=(c == 0), stop=(c == 1))
                    last.then_inc(logits_mm, 1)
                    pe.wait_ge(parts_ready, 1)
                    for g in range(B // G):
                        for u in range(G):
                            last = nc.tensor.transpose(ps[:48, 1 + g, u * T:(u + 1) * T],
                                                       parts[:, g * G + u, :, :].rearrange("p k e -> p (k e)"), sh.c("ident")[:T, :T])
                        last.then_inc(wT_mm, 1)

                @block.scalar
                def _(act):
                    nc.scalar.copy(x_high[:, :, :, :], sh.xnT[:, :, :, :]).then_inc(x_rounded, 1)

                    def round_weights(e):
                        act.wait_ge(w_loaded[e % STAGED], 48 * (e // STAGED + 1))
                        nc.scalar.copy(w_high[:, e, :, :], staged[:, e % STAGED, :, :]).then_inc(w_rounded, 1)

                    for e in range(4):
                        round_weights(e)
                    act.wait_ge(logit_ready, 1)
                    nc.scalar.activation(v[:, :, :], v[:, :, :], ACT.Exp, scale=-1.0).then_inc(exp_done, 1)
                    for e in range(4, NE):
                        round_weights(e)
                    for g in range(B // G):
                        act.wait_ge(wT_mm, g + 1)
                        nc.scalar.copy(wT[:, g * G:(g + 1) * G, :], ps[:48, 1 + g, 0:GT].rearrange("p (b t) -> p b t", b=G))

                @block.vector
                def _(dve):
                    link = chained(dve, chain, 0)
                    dve.wait_ge(x_rounded, 1)
                    nc.vector.tensor_tensor(x_low[:, :, :, :], sh.xnT[:, :, :, :], x_high[:, :, :, :].bitcast(F32), ALU.subtract)
                    for n in range(2):
                        dve.wait_ge(pick_loaded, 16 * n + 16)
                        nc.vector.tensor_copy(pick[:, n * HP:(n + 1) * HP], pick32[:, :]).then_inc(pick_half, 1)
                    dve.wait_ge(sh.w_loaded["gate0"], 32)
                    dve.wait_ge(logits_mm, 1)
                    nc.vector.tensor_tensor(v[:, :, :], ps[:T, 0, 0:B * E0].rearrange("p (b e) -> p b e", e=E0),
                                            mid(w.gate_b[:, :], B), ALU.add).then_inc(logit_ready, 1)
                    dve.wait_ge(exp_done, 1)
                    link(nc.vector.tensor_scalar(v[:, :, :], v[:, :, :], 1.0, None, ALU.add))
                    link(nc.vector.reciprocal(v[:, :, :], v[:, :, :]))
                    top_two(nc, link, v, B, E0, sh.c("count16")[:T, :], m)
                    link(nc.vector.tensor_tensor(m.r[:, :], m.m1[:, :], m.m2[:, :], ALU.add))
                    link(nc.vector.reciprocal(m.r[:, :], m.r[:, :]))
                    link(nc.vector.tensor_tensor(m.m1[:, :], m.m1[:, :], m.r[:, :], ALU.mult))
                    link(nc.vector.tensor_tensor(m.m2[:, :], m.m2[:, :], m.r[:, :], ALU.mult))
                    link(nc.vector.tensor_tensor(m.oh1[:, :, :], m.oh1[:, :, :], bc(m.m1[:, :], E0), ALU.mult))
                    link(nc.vector.tensor_tensor(m.oh2[:, :, :], m.oh2[:, :, :], bc(m.m2[:, :], E0), ALU.mult))
                    link(nc.vector.tensor_tensor(v[:, :, :], m.oh1[:, :, :], m.oh2[:, :, :], ALU.add))
                    link(nc.vector.tensor_copy(high[:, :, :], v[:, :, :]))
                    link(nc.vector.tensor_tensor(v[:, :, :], v[:, :, :], high[:, :, :], ALU.subtract))
                    link(nc.vector.tensor_copy(middle[:, :, :], v[:, :, :]))
                    nc.vector.tensor_copy(parts[:, :, 0, :], high[:, :, :])
                    nc.vector.tensor_copy(parts[:, :, 1, :], middle[:, :, :])
                    nc.vector.tensor_tensor(parts[:, :, 2, :], v[:, :, :], middle[:, :, :], ALU.subtract).then_inc(parts_ready, 1)
                    for e in range(POOL_E, NE):
                        dve.wait_ge(w_rounded, e + 1)
                        nc.vector.tensor_tensor(w_low[:, e, :, :], staged[:, e % STAGED, :, :], w_high[:, e, :, :].bitcast(F32),
                                                ALU.subtract).then_inc(w_split_late, 1)

        act_out = sb("act_out", [128, 2, GT])
        gated = sb("gated", [128, 2, GT])
        hidden = sb("hidden", [128, 2, GT])
        hidden_high, hidden_low = sb("hidden_high", [128, 2, GT], F32R), sb("hidden_low", [128, 2, GT], F32R)
        gate_mm, up_mm, silu_done, hidden_ready, sum_mm, sum_taken = (
            sem("gate_mm"), sem("up_mm"), sem("silu_done"), sem("hidden_ready"), sem("sum_mm"), sem("sum_taken"))
        chain, chain_h = sem("chain"), sem("chain_h")
        with nc.Block() as block:
            @block.scalar
            def _(act):
                with act.Fori(0, B // G) as g:
                    for e in range(NE):
                        act.wait_ge(gate_mm, g * NE + e + 1)
                        nc.scalar.activation(act_out[:, e % 2, :], ps[:, 3 * (e % 2), 0:GT], ACT.Silu).then_inc(silu_done, 1)

            @block.vector
            def _(dve):
                dve.sem_inc(sum_taken, 1)
                with dve.Fori(0, B // G) as g:
                    link = chained(dve, chain_h, g * NE * 2)
                    for e in range(NE):
                        par = e % 2
                        dve.wait_ge(silu_done, g * NE + e + 1)
                        dve.wait_ge(up_mm, g * NE + e + 1)
                        if e < E0:
                            nc.vector.tensor_tensor(gated[:, par, :], act_out[:, par, :], ps[:, 3 * par + 1, 0:GT], ALU.mult).then_inc(chain, 1)
                            dve.wait_ge(chain, g * E0 + e + 1)
                            link(nc.vector.tensor_tensor(hidden[:, par, :], gated[:, par, :], ps[:, 3 * par + 2, 0:GT], ALU.mult))
                        else:
                            link(nc.vector.tensor_tensor(hidden[:, par, :], act_out[:, par, :], ps[:, 3 * par + 1, 0:GT], ALU.mult))
                        link(nc.vector.tensor_copy(hidden_high[:, par, :], hidden[:, par, :]))
                        nc.vector.tensor_tensor(hidden_low[:, par, :], hidden[:, par, :], hidden_high[:, par, :].bitcast(F32),
                                                ALU.subtract).then_inc(hidden_ready, 1)
                    dve.wait_ge(sum_mm, g + 1)
                    x = sh.xnT[:, :, bass.ds(g * G, G), :].rearrange("p c b t -> p c (b t)")
                    nc.vector.tensor_tensor(x, x, ps[:, 6:8, 0:GT], ALU.add).then_inc(sum_taken, 1)

            @block.tensor
            def _(pe):
                def down(g, e):
                    pe.wait_ge(hidden_ready, g * NE + e + 1)
                    if e == 0:
                        pe.wait_ge(sum_taken, g + 1)
                    for mo in range(2):
                        m = slice(mo * 128, (mo + 1) * 128)
                        last = split_products(nc, ps[:, 6 + mo, 0:GT], [(w_high[:, e, 2, m], hidden_high[:, e % 2, :])],
                                              [(w_low[:, e, 2, m], hidden_low[:, e % 2, :])], e == 0, e == NE - 1)
                    return last

                with pe.Fori(0, B // G) as g:
                    xh, xl = (x[:, :, bass.ds(g * G, G), :].rearrange("p c b t -> p c (b t)") for x in (x_high, x_low))
                    for e in range(NE):
                        bank = 3 * (e % 2)
                        for n in range(2):
                            cs = [slice(c * 128, (c + 1) * 128) for c in range(2)]
                            last = split_products(nc, ps[:, bank + n, 0:GT], [(w_high[:, e, n, cs[c]], xh[:, c, :]) for c in range(2)],
                                                  [(w_low[:, e, n, cs[c]], xl[:, c, :]) for c in range(2)], True, True)
                            if n == 0:
                                last.then_inc(gate_mm, 1)
                        if e < E0:
                            last = nc.tensor.matmul(ps[:, bank + 2, 0:GT], pick[:, e * 128:(e + 1) * 128],
                                                    wT[:, bass.ds(g * G, G), :].rearrange("p b t -> p (b t)"), start=True, stop=True)
                        last.then_inc(up_mm, 1)
                        if e > 0:
                            down(g, e - 1)
                    down(g, NE - 1).then_inc(sum_mm, 1)



def self_attention_1(nc, sh, w):
    cfg = Shared()
    cfg.tag, cfg.heads, cfg.dh, cfg.per_stage, cfg.keys, cfg.key_chunks = "s1_", 16, 64, 4, T, 1
    cfg.out_chunks, cfg.n_oT_steps = 8, 2
    cfg.banks, cfg.score_banks, cfg.pt_buffers = (0, 2, 4, 6, 2), 1, 2
    cfg.scale = 1.0 / 8
    cfg.fin_at = [0, 1, 3, 8]
    cfg.slot_of = [0, 0, 0, 1, 2, 3, 4, 4, 5, 5]
    cfg.twice, cfg.keep_rows = True, False
    cfg.out_bias = cfg.v_bias = None
    cfg.w_out = w.out
    cfg.dve_slot = cfg.dve_before = cfg.dve_before_end = cfg.act_before = None
    cfg.stage_heads = lambda i: [4 * i + x for x in range(4)]
    cfg.stage_columns = lambda i: slice(4 * i, 4 * i + 4)
    wv = w.qkv[:, :, :].rearrange("p c (n j) -> p c j n", j=3)

    def allocate(ctx, sb, sem):
        cfg.kT = sb("kT", [128, 2, 8, T])
        cfg.qT = sb("qT", [128, 2, 2, 8, T])
        cfg.own = sb("own", [128, 2, T])

    cfg.allocate = allocate

    def head_operands(par, h):
        return cfg.qT[:, par, h % 2, h // 2, :], cfg.kT[:, par, h // 2, :]

    cfg.head_operands = head_operands
    cfg.wait_weights = lambda eng: eng.wait_ge(sh.w_loaded["s1"], 32)

    def queries_keys(pe, k, bank, b, at, par):
        for u in range(4):
            n = k % 2 * 4 + u
            for c in range(2):
                last = nc.tensor.matmul(bank[:, u * T:(u + 1) * T], wv[:, c, k // 2, n * 128:(n + 1) * 128], sh.xnT[:, c, b, :],
                                        start=(c == 0), stop=(c == 1))
        return last

    def values(pe, k, bank, b, at, par):
        if k == 4:
            pe.wait_ge(cfg.sem_side_done, at - 1)
        for c in range(2):
            last = nc.tensor.matmul(bank[:T, :], cfg.own[:, c, :], wv[:, c, 2, (k - 4) * 512:(k - 3) * 512],
                                    start=(c == 0), stop=(c == 1))
        return last

    cfg.prep_mm = [queries_keys] * 4 + [values] * 2
    cfg.first_v_step = 4

    def prep_act(k, bank, b, par):
        if k < 4:
            pairs, src = slice(k % 2 * 4, k % 2 * 4 + 4), bank[:, 0:4 * T].rearrange("p (u t) -> p u t", u=4)
            if k >= 2:
                return nc.scalar.copy(cfg.kT[:, par, pairs, :], src)
            for half in range(2):
                rows = slice(64 * half, 64 * half + 64)
                last = nc.scalar.copy(cfg.qT[rows, par, half, pairs, :], src[rows])
            if k == 0:
                last = nc.scalar.copy(cfg.own[:, :, :], sh.xnT[:, :, b, :])
            return last
        return nc.scalar.copy(cfg.v_at(par, 0)[:, (k - 4) * 4:(k - 3) * 4], bank[:T, :].rearrange("p (c j d) -> p c j d", c=4, d=64))

    cfg.prep_act = prep_act

    def xnT_act(b, src):
        for c in range(2):
            last = nc.scalar.activation(sh.xnT[:, c, b, :], src[:, c, :], ACT.Identity,
                                        bias=sh.columns[:, 146 + c:147 + c], scale=sh.columns[:, 144 + c:145 + c])
        return last

    cfg.xnT_act = xnT_act
    cfg.sync = lambda sp, plan: None

    def pool(eng, plan, ln):
        with eng.Fori(0, B) as b:
            norm_power(nc, sh, eng, ln, b * 2 + 1)
            norm_power(nc, sh, eng, ln, b * 2 + 2)

    cfg.pool = pool
    attention(nc, sh, cfg)



def context_attention_1(nc, sh, w):
    cfg = Shared()
    cfg.tag, cfg.heads, cfg.dh, cfg.per_stage, cfg.keys, cfg.key_chunks = "c1_", 8, 64, 1, S, NK
    cfg.out_chunks, cfg.n_oT_steps = 4, 1
    cfg.banks, cfg.score_banks, cfg.pt_buffers = (0, 2, 4, 5, 3), 1, 2
    cfg.scale = 1.0 / 8
    cfg.fin_at = [0, 2, 8]
    cfg.slot_of = [0, 1, 2, 3, 4, 5, 6, 6, 6, 7, 8, 8, 9]
    cfg.twice, cfg.keep_rows = False, True
    cfg.out_bias, cfg.v_bias, cfg.w_out = w.bo[:, :], None, w.out
    ident = sh.c("ident")
    cfg.stage_heads = lambda i: [i]
    cfg.stage_columns = lambda i: slice(i, i + 1)

    def allocate(ctx, sb, sem):
        cfg.ctx_in = sb("ctx_in", [KC, 2, NK, D])
        cfg.cn = sb("cn", [KC, NK, D])
        cfg.ctxT = sb("ctxT", [128, 2, S])
        cfg.ctx_high, cfg.ctx_low = sb("ctx_high", [128, 2, S + 1], F32R), sb("ctx_low", [128, 2, S + 1], F32R)
        cfg.kv_high, cfg.kv_low = sb("kv_high", [128, 2, 1024], F32R), sb("kv_low", [128, 2, 1024], F32R)
        cfg.kv_rounded, cfg.ctx_split = sem("kv_rounded"), sem("ctx_split")
        cfg.kT = sb("kT", [128, 2, 4, S])
        cfg.qT = sb("qT", [128, 2, 2, 4, T])
        cfg.stats = sb("ctx_stats", [KC, NK, 6])
        cfg.mv = sb("ctx_mean_var", [KC, NK, 2])
        cfg.veps = sb("ctx_var_eps", [KC, NK])
        cfg.rstd = sb("ctx_rstd", [KC, NK])
        cfg.ctx_loaded = [sem(f"ctx_loaded{u}") for u in range(2)]
        cfg.ctx_var, cfg.ctx_rstd, cfg.cn_ready, cfg.chain = sem("ctx_var"), sem("ctx_rstd"), sem("cn_ready"), sem("ctx_chain")

    cfg.allocate = allocate

    def head_operands(par, h):
        return cfg.qT[:, par, h % 2, h // 2, :], cfg.kT[:, par, h // 2, :]

    cfg.head_operands = head_operands
    cfg.wait_weights = lambda eng: eng.wait_ge(sh.w_loaded["c1"], 64)

    def queries(pe, k, bank, b, at, par):
        for m in range(4):
            for c in range(2):
                last = nc.tensor.matmul(bank[:, m * T:(m + 1) * T], w.q[:, c, m * 128:(m + 1) * 128], sh.xnT[:, c, b, :],
                                        start=(c == 0), stop=(c == 1))
        return last

    def transposes(pe, k, bank, b, at, par):
        if k == 1:
            pe.wait_ge(cfg.cn_ready, b + 1)
        for j in range(NK):
            last = nc.tensor.transpose(bank[:, j * KC:(j + 1) * KC], cfg.cn[:, j, (k - 1) * 128:k * 128], ident[:KC, :KC])
        return last

    def keys(pe, k, bank, b, at, par):
        m = k - 3
        if m == 0:
            pe.wait_ge(cfg.ctx_split, b + 1)
        cols = slice(m * 128, (m + 1) * 128)
        return split_products(nc, bank[:, 0:S + 1], [(cfg.kv_high[:, c, cols], cfg.ctx_high[:, c, :]) for c in range(2)],
                              [(cfg.kv_low[:, c, cols], cfg.ctx_low[:, c, :]) for c in range(2)], True, True)

    def values(pe, k, bank, b, at, par):
        j = k - 7
        keys = slice(j * KC, (j + 1) * KC)
        return split_products(nc, bank[:KC, :], [(cfg.ctx_high[:, c, keys], cfg.kv_high[:, c, 512:1024]) for c in range(2)],
                              [(cfg.ctx_low[:, c, keys], cfg.kv_low[:, c, 512:1024]) for c in range(2)], True, True)

    cfg.prep_mm = [queries] + [transposes] * 2 + [keys] * 4 + [values] * 3
    cfg.first_v_step = 7

    def prep_act(k, bank, b, par):
        if k == 0:
            for half in range(2):
                rows = slice(64 * half, 64 * half + 64)
                last = nc.scalar.copy(cfg.qT[rows, par, half, :, :], bank[rows, 0:4 * T].rearrange("p (m t) -> p m t", m=4))
            return last
        if k < 3:
            c = k - 1
            for out in (cfg.ctxT, cfg.ctx_high):
                last = nc.scalar.activation(out[:, c, 0:S], bank[:, 0:S], ACT.Identity,
                                            bias=sh.columns[:, 150 + c:151 + c], scale=sh.columns[:, 148 + c:149 + c])
            return last
        if k < 7:
            return nc.scalar.copy(cfg.kT[:, par, k - 3, :], bank[:, 0:S])
        return nc.scalar.copy(cfg.v_at(par, k - 7), bank[:KC, :].rearrange("p (c j d) -> p c j d", c=4, d=64))

    cfg.prep_act = prep_act

    def act_before(act):
        nc.scalar.copy(cfg.kv_high[:, :, :], w.kv[:, :, :]).then_inc(cfg.kv_rounded, 1)

    cfg.act_before = act_before
    cfg.xnT_act = lambda b, src: nc.scalar.copy(sh.xnT[:, :, b, :], src)

    def context_statistics(dve, b, par):
        dve.wait_ge(cfg.ctx_loaded[par], b * 8 + 16 - 8 * par)
        dve.sem_inc(cfg.passed, 1)
        for j in range(NK):
            last = nc.vector.bn_stats(cfg.stats[:, j, :], cfg.ctx_in[:, par, j, :])
        last.then_inc(cfg.chain, 1)

    def context_variance(dve, b, par):
        link = chained(dve, cfg.chain, b * 2 + 1)
        dve.wait_ge(cfg.chain, b * 2 + 1)
        dve.sem_inc(cfg.passed, 1)
        for j in range(NK):
            last = nc.vector.bn_aggr(cfg.mv[:, j, :], cfg.stats[:, j, :])
        link(last)
        nc.vector.tensor_scalar(cfg.veps[:, :], cfg.mv[:, :, 1], LN_EPS, None, ALU.add).then_inc(cfg.ctx_var, 1)

    def context_rows(dve, b, par):
        dve.wait_ge(cfg.ctx_rstd, b + 1)
        for j in range(NK):
            last = nc.vector.tensor_scalar(cfg.cn[:, j, :], cfg.ctx_in[:, par, j, :], cfg.mv[:, j, 0:1],
                                           cfg.rstd[:, j:j + 1], ALU.subtract, ALU.mult)
        last.then_inc(cfg.cn_ready, 1)

    norm_pieces = (context_statistics, context_variance, context_rows)

    def dve_before(dve, ln):
        cfg.passed = ln.passed
        for piece in norm_pieces:
            piece(dve, 0, 0)

    def dve_before_end(dve):
        dve.wait_ge(cfg.sem_side_done, 3)

    cfg.dve_before_end = dve_before_end

    def dve_slot(dve, s, b, par, ln, more):
        if s < 3 and more:
            norm_pieces[s](dve, b + 1, par)

    cfg.dve_before, cfg.dve_slot = dve_before, dve_slot

    def pool(eng, plan, ln):
        def of_context(b):
            eng.wait_ge(cfg.ctx_var, b + 1)
            nc.gpsimd.tensor_tensor(cfg.rstd[:, :], cfg.veps[:, :], sh.c("minus_half")[:KC, 0:NK], ALU.pow).then_inc(cfg.ctx_rstd, 1)

        def split_context(side_steps):
            for c in range(2):
                eng.wait_ge(cfg.sem_side_done, side_steps - 1 + c)
                last = nc.gpsimd.tensor_tensor(cfg.ctx_low[:, c, 0:S], cfg.ctxT[:, c, :], cfg.ctx_high[:, c, 0:S].bitcast(F32),
                                               ALU.subtract)
            last.then_inc(cfg.ctx_split, 1)

        of_context(0)
        for part in (cfg.ctx_high, cfg.ctx_low):
            nc.gpsimd.memset(part[:, :, S:S + 1].bitcast(F32), 0.0)
        eng.wait_ge(cfg.kv_rounded, 1)
        nc.gpsimd.tensor_tensor(cfg.kv_low[:, :, :], w.kv[:, :, :], cfg.kv_high[:, :, :].bitcast(F32), ALU.subtract)
        split_context(3)
        of_context(1)
        split_context(plan.n_prep + 3)
        at = plan.full.index(("prep", 2)) + 1
        with eng.Fori(0, B - 2) as b:
            of_context(b + 2)
            split_context(plan.base(b + 1) + at)
            norm_power(nc, sh, eng, ln, b + 1)
        norm_power(nc, sh, eng, ln, B - 1)
        norm_power(nc, sh, eng, ln, B)

    cfg.pool = pool

    def sync(sp, plan):
        src = sh.ins["ctx_1024"].rearrange("b (j p) d -> b p j d", p=KC)
        for u in range(2):
            sp.dma_start(cfg.ctx_in[:, u, :, :], src[u]).then_inc(cfg.ctx_loaded[u], 16)
        with sp.Fori(2, B - 1, 2) as b:
            for u in range(2):
                sp.wait_ge(cfg.cn_ready, b + u - 1)
                sp.dma_start(cfg.ctx_in[:, u, :, :], src[b + u]).then_inc(cfg.ctx_loaded[u], 16)

    cfg.sync = sync
    attention(nc, sh, cfg)



def experts_1(nc, sh, w):
    NS = E1 * CAP
    HALF = B * CAP // 2
    NJ = H1 // 128
    with ExitStack() as ctx:
        sb = lambda name, shape, dt=F32: ctx.enter_context(nc.sbuf_tensor("e1_" + name, shape, dt))
        sem = sem_maker(nc, ctx, "e1_")
        ps = sh.ps
        m = Shared()
        m.t, m.r, m.oh1, m.oh2 = sb("t", [T, B, E1]), sb("r", [T, B]), sb("oh1", [T, B, E1]), sb("oh2", [T, B, E1])
        m.m1, m.m2 = sb("m1", [T, B]), sb("m2", [T, B])
        lg = sb("lg", [T, B, E1])
        pos = sb("pos", [T, 2, B])
        held = sb("held", [T, 2, B])
        prob = sb("prob", [T, 2, B])
        ex = sb("ex", [128, 2, E1, B * CAP])
        logits_mm, hot_ready, counts_mm, diff_ready, ediff_ready, chain = (
            sem("logits_mm"), sem("hot_ready"), sem("counts_mm"), sem("diff_ready"), sem("ediff_ready"), sem("chain"))

        wfc, wgt = sb("wfc", [128, 2, 2, H1]), sb("wgt", [128, 2, 2, H1])
        wpj = sb("wpj", [128, 2, NJ, D])
        w_in = [sem(f"w_in{u}") for u in range(2)]

        def load_expert(sp, e, u):
            for dst, name, pat in ((wgt, "w_gate", "e (c p) n -> e p c n"), (wfc, "w_c_fc", "e (c p) n -> e p c n"),
                                   (wpj, "w_c_proj", "e (j p) n -> e p j n")):
                sp.dma_start(dst[:, u, :, :], sh.ins["L1_ffn_" + name].rearrange(pat, p=128)[e]).then_inc(w_in[u], 16)

        with nc.Block() as block:
            @block.sync
            def _(sp):
                load_expert(sp, 0, 0)
                load_expert(sp, 1, 1)

            @block.tensor
            def _(pe):
                pe.wait_ge(sh.w_loaded["router1"], 32)
                for b in range(B):
                    for c in range(2):
                        last = nc.tensor.matmul(ps[:T, 0, b * E1:(b + 1) * E1], sh.xnT[:, c, b, :], w.router[:, c, :],
                                                start=(c == 0), stop=(c == 1))
                last.then_inc(logits_mm, 1)
                pe.wait_ge(hot_ready, 1)
                flat = lambda a: a[:, :, :].rearrange("p b e -> p (b e)")
                nc.tensor.matmul(ps[:T, 1, 0:B * E1], sh.c("upto")[:T, :], flat(m.oh1), start=True, stop=True)
                nc.tensor.matmul(ps[:T, 2, 0:B * E1], sh.c("upto")[:T, :], flat(m.oh2), start=True, stop=False)
                nc.tensor.matmul(ps[:T, 2, 0:B * E1], sh.c("ones")[:T, :], flat(m.oh1), start=False, stop=True).then_inc(counts_mm, 1)

            @block.scalar
            def _(act):
                act.wait_ge(diff_ready, 1)
                nc.scalar.activation(prob[:, 1, :], m.r[:, :], ACT.Exp).then_inc(ediff_ready, 1)

            @block.vector
            def _(dve):
                link = chained(dve, chain, 0)
                dve.wait_ge(sh.w_loaded["router1"], 32)
                dve.wait_ge(logits_mm, 1)
                link(nc.vector.tensor_tensor(lg[:, :, :], ps[:T, 0, 0:B * E1].rearrange("p (b e) -> p b e", e=E1),
                                             mid(w.router_b[:, :], B), ALU.add))
                top_two(nc, link, lg, B, E1, sh.c("count16")[:T, 16 - E1:16], m)
                dve.sem_inc(hot_ready, 1)
                nc.vector.tensor_tensor(m.r[:, :], m.m2[:, :], m.m1[:, :], ALU.subtract).then_inc(diff_ready, 1)
                dve.wait_ge(ediff_ready, 1)
                link(nc.vector.tensor_scalar(prob[:, 0, :], prob[:, 1, :], 1.0, None, ALU.add))
                link(nc.vector.reciprocal(prob[:, 0, :], prob[:, 0, :]))
                link(nc.vector.tensor_tensor(prob[:, 1, :], prob[:, 1, :], prob[:, 0, :], ALU.mult))
                dve.wait_ge(counts_mm, 1)
                for n, hot in enumerate((m.oh1, m.oh2)):
                    link(nc.vector.tensor_tensor(m.t[:, :, :], hot[:, :, :], ps[:T, 1 + n, 0:B * E1].rearrange("p (b e) -> p b e", e=E1), ALU.mult))
                    link(nc.vector.tensor_reduce(pos[:, n, :], m.t[:, :, :], AX.X, ALU.add))
                link(nc.vector.tensor_scalar(pos[:, :, :], pos[:, :, :], -1.0, None, ALU.add))
                link(nc.vector.tensor_scalar(held[:, :, :], pos[:, :, :], float(CAP - 1), None, ALU.min))

        sel = sb("sel", [T, 2, CAP])
        part = sb("part", [T, 2, E1, CAP])
        oneh = sb("oneh", [T, 2, E1, CAP])
        flat_xnT = sh.xnT[:, :, :, :].rearrange("p c b t -> p (c b t)")
        spare = lambda at, n: flat_xnT[:, at:at + n]
        own = spare(10 * HALF, 2 * D)[:T].rearrange("p (u d) -> p u d", u=2)

        def sequences(eng, step):
            step(0, 0, False)
            step(1, 1, False)
            with eng.Fori(2, B - 1, 2) as b:
                for u in range(2):
                    step(b + u, u, True)

        oneh_ready, own_ready, slots_mm, slots_ready, sel_chain = (
            sem("oneh_ready"), sem("own_ready"), sem("slots_mm"), sem("slots_ready"), sem("sel_chain"))

        def one_hot(dve, link, at, b, scaled):
            for n in range(2):
                if scaled:
                    last = nc.vector.tensor_scalar(sel[:, n, :], sh.c("slots")[:T, :], at[:, n, b:b + 1] if isinstance(b, int) else at[:, n, bass.ds(b, 1)],
                                                   prob[:, n, b:b + 1] if isinstance(b, int) else prob[:, n, bass.ds(b, 1)], ALU.is_equal, ALU.mult)
                else:
                    last = nc.vector.tensor_scalar(sel[:, n, :], sh.c("slots")[:T, :], at[:, n, b:b + 1] if isinstance(b, int) else at[:, n, bass.ds(b, 1)],
                                                   None, ALU.is_equal)
            link(last)
            for n, hot in enumerate((m.oh1, m.oh2)):
                last = nc.vector.tensor_tensor(part[:, n, :, :], bc(hot[:, b, :], CAP), mid(sel[:, n, :], E1), ALU.mult)
            link(last)

        with nc.Block() as block:
            @block.vector
            def _(dve):
                def step(b, u, later):
                    link = chained(dve, sel_chain, b * 2)
                    one_hot(dve, link, pos, b, False)
                    if later:
                        dve.wait_ge(slots_mm, b - 1)
                    nc.vector.tensor_tensor(oneh[:, u, :, :], part[:, 0, :, :], part[:, 1, :, :], ALU.add).then_inc(oneh_ready, 1)

                sequences(dve, step)

            @block.scalar
            def _(act):
                def take(b, u):
                    act.wait_ge(slots_mm, b + 1)
                    for c in range(2):
                        last = nc.scalar.copy(ex[:, c, :, bass.ds(b * CAP, CAP)], ps[:, 2 * u + c, 0:NS].rearrange("p (e s) -> p e s", e=E1))
                    last.then_inc(slots_ready, 1)

                def step(b, u, later):
                    if later:
                        take(b - 2, u)
                    nc.scalar.copy(own[:, u, :], sh.XN[:, b, :]).then_inc(own_ready, 1)

                sequences(act, step)
                for u in range(2):
                    take(B - 2 + u, u)

            @block.tensor
            def _(pe):
                def step(b, u, later):
                    pe.wait_ge(own_ready, b + 1)
                    pe.wait_ge(oneh_ready, b + 1)
                    if later:
                        pe.wait_ge(slots_ready, b - 1)
                    for c in range(2):
                        last = nc.tensor.matmul(ps[:, 2 * u + c, 0:NS], own[:, u, c * 128:(c + 1) * 128],
                                                oneh[:, u, :, :].rearrange("p e s -> p (e s)"), start=True, stop=True)
                    last.then_inc(slots_mm, 1)

                sequences(pe, step)

        ffn = ctx.enter_context(ExitStack())
        fb = lambda name, shape, dt=F32: ffn.enter_context(nc.sbuf_tensor("e1_" + name, shape, dt))
        w_high, w_low = fb("w_high", [128, NJ, 3, D], F32R), fb("w_low", [128, NJ, 3, D], F32R)
        ex_high, ex_low = fb("ex_high", [128, 2, 2, B * CAP], F32R), fb("ex_low", [128, 2, 2, B * CAP], F32R)
        hid_high, hid_low = fb("hid_high", [128, 2, HALF], F32R), fb("hid_low", [128, 2, HALF], F32R)
        gbuf = spare(0, 2 * HALF).rearrange("p (a n) -> p a n", a=2)
        ubuf = spare(2 * HALF, 4 * HALF).rearrange("p (u a n) -> p u a n", u=2, a=2)
        hid = spare(6 * HALF, 4 * HALF).rearrange("p (u a n) -> p u a n", u=2, a=2)
        g_mm, h_mm, g_taken, u_ready, hid_done, hid_ready, out_taken, passed = (
            sem("g_mm"), sem("h_mm"), sem("g_taken"), sem("u_ready"), sem("hid_done"), sem("hid_ready"), sem("out_taken"), sem("passed"))
        piece_rounded, piece_split, piece_used, ex_rounded, ex_split, chain_h, passed2 = (
            sem("piece_rounded"), sem("piece_split"), sem("piece_used"), sem("ex_rounded"), sem("ex_split"), sem("chain_h"), sem("passed2"))
        AHEAD = NJ - 2
        with nc.Block() as block:
            def pairs(eng, pair):
                pair(0, True, False)
                with eng.Fori(2, E1 - 3, 2) as e2:
                    pair(e2, False, False)
                pair(E1 - 2, False, True)

            @block.sync
            def _(sp):
                with sp.Fori(2, E1 - 1, 2) as e:
                    for u in range(2):
                        sp.wait_ge(piece_split, (e + u - 1) * NJ)
                        load_expert(sp, e + u, u)

            def of_piece(u, j):
                m = slice(j * 128, (j + 1) * 128)
                return wgt[:, u, :, m], wfc[:, u, :, m], wpj[:, u, j, :].rearrange("p (c n) -> p c n", c=2)

            def parts_of(split, j):
                return [split[:, j, k, :].rearrange("p (c n) -> p c n", c=2) for k in range(3)]

            @block.gpsimd
            def _(pool):
                with pool.Fori(0, E1 - 1, 2) as e2:
                    for n in range(2 * NJ):
                        j = n % NJ
                        pool.wait_ge(piece_rounded, e2 * NJ + n + 1)
                        for low, high, whole in zip(parts_of(w_low, j), parts_of(w_high, j), of_piece(n // NJ, j)):
                            last = nc.gpsimd.tensor_tensor(low, whole, high.bitcast(F32), ALU.subtract)
                        last.then_inc(piece_split, 1)

            @block.scalar
            def _(act):
                def round_piece(e2, n):
                    u, j = n // NJ % 2, n % NJ
                    if j == 0:
                        act.wait_ge(w_in[u], (e2 + n // NJ - u) * 24 + 48)
                    for high, whole in zip(parts_of(w_high, j), of_piece(u, j)):
                        last = nc.scalar.copy(high, whole)
                    last.then_inc(piece_rounded, 1)

                def pair(e2, is_first, is_last):
                    for n in range(2 * NJ):
                        j = n % NJ
                        n_all = e2 * NJ + n
                        act.wait_ge(g_mm, n_all + 1)
                        act.sem_inc(passed, 1)
                        nc.scalar.activation(gbuf[:, :, :], ps[:, 2:4, 0:HALF], ACT.Identity,
                                             bias=sh.columns[:, bass.ds(n_all + 64, 1)]).then_inc(g_taken, 1)
                        if not (is_last and n + AHEAD >= 2 * NJ):
                            round_piece(e2, n + AHEAD)
                        act.wait_ge(u_ready, n_all + 2)
                        nc.scalar.activation(hid[:, j % 2, :, :], ubuf[:, j % 2, :, :], ACT.Silu).then_inc(hid_done, 1)

                act.sem_inc(g_taken, 1)
                for n in range(AHEAD):
                    round_piece(0, n)
                pairs(act, pair)

            @block.vector
            def _(dve):
                def round_inputs(e, u):
                    nc.vector.tensor_copy(ex_high[:, u, :, :], ex[:, :, e, :]).then_inc(ex_rounded, 1)

                def split_inputs(e, u):
                    dve.wait_ge(ex_rounded, e + 1)
                    dve.sem_inc(passed2, 1)
                    nc.vector.tensor_tensor(ex_low[:, u, :, :], ex[:, :, e, :], ex_high[:, u, :, :].bitcast(F32),
                                            ALU.subtract).then_inc(ex_split, 1)

                def take_outputs(e):
                    dve.wait_ge(piece_used, (e + 1) * NJ)
                    dve.sem_inc(passed2, 1)
                    for mo in range(2):
                        last = nc.vector.tensor_scalar(ex[:, mo, e, :].rearrange("p (a n) -> p a n", a=2),
                                                       ps[:, 4 + 2 * mo:6 + 2 * mo, 0:HALF],
                                                       sh.columns[:, bass.ds(e * 2 + 128 + mo, 1)], None, ALU.add)
                    last.then_inc(out_taken, 1)

                def pair(e2, is_first, is_last):
                    link = chained(dve, chain_h, e2 * NJ)
                    for n in range(2 * NJ):
                        u, j = n // NJ, n % NJ
                        e = e2 + u
                        n_all = e2 * NJ + n
                        dve.wait_ge(h_mm, n_all + 1)
                        dve.wait_ge(g_taken, n_all + 2)
                        nc.vector.scalar_tensor_tensor(ubuf[:, j % 2, :, :], ps[:, 0:2, 0:HALF], sh.columns[:, bass.ds(n_all, 1)],
                                                       gbuf[:, :, :], ALU.add, ALU.mult).then_inc(u_ready, 1)
                        dve.wait_ge(hid_done, n_all + 1)
                        if not (is_first and n == 0):
                            dve.wait_ge(piece_used, n_all)
                            dve.sem_inc(passed2, 1)
                        link(nc.vector.tensor_copy(hid_high[:, :, :], hid[:, j % 2, :, :]))
                        nc.vector.tensor_tensor(hid_low[:, :, :], hid[:, j % 2, :, :], hid_high[:, :, :].bitcast(F32),
                                                ALU.subtract).then_inc(hid_ready, 1)
                        if j == 0 and not (is_first and u == 0):
                            take_outputs(e - 1)
                        if j == 3 and not (is_last and u == 1):
                            round_inputs(e + 1, 1 - u)
                        if j == 5 and not (is_last and u == 1):
                            split_inputs(e + 1, 1 - u)

                dve.sem_inc(u_ready, 1)
                dve.sem_inc(out_taken, 1)
                round_inputs(0, 0)
                split_inputs(0, 0)
                pairs(dve, pair)
                take_outputs(E1 - 1)

            @block.tensor
            def _(pe):
                def hidden_products(u, j, n_all):
                    pe.wait_ge(piece_split, n_all + 1)
                    for k, bank, free, done in ((0, 2, g_taken, g_mm), (1, 0, u_ready, h_mm)):
                        pe.wait_ge(free, n_all + 1)
                        for half in range(2):
                            cols = slice(half * HALF, (half + 1) * HALF)
                            last = split_products(nc, ps[:, bank + half, 0:HALF],
                                                  [(w_high[:, j, k, c * 128:(c + 1) * 128], ex_high[:, u, c, cols]) for c in range(2)],
                                                  [(w_low[:, j, k, c * 128:(c + 1) * 128], ex_low[:, u, c, cols]) for c in range(2)],
                                                  True, True)
                        last.then_inc(done, 1)

                def out_products(e, j, n_all):
                    pe.wait_ge(hid_ready, n_all + 1)
                    if j == 0:
                        pe.wait_ge(out_taken, e + 1)
                    for mo in range(2):
                        m = slice(mo * 128, (mo + 1) * 128)
                        for half in range(2):
                            last = split_products(nc, ps[:, 4 + 2 * mo + half, 0:HALF],
                                                  [(w_high[:, j, 2, m], hid_high[:, half, :])],
                                                  [(w_low[:, j, 2, m], hid_low[:, half, :])], j == 0, j == NJ - 1)
                    last.then_inc(piece_used, 1)

                def pair(e2, is_first, is_last):
                    for n in range(2 * NJ):
                        u, j = n // NJ, n % NJ
                        if j == 0:
                            pe.wait_ge(ex_split, e2 + u + 1)
                        hidden_products(u, j, e2 * NJ + n)
                        if not (is_first and n == 0):
                            out_products(e2 + (n - 1) // NJ, (n - 1) % NJ, e2 * NJ + n - 1)

                pairs(pe, pair)
                out_products(E1 - 1, NJ - 1, E1 * NJ - 1)

        ffn.close()

        CH = [(0, 3), (3, 6), (6, 8)]
        Y_BANK = 3
        own_ex = sb("own_ex", [128, 2, 2, E1, CAP])
        gT = sb("gT", [3 * CAP, 2, 3, T])
        oS = sb("oS", [3 * CAP, 2, 3, D])
        ohc_ready, ownx_ready, tr_mm, tr_ready, y_mm, x_ready, comb_chain = (
            sem("ohc_ready"), sem("ownx_ready"), sem("tr_mm"), sem("tr_ready"), sem("y_mm"), sem("x_ready"), sem("comb_chain"))
        stored = sem("stored")
        with nc.Block() as block:
            @block.sync
            def _(sp):
                with sp.Fori(0, B) as b:
                    sp.wait_ge(x_ready, b + 1)
                    sp.dma_start(sh.out[b], sh.X[:, b, :]).then_inc(stored, 16)
                sp.wait_ge(stored, 16 * B)

            @block.vector
            def _(dve):
                def matrix(b, u, later):
                    link = chained(dve, comb_chain, b * 2)
                    one_hot(dve, link, held, b, True)
                    if later:
                        dve.wait_ge(tr_mm, b - 1)
                    nc.vector.tensor_tensor(oneh[:, u, :, :], part[:, 0, :, :], part[:, 1, :, :], ALU.add).then_inc(ohc_ready, 1)

                def rows(b, u):
                    dve.wait_ge(y_mm, b + 1)
                    nc.vector.tensor_tensor(sh.X[:, b, :], sh.X[:, b, :], ps[:T, Y_BANK + 4 * u, 0:D], ALU.add).then_inc(x_ready, 1)

                matrix(0, 0, False)
                matrix(1, 1, False)
                with dve.Fori(0, B - 3, 2) as b:
                    for u in range(2):
                        matrix(b + 2 + u, u, True)
                        rows(b + u, u)
                for u in range(2):
                    rows(B - 2 + u, u)

            @block.gpsimd
            def _(pool):
                def step(b, u, later):
                    if later:
                        pool.wait_ge(tr_mm, b - 1)
                        pool.sem_inc(passed, 1)
                    for c in range(2):
                        last = nc.gpsimd.tensor_copy(own_ex[:, u, c, :, :], ex[:, c, :, bass.ds(b * CAP, CAP)])
                    last.then_inc(ownx_ready, 1)

                sequences(pool, step)

            @block.scalar
            def _(act):
                def step(b, u, later):
                    act.wait_ge(tr_mm, b + 1)
                    if later:
                        act.wait_ge(y_mm, b - 1)
                    k = 4 * u
                    nc.scalar.copy(gT[:, u, 0:2, :], ps[:3 * CAP, k, 0:2 * T].rearrange("p (q t) -> p q t", q=2))
                    nc.scalar.copy(gT[:2 * CAP, u, 2, :], ps[:2 * CAP, k, 2 * T:3 * T])
                    nc.scalar.copy(oS[:, u, 0:2, :], ps[:3 * CAP, k + 1, :].rearrange("p (q n) -> p q n", q=2))
                    nc.scalar.copy(oS[:2 * CAP, u, 2, :], ps[:2 * CAP, k + 2, 0:D]).then_inc(tr_ready, 1)

                sequences(act, step)

            @block.tensor
            def _(pe):
                ident = sh.c("ident")

                def transposes(b, u, later=True):
                    pe.wait_ge(ohc_ready, b + 1)
                    pe.wait_ge(ownx_ready, b + 1)
                    if later:
                        pe.wait_ge(tr_ready, b - 1)
                    k = 4 * u
                    for q, (lo, hi) in enumerate(CH):
                        n = (hi - lo) * CAP
                        nc.tensor.transpose(ps[:n, k, q * T:(q + 1) * T], oneh[:, u, lo:hi, :].rearrange("p e s -> p (e s)"), ident[:T, :T])
                        for c in range(2):
                            last = nc.tensor.transpose(ps[:n, k + 1 + q // 2, q % 2 * D + c * 128:q % 2 * D + (c + 1) * 128],
                                                       own_ex[:, u, c, lo:hi, :].rearrange("p e s -> p (e s)"), ident)
                    last.then_inc(tr_mm, 1)

                def product(b, u, later=True):
                    pe.wait_ge(tr_ready, b + 1)
                    if later:
                        pe.wait_ge(x_ready, b - 1)
                    for q, (lo, hi) in enumerate(CH):
                        n = (hi - lo) * CAP
                        last = nc.tensor.matmul(ps[:T, Y_BANK + 4 * u, 0:D], gT[:n, u, q, :], oS[:n, u, q, :],
                                                start=(q == 0), stop=(q == 2))
                    last.then_inc(y_mm, 1)

                transposes(0, 0, False)
                transposes(1, 1, False)
                product(0, 0, False)
                transposes(2, 0)
                product(1, 1, False)
                with pe.Fori(2, B - 3, 2) as b:
                    for u in range(2):
                        transposes(b + u + 1, 1 - u)
                        product(b + u, u)
                transposes(B - 1, 1)
                product(B - 2, 0)
                product(B - 1, 1)


def decoder(nc, ins, consts_in, out):
    with ExitStack() as ctx:
        sb = lambda name, shape, dt=F32: ctx.enter_context(nc.sbuf_tensor(name, shape, dt))
        sem = lambda name: ctx.enter_context(nc.semaphore(name))
        sh = Shared()
        sh.ins, sh.consts_in, sh.out = ins, consts_in, out
        sh.const = sb("const", [128, N_CONST])
        sh.c = lambda name: sh.const[:, CONSTS[name][0]:CONSTS[name][0] + CONSTS[name][1]]
        sh.X = sb("X", [T, B, D])
        sh.xnT = sb("xnT", [128, 2, B, T])
        sh.columns = sb("columns", [128, 160])
        sh.ps = ctx.enter_context(nc.psum_tensor("ps", [128, 8, 512], F32))
        sh.const_loaded, sh.x_loaded, stored = sem("const_loaded"), sem("x_loaded"), sem("stored")
        sh.w_loaded = {}
        sh.early_loads = []

        def early(name, dst, src):
            if name not in sh.w_loaded:
                sh.w_loaded[name] = sem("loaded_" + name)
            sh.early_loads.append((dst, src, name))

        sh.early = early
        e0 = Shared()
        e0.gate, e0.gate_b = sb("e0_gate", [128, 2, E0]), sb("e0_gate_b", [T, E0])
        early("gate0", e0.gate[:, :, :], ins["L0_ffn_gate_w"].rearrange("(c p) n -> p c n", p=128))
        early("gate0", e0.gate_b[:, :], ins["L0_ffn_gate_b"].partition_broadcast(T))
        layer0 = ExitStack()
        s0 = lambda name, shape, dt=F32: layer0.enter_context(nc.sbuf_tensor(name, shape, dt))
        wo0 = s0("wo0", [128, 2, D])
        bo0 = s0("bo0", [T, D])
        bias_rows = [s0(f"bias_rows{n}", [128, 128]) for n in range(2)]
        load_bias_rows(sh, bias_rows)
        early("wo0", wo0[:, :, :], ins["L0_attn_Wo"].rearrange("(c p) n -> p c n", p=128))
        early("wo0", bo0[:, :], ins["L0_attn_bo"].partition_broadcast(T))
        w0 = Shared()
        w0.bv, w0.bo = sh.columns[:, 156:158], s0("c0_bo", [T, D])
        early("c0", w0.bo[:, :], ins["L0_xattn_b_O"].partition_broadcast(T))
        w0.n_loads = 5
        w0.bk, w0.bq_scaled = sh.columns[:, 154:156], sh.columns[:, 158:160]
        w0.wq, w0.wk, w0.wv, w0.wo = (s0("c0_w" + n, [128, 2, D]) for n in "qkvo")
        for n, t in (("Q", w0.wq), ("K", w0.wk), ("V", w0.wv), ("O", w0.wo)):
            early("c0", t[:, :, :], ins["L0_xattn_W_" + n].rearrange("(c p) n -> p c n", p=128))
        with nc.sbuf_tensor("attnT", [128, 2, B, T], F32) as attnT:
            sh.attnT = attnT
            linear_attention(nc, sh)
            L = T // B
            permuted = attnT[:, :, :, :].rearrange("p c b l -> p c l b")
            with nc.Block() as block:
                @block.tensor
                def _(pe):
                    pe.wait_ge(sh.w_loaded["wo0"], 32)

                @block.vector
                def _(dve):
                    dve.wait_ge(sh.w_loaded["wo0"], 32)
            add_and_norm(nc, sh, "ao_", lambda p: permuted[:, :, bass.ds(2 * p * L, 2 * L), :], wo0, bo0[:, :])
        bias_columns(nc, sh, bias_rows)
        weights = Shared()

        def load_now(name, dst, src):
            if name not in sh.w_loaded:
                sh.w_loaded[name] = sem("loaded_" + name)
            sh.now.append((dst, src, name))

        def issue():
            with nc.Block() as block:
                @block.sync
                def _(sp):
                    for dst, src, name in sh.now:
                        sp.dma_start(dst, src).then_inc(sh.w_loaded[name], 16)
            sh.now = []

        sh.now = []
        with layer0:
            context_attention_0(nc, sh, w0)
        experts_0(nc, sh, e0)
        add_and_norm(nc, sh, "ea_", lambda p: sh.xnT[:, :, bass.ds(2 * p, 2), :])
        s1, c1, e1 = Shared(), Shared(), Shared()
        e1.router, e1.router_b = sb("e1_router", [128, 2, E1]), sb("e1_router_b", [T, E1])
        sh.XN = sb("XN", [T, B, D])
        attentions1 = ctx.enter_context(ExitStack())
        sa = lambda name, shape, dt=F32: attentions1.enter_context(nc.sbuf_tensor(name, shape, dt))
        s1.qkv, s1.out = sa("s1_qkv", [128, 2, 3072]), sa("s1_out", [128, 8, D])
        load_now("s1", s1.qkv[:, :, :], ins["L1_attn_W_qkv"].rearrange("(c p) n -> p c n", p=128))
        load_now("s1", s1.out[:, :, :], ins["L1_attn_W_out"].rearrange("(c p) n -> p c n", p=128))
        c1.q, c1.kv, c1.out, c1.bo = (sa("c1_q", [128, 2, 512]), sa("c1_kv", [128, 2, 1024]), sa("c1_out", [128, 4, D]),
                                      sa("c1_bo", [T, D]))
        load_now("c1", c1.q[:, :, :], ins["L1_xattn_Wq"].rearrange("(c p) n -> p c n", p=128))
        load_now("c1", c1.kv[:, :, :], ins["L1_xattn_Wkv"].rearrange("(c p) n -> p c n", p=128))
        load_now("c1", c1.out[:, :, :], ins["L1_xattn_Wout"].rearrange("(c p) n -> p c n", p=128))
        load_now("c1", c1.bo[:, :], ins["L1_xattn_bout"].partition_broadcast(T))
        load_now("router1", e1.router[:, :, :], ins["L1_ffn_router_w"].rearrange("(c p) n -> p c n", p=128))
        load_now("router1", e1.router_b[:, :], ins["L1_ffn_router_b"].partition_broadcast(T))
        issue()
        self_attention_1(nc, sh, s1)
        context_attention_1(nc, sh, c1)
        attentions1.close()
        experts_1(nc, sh, e1)


_INS = ["x", "ctx_1024"] + ["L0_attn_" + n for n in ("Wq", "bq", "Wk", "bk", "Wv", "bv", "Wo", "bo")] \
    + ["L0_xattn_" + n for n in ("W_Q", "b_Q", "W_K", "b_K", "W_V", "b_V", "W_O", "b_O")] \
    + ["L0_ffn_" + n for n in ("gate_w", "gate_b", "shared_wg", "shared_wu", "shared_wd", "experts_wg", "experts_wu", "experts_wd")] \
    + ["L1_attn_W_qkv", "L1_attn_W_out"] \
    + ["L1_xattn_" + n for n in ("g1", "b1", "g2", "b2", "Wq", "Wkv", "Wout", "bout")] \
    + ["L1_ffn_" + n for n in ("router_w", "router_b", "w_c_fc", "b_c_fc", "w_gate", "b_gate", "w_c_proj", "b_c_proj")]


def kernel(**inputs):
    import numpy as _np
    import concourse.bacc as _bacc
    from concourse import mybir as _mybir
    from concourse.bass_utils import run_bass_kernel_spmd as _run

    nc = _bacc.Bacc("TRN2", target_bir_lowering=False, num_devices=1)
    arrays, ins = {}, {}
    for name in _INS:
        a = _np.ascontiguousarray(inputs[name])
        arrays["in_" + name] = a
        ins[name] = nc.dram_tensor("in_" + name, a.shape, _mybir.dt.from_np(a.dtype), kind="ExternalInput").ap()
    arrays["in_consts"] = CONST_ARRAY
    consts_in = nc.dram_tensor("in_consts", CONST_ARRAY.shape, _mybir.dt.float32, kind="ExternalInput").ap()
    out = nc.dram_tensor("out", (B, T, D), _mybir.dt.float32, kind="ExternalOutput").ap()
    decoder(nc, ins, consts_in, out)
    r = _run(nc, [arrays], core_ids=[0])
    return r.results[0]["out"]
```
